# Optimizing a Trainium2 kernel written in Bass

```python
import numpy as np
import jax
import jax.numpy as jnp

def _softmax(x, axis=-1):
    return jax.nn.softmax(x, axis=axis)

def _gelu(x):
    return jax.nn.gelu(x, approximate=True)

def _silu(x):
    return jax.nn.silu(x)

def _sigmoid(x):
    return jax.nn.sigmoid(x)

def _layernorm(x, axis=-1, eps=1e-05):
    m = jnp.mean(x, axis=axis, keepdims=True)
    v = jnp.var(x, axis=axis, keepdims=True)
    return (x - m) / jnp.sqrt(v + eps)

def _scatter_add(tgt, idx, src, axis=0):
    return tgt.at[idx].add(src)

def _segment_sum(src, seg, n):
    return jax.ops.segment_sum(src, seg, n)
kernel_name = 'mk_hybrid_d2_jaxref_r8_969c8b'

def setup_inputs(seed: int=0):
    np.random.seed(seed)
    _w = jnp.asarray

    def _L0_attn_a_setup():
        import jax, jax.numpy as jnp
        import numpy as np
        INF_APPROX = 1e+30
        ROTARY_BASE = 10000.0
        D_HEAD = 128

        def _rope(x, base=ROTARY_BASE):
            _, length, _, width = x.shape
            half = width // 2
            positions = jnp.arange(length, dtype=x.dtype)
            dims = jnp.arange(half, dtype=x.dtype)
            ang_freqs = jnp.power(base, -dims / half)
            radians = positions[:, None] * ang_freqs[None, :]
            cos = jnp.cos(radians)[None, :, None, :]
            sin = jnp.sin(radians)[None, :, None, :]
            even, odd = jnp.split(x, 2, axis=-1)
            return jnp.concatenate([even * cos - odd * sin, even * sin + odd * cos], axis=-1)
        key = jax.random.key(seed)
        k1, k2, k3, k4, k5 = jax.random.split(key, 5)
        B, T, M, H, D = (2, 512, 128, 8, 128)
        n_layer = 24
        x = jax.random.normal(k1, (B, T, M), dtype=jnp.float32)
        std_qkv = M ** (-0.5)
        std_o = (M * 2 * n_layer) ** (-0.5)
        w_aq = jnp.zeros((M, H, D), dtype=jnp.float32)
        w_ak = std_qkv * jax.random.normal(k3, (M, H, D), dtype=jnp.float32)
        w_av = std_qkv * jax.random.normal(k4, (M, H, D), dtype=jnp.float32)
        w_ao = std_o * jax.random.normal(k5, (H, D, M), dtype=jnp.float32)
        return {'x': x, 'w_aq': w_aq, 'w_ak': w_ak, 'w_av': w_av, 'w_ao': w_ao}
    _L0_attn_a_in = _L0_attn_a_setup()

    def _L0_attn_b_setup():
        import jax, jax.numpy as jnp
        import numpy as np
        B, L, E, H, D = (4, 256, 128, 16, 64)

        def alibi_matrix(n, n_heads, causal=True):
            idx = jnp.arange(n, dtype=jnp.float32)
            dists = -jnp.abs(idx[None, :] - idx[:, None])
            slopes = 2.0 ** (-jnp.linspace(1.0, 8.0, n_heads, dtype=jnp.float32))
            alibi = slopes[:, None, None] * dists[None, :, :]
            if causal:
                causal_ok = idx[:, None] >= idx[None, :]
                alibi = jnp.where(causal_ok[None, :, :], alibi, -jnp.inf)
            return alibi[None]
        key = jax.random.key(seed)
        k1, k2, k3 = jax.random.split(key, 3)
        X = jax.random.normal(k1, (B, L, E), dtype=jnp.float32)
        s_in = 1.0 / np.sqrt(E)
        s_hd = 1.0 / np.sqrt(H * D)
        W_qkv = jax.random.uniform(k2, (E, H * 3 * D), jnp.float32, -s_in, s_in)
        b_qkv = jnp.zeros((H * 3 * D,), jnp.float32)
        W_out = jax.random.uniform(k3, (H * D, E), jnp.float32, -s_hd, s_hd)
        b_out = jnp.zeros((E,), jnp.float32)
        return {'X': X, 'W_qkv': W_qkv, 'b_qkv': b_qkv, 'W_out': W_out, 'b_out': b_out}
    _L0_attn_b_in = _L0_attn_b_setup()

    def _L0_ffn_setup():
        import jax, jax.numpy as jnp
        import numpy as np
        B, N, D, H, E = (4, 128, 128, 16, 8)
        DK = D // H
        HID = 4 * D
        EPS = 1e-05

        def _layernorm(x, w, b):
            m = jnp.mean(x, axis=-1, keepdims=True)
            v = jnp.mean(jnp.square(x - m), axis=-1, keepdims=True)
            return (x - m) * jax.lax.rsqrt(v + EPS) * w + b

        def _msa(x, w_qkv, w_proj):
            b, n, d = x.shape
            qkv = (x @ w_qkv).reshape(b, n, 3, H, DK)
            q = qkv[:, :, 0].transpose(0, 2, 1, 3)
            k = qkv[:, :, 1].transpose(0, 2, 1, 3)
            v = qkv[:, :, 2].transpose(0, 2, 1, 3)
            attn = jnp.einsum('bhnd,bhmd->bhnm', q, k) * (1.0 / np.sqrt(DK))
            attn = jax.nn.softmax(attn, axis=-1)
            y = jnp.einsum('bhnm,bhmd->bhnd', attn, v)
            y = y.transpose(0, 2, 1, 3).reshape(b, n, d)
            return y @ w_proj

        def _moe_mlp(x, gate_w, gate_b, w1, w2):
            b, n, d = x.shape
            xf = x.reshape(b * n, d)
            logits = xf @ gate_w + gate_b
            one_hot = jax.nn.one_hot(jnp.argmax(logits, axis=-1), E, dtype=xf.dtype)
            h = jax.nn.gelu(jnp.einsum('td,edh->teh', xf, w1), approximate=True)
            y = jnp.einsum('teh,ehd->ted', h, w2)
            out = jnp.einsum('te,ted->td', one_hot, y)
            return out.reshape(b, n, d)
        key = jax.random.key(seed)
        ks = jax.random.split(key, 8)
        s = 0.02
        return {'x': jax.random.normal(ks[0], (B, N, D), jnp.float32), 'ln1_w': jnp.ones((D,), jnp.float32), 'ln1_b': jnp.zeros((D,), jnp.float32), 'w_qkv': jax.random.normal(ks[1], (D, 3 * D), jnp.float32) * s, 'w_proj': jax.random.normal(ks[2], (D, D), jnp.float32) * s, 'ln2_w': jnp.ones((D,), jnp.float32), 'ln2_b': jnp.zeros((D,), jnp.float32), 'gate_w': jax.random.normal(ks[3], (D, E), jnp.float32) * s, 'gate_b': jnp.zeros((E,), jnp.float32), 'w1': jax.random.normal(ks[4], (E, D, HID), jnp.float32) * s, 'w2': jax.random.normal(ks[5], (E, HID, D), jnp.float32) * s}
    _L0_ffn_in = _L0_ffn_setup()

    def _L1_attn_a_setup():
        import jax, jax.numpy as jnp
        import numpy as np
        B, L, D, N = (2, 256, 128, 16)
        H = D // N
        THETA = 10000.0

        def apply_rope(x):
            l, h = (x.shape[-2], x.shape[-1])
            freqs = THETA ** (-jnp.arange(0, h, 2, dtype=jnp.float32) / h)
            ang = jnp.arange(l, dtype=jnp.float32)[:, None] * freqs
            cos, sin = (jnp.cos(ang), jnp.sin(ang))
            x_even = x[..., 0::2]
            x_odd = x[..., 1::2]
            out_even = cos * x_even - sin * x_odd
            out_odd = sin * x_even + cos * x_odd
            return jnp.stack((out_even, out_odd), axis=-1).reshape(x.shape)
        key = jax.random.key(seed)
        ks = jax.random.split(key, 9)
        s = 0.02
        return {'x': jax.random.normal(ks[0], (B, L, D), dtype=jnp.float32), 'Wq': jax.random.normal(ks[1], (D, D), dtype=jnp.float32) * s, 'bq': jax.random.normal(ks[2], (D,), dtype=jnp.float32) * s, 'Wk': jax.random.normal(ks[3], (D, D), dtype=jnp.float32) * s, 'bk': jax.random.normal(ks[4], (D,), dtype=jnp.float32) * s, 'Wv': jax.random.normal(ks[5], (D, D), dtype=jnp.float32) * s, 'bv': jax.random.normal(ks[6], (D,), dtype=jnp.float32) * s, 'Wo': jax.random.normal(ks[7], (D, D), dtype=jnp.float32) * s, 'bo': jax.random.normal(ks[8], (D,), dtype=jnp.float32) * s, 'scale': jnp.ones((1,), dtype=jnp.float32) * H ** (-0.5)}
    _L1_attn_a_in = _L1_attn_a_setup()

    def _L1_attn_b_setup():
        import jax, jax.numpy as jnp
        import numpy as np
        EPS = 1e-05
        N_HEADS, KV_HEADS = (16, 4)

        def layernorm(x, g, b):
            m = jnp.mean(x, -1, keepdims=True)
            v = jnp.var(x, -1, keepdims=True)
            return (x - m) / jnp.sqrt(v + EPS) * g + b

        def mamba_block(x, ln_g, ln_b, in_w, conv_w, conv_b, xp_w, dt_w, dt_b, A_log, D_skip, out_w):
            Bsz, L, _ = x.shape
            d_inner = D_skip.shape[0]
            d_conv = conv_w.shape[-1]
            res = x
            h = layernorm(x, ln_g, ln_b)
            xs, gate = jnp.split(h @ in_w, 2, axis=-1)
            xc = jnp.pad(xs.transpose(0, 2, 1), ((0, 0), (0, 0), (d_conv - 1, 0)))
            xc = jax.lax.conv_general_dilated(xc, conv_w, (1,), 'VALID', dimension_numbers=('NCH', 'OIH', 'NCH'), feature_group_count=d_inner)
            xs = jax.nn.silu(xc.transpose(0, 2, 1) + conv_b)
            Bm, Cm = jnp.split(xs @ xp_w, 2, axis=-1)
            dt = jax.nn.softplus(Bm @ dt_w + dt_b)
            A = -jnp.exp(A_log)

            def step(hst, inp):
                xt, dtt, Bt, Ct = inp
                dA = jnp.exp(dtt[..., None] * A)
                hst = hst * dA + dtt[..., None] * Bt[:, None, :] * xt[..., None]
                yt = jnp.sum(hst * Ct[:, None, :], -1)
                return (hst, yt)
            h0 = jnp.zeros((Bsz, d_inner, A.shape[-1]), xs.dtype)
            _, y = jax.lax.scan(step, h0, (xs.transpose(1, 0, 2), dt.transpose(1, 0, 2), Bm.transpose(1, 0, 2), Cm.transpose(1, 0, 2)))
            y = y.transpose(1, 0, 2)
            y = (y + D_skip * xs) * jax.nn.silu(gate)
            return y @ out_w + res

        def attn_block(x, ln_g, ln_b, q_w, k_w, v_w, o_w):
            Bsz, L, D = x.shape
            H, KV = (N_HEADS, KV_HEADS)
            dh = D // H
            res = x
            h = layernorm(x, ln_g, ln_b)
            q = (h @ q_w).reshape(Bsz, L, H, dh).transpose(0, 2, 1, 3)
            k = (h @ k_w).reshape(Bsz, L, KV, dh).transpose(0, 2, 1, 3)
            v = (h @ v_w).reshape(Bsz, L, KV, dh).transpose(0, 2, 1, 3)
            inv = 1.0 / 10000.0 ** (jnp.arange(0, dh, 2, dtype=jnp.float32) / dh)
            fr = jnp.arange(L, dtype=jnp.float32)[:, None] * inv
            emb = jnp.concatenate([fr, fr], -1)
            cos, sin = (jnp.cos(emb), jnp.sin(emb))

            def rot(t):
                t1, t2 = jnp.split(t, 2, -1)
                return jnp.concatenate([-t2, t1], -1)
            q = q * cos + rot(q) * sin
            k = k * cos + rot(k) * sin
            g = H // KV
            k = jnp.repeat(k, g, axis=1)
            v = jnp.repeat(v, g, axis=1)
            sc = jnp.einsum('bhqd,bhkd->bhqk', q, k) / jnp.sqrt(jnp.float32(dh))
            mask = jnp.where(jnp.tril(jnp.ones((L, L), bool)), 0.0, -1000000000.0)
            p = jax.nn.softmax((sc + mask).astype(jnp.float32), -1).astype(q.dtype)
            o = jnp.einsum('bhqk,bhkd->bhqd', p, v).transpose(0, 2, 1, 3).reshape(Bsz, L, D)
            return o @ o_w + res
        key = jax.random.key(seed)
        B, L, D = (4, 128, 128)
        d_inner, d_state, d_conv = (256, 16, 4)
        H, KV, dh = (N_HEADS, KV_HEADS, D // N_HEADS)
        dff = 512
        ks = jax.random.split(key, 16)
        w = lambda k, shape: jax.random.normal(k, shape, jnp.float32) * 0.02
        return {'x': jax.random.normal(ks[0], (B, L, D), jnp.float32), 'ln1_g': jnp.ones(D), 'ln1_b': jnp.zeros(D), 'in_proj_w': w(ks[1], (D, 2 * d_inner)), 'conv_w': w(ks[2], (d_inner, 1, d_conv)), 'conv_b': jnp.zeros(d_inner), 'x_proj_w': w(ks[3], (d_inner, 2 * d_state)), 'dt_proj_w': w(ks[4], (d_state, d_inner)), 'dt_proj_b': jnp.zeros(d_inner), 'A_log': jnp.log(jnp.tile(jnp.arange(1, d_state + 1, dtype=jnp.float32), (d_inner, 1))), 'D_skip': jnp.ones(d_inner), 'out_proj_w': w(ks[5], (d_inner, D)), 'ln2_g': jnp.ones(D), 'ln2_b': jnp.zeros(D), 'q_w': w(ks[6], (D, H * dh)), 'k_w': w(ks[7], (D, KV * dh)), 'v_w': w(ks[8], (D, KV * dh)), 'o_w': w(ks[9], (H * dh, D)), 'ln3_g': jnp.ones(D), 'ln3_b': jnp.zeros(D), 'w1': w(ks[10], (D, dff)), 'w2': w(ks[11], (dff, D)), 'w3': w(ks[12], (D, dff))}
    _L1_attn_b_in = _L1_attn_b_setup()

    def _L1_ffn_setup():
        import jax, jax.numpy as jnp
        import numpy as np
        import math
        B, S, D = (4, 256, 128)
        H = 16
        E = 8
        K = 2
        F = 512

        def _layernorm(x, g, b, eps=1e-05):
            mu = jnp.mean(x, axis=-1, keepdims=True)
            var = jnp.mean(jnp.square(x - mu), axis=-1, keepdims=True)
            return (x - mu) * jax.lax.rsqrt(var + eps) * g + b

        def _attention(x, Wq, bq, Wk, bk, Wv, bv, Wo, bo):
            b, s, d = x.shape
            dh = d // H
            q = (x @ Wq + bq).reshape(b, s, H, dh)
            k = (x @ Wk + bk).reshape(b, s, H, dh)
            v = (x @ Wv + bv).reshape(b, s, H, dh)
            scores = jnp.einsum('bqhd,bkhd->bhqk', q, k) / math.sqrt(dh)
            attn = jax.nn.softmax(scores, axis=-1)
            out = jnp.einsum('bhqk,bkhd->bqhd', attn, v).reshape(b, s, d)
            return out @ Wo + bo

        def _moe(x, gate_w, gate_b, W1, b1, W2, b2):
            b, s, d = x.shape
            xt = x.reshape(b * s, d)
            probs = jax.nn.softmax(xt @ gate_w + gate_b, axis=-1)
            top_v, top_i = jax.lax.top_k(probs, K)
            combine = jnp.sum(jax.nn.one_hot(top_i, E, dtype=xt.dtype) * top_v[..., None], axis=1)
            out = jnp.zeros_like(xt)
            for e in range(E):
                h = jax.nn.gelu(xt @ W1[e] + b1[e], approximate=False) @ W2[e] + b2[e]
                out = out + combine[:, e:e + 1] * h
            return out.reshape(b, s, d)
        key = jax.random.key(seed)
        ks = jax.random.split(key, 16)
        s_d = 1.0 / math.sqrt(D)
        s_f = 1.0 / math.sqrt(F)
        return {'x': jax.random.normal(ks[0], (B, S, D), jnp.float32), 'Wq': jax.random.normal(ks[1], (D, D), jnp.float32) * s_d, 'Wk': jax.random.normal(ks[2], (D, D), jnp.float32) * s_d, 'Wv': jax.random.normal(ks[3], (D, D), jnp.float32) * s_d, 'Wo': jax.random.normal(ks[4], (D, D), jnp.float32) * s_d, 'bq': jnp.zeros((D,), jnp.float32), 'bk': jnp.zeros((D,), jnp.float32), 'bv': jnp.zeros((D,), jnp.float32), 'bo': jnp.zeros((D,), jnp.float32), 'ln1_g': jnp.ones((D,), jnp.float32), 'ln1_b': jnp.zeros((D,), jnp.float32), 'ln2_g': jnp.ones((D,), jnp.float32), 'ln2_b': jnp.zeros((D,), jnp.float32), 'gate_w': jax.random.normal(ks[5], (D, E), jnp.float32) * s_d, 'gate_b': jnp.zeros((E,), jnp.float32), 'W1': jax.random.normal(ks[6], (E, D, F), jnp.float32) * s_d, 'b1': jnp.zeros((E, F), jnp.float32), 'W2': jax.random.normal(ks[7], (E, F, D), jnp.float32) * s_f, 'b2': jnp.zeros((E, D), jnp.float32)}
    _L1_ffn_in = _L1_ffn_setup()
    _d = {'L0_attn_a_x': _L0_attn_a_in['x'], 'L0_attn_a_w_aq': _L0_attn_a_in['w_aq'], 'L0_attn_a_w_ak': _L0_attn_a_in['w_ak'], 'L0_attn_a_w_av': _L0_attn_a_in['w_av'], 'L0_attn_a_w_ao': _L0_attn_a_in['w_ao'], 'L0_attn_b_W_qkv': _L0_attn_b_in['W_qkv'], 'L0_attn_b_b_qkv': _L0_attn_b_in['b_qkv'], 'L0_attn_b_W_out': _L0_attn_b_in['W_out'], 'L0_attn_b_b_out': _L0_attn_b_in['b_out'], 'L0_ffn_ln1_w': _L0_ffn_in['ln1_w'], 'L0_ffn_ln1_b': _L0_ffn_in['ln1_b'], 'L0_ffn_w_qkv': _L0_ffn_in['w_qkv'], 'L0_ffn_w_proj': _L0_ffn_in['w_proj'], 'L0_ffn_ln2_w': _L0_ffn_in['ln2_w'], 'L0_ffn_ln2_b': _L0_ffn_in['ln2_b'], 'L0_ffn_gate_w': _L0_ffn_in['gate_w'], 'L0_ffn_gate_b': _L0_ffn_in['gate_b'], 'L0_ffn_w1': _L0_ffn_in['w1'], 'L0_ffn_w2': _L0_ffn_in['w2'], 'L1_attn_a_Wq': _L1_attn_a_in['Wq'], 'L1_attn_a_bq': _L1_attn_a_in['bq'], 'L1_attn_a_Wk': _L1_attn_a_in['Wk'], 'L1_attn_a_bk': _L1_attn_a_in['bk'], 'L1_attn_a_Wv': _L1_attn_a_in['Wv'], 'L1_attn_a_bv': _L1_attn_a_in['bv'], 'L1_attn_a_Wo': _L1_attn_a_in['Wo'], 'L1_attn_a_bo': _L1_attn_a_in['bo'], 'L1_attn_a_scale': _L1_attn_a_in['scale'], 'L1_attn_b_ln1_g': _L1_attn_b_in['ln1_g'], 'L1_attn_b_ln1_b': _L1_attn_b_in['ln1_b'], 'L1_attn_b_in_proj_w': _L1_attn_b_in['in_proj_w'], 'L1_attn_b_conv_w': _L1_attn_b_in['conv_w'], 'L1_attn_b_conv_b': _L1_attn_b_in['conv_b'], 'L1_attn_b_x_proj_w': _L1_attn_b_in['x_proj_w'], 'L1_attn_b_dt_proj_w': _L1_attn_b_in['dt_proj_w'], 'L1_attn_b_dt_proj_b': _L1_attn_b_in['dt_proj_b'], 'L1_attn_b_A_log': _L1_attn_b_in['A_log'], 'L1_attn_b_D_skip': _L1_attn_b_in['D_skip'], 'L1_attn_b_out_proj_w': _L1_attn_b_in['out_proj_w'], 'L1_attn_b_ln2_g': _L1_attn_b_in['ln2_g'], 'L1_attn_b_ln2_b': _L1_attn_b_in['ln2_b'], 'L1_attn_b_q_w': _L1_attn_b_in['q_w'], 'L1_attn_b_k_w': _L1_attn_b_in['k_w'], 'L1_attn_b_v_w': _L1_attn_b_in['v_w'], 'L1_attn_b_o_w': _L1_attn_b_in['o_w'], 'L1_attn_b_ln3_g': _L1_attn_b_in['ln3_g'], 'L1_attn_b_ln3_b': _L1_attn_b_in['ln3_b'], 'L1_attn_b_w1': _L1_attn_b_in['w1'], 'L1_attn_b_w2': _L1_attn_b_in['w2'], 'L1_attn_b_w3': _L1_attn_b_in['w3'], 'L1_ffn_Wq': _L1_ffn_in['Wq'], 'L1_ffn_bq': _L1_ffn_in['bq'], 'L1_ffn_Wk': _L1_ffn_in['Wk'], 'L1_ffn_bk': _L1_ffn_in['bk'], 'L1_ffn_Wv': _L1_ffn_in['Wv'], 'L1_ffn_bv': _L1_ffn_in['bv'], 'L1_ffn_Wo': _L1_ffn_in['Wo'], 'L1_ffn_bo': _L1_ffn_in['bo'], 'L1_ffn_ln1_g': _L1_ffn_in['ln1_g'], 'L1_ffn_ln1_b': _L1_ffn_in['ln1_b'], 'L1_ffn_ln2_g': _L1_ffn_in['ln2_g'], 'L1_ffn_ln2_b': _L1_ffn_in['ln2_b'], 'L1_ffn_gate_w': _L1_ffn_in['gate_w'], 'L1_ffn_gate_b': _L1_ffn_in['gate_b'], 'L1_ffn_W1': _L1_ffn_in['W1'], 'L1_ffn_b1': _L1_ffn_in['b1'], 'L1_ffn_W2': _L1_ffn_in['W2'], 'L1_ffn_b2': _L1_ffn_in['b2']}
    _x0 = _d['L0_attn_a_x']
    _d['L0_attn_a_x'] = jax.random.normal(jax.random.fold_in(jax.random.key(seed), 1), (16, 256, 128), dtype=_x0.dtype)
    del _x0
    return _d

def reference(L0_attn_a_x, L0_attn_a_w_aq, L0_attn_a_w_ak, L0_attn_a_w_av, L0_attn_a_w_ao, L0_attn_b_W_qkv, L0_attn_b_b_qkv, L0_attn_b_W_out, L0_attn_b_b_out, L0_ffn_ln1_w, L0_ffn_ln1_b, L0_ffn_w_qkv, L0_ffn_w_proj, L0_ffn_ln2_w, L0_ffn_ln2_b, L0_ffn_gate_w, L0_ffn_gate_b, L0_ffn_w1, L0_ffn_w2, L1_attn_a_Wq, L1_attn_a_bq, L1_attn_a_Wk, L1_attn_a_bk, L1_attn_a_Wv, L1_attn_a_bv, L1_attn_a_Wo, L1_attn_a_bo, L1_attn_a_scale, L1_attn_b_ln1_g, L1_attn_b_ln1_b, L1_attn_b_in_proj_w, L1_attn_b_conv_w, L1_attn_b_conv_b, L1_attn_b_x_proj_w, L1_attn_b_dt_proj_w, L1_attn_b_dt_proj_b, L1_attn_b_A_log, L1_attn_b_D_skip, L1_attn_b_out_proj_w, L1_attn_b_ln2_g, L1_attn_b_ln2_b, L1_attn_b_q_w, L1_attn_b_k_w, L1_attn_b_v_w, L1_attn_b_o_w, L1_attn_b_ln3_g, L1_attn_b_ln3_b, L1_attn_b_w1, L1_attn_b_w2, L1_attn_b_w3, L1_ffn_Wq, L1_ffn_bq, L1_ffn_Wk, L1_ffn_bk, L1_ffn_Wv, L1_ffn_bv, L1_ffn_Wo, L1_ffn_bo, L1_ffn_ln1_g, L1_ffn_ln1_b, L1_ffn_ln2_g, L1_ffn_ln2_b, L1_ffn_gate_w, L1_ffn_gate_b, L1_ffn_W1, L1_ffn_b1, L1_ffn_W2, L1_ffn_b2):

    def _L0_attn_a_ref(x, w_aq, w_ak, w_av, w_ao):
        import jax, jax.numpy as jnp
        import numpy as np
        INF_APPROX = 1e+30
        ROTARY_BASE = 10000.0
        D_HEAD = 128

        def _rope(x, base=ROTARY_BASE):
            _, length, _, width = x.shape
            half = width // 2
            positions = jnp.arange(length, dtype=x.dtype)
            dims = jnp.arange(half, dtype=x.dtype)
            ang_freqs = jnp.power(base, -dims / half)
            radians = positions[:, None] * ang_freqs[None, :]
            cos = jnp.cos(radians)[None, :, None, :]
            sin = jnp.sin(radians)[None, :, None, :]
            even, odd = jnp.split(x, 2, axis=-1)
            return jnp.concatenate([even * cos - odd * sin, even * sin + odd * cos], axis=-1)
        B, T, M = x.shape
        q = jnp.einsum('btm,mhd->bthd', x, w_aq)
        k = jnp.einsum('btm,mhd->bthd', x, w_ak)
        v = jnp.einsum('btm,mhd->bthd', x, w_av)
        q = _rope(q)
        k = _rope(k)
        s = jnp.einsum('bihd,bjhd->bhij', q, k) / D_HEAD
        i = jnp.arange(T)[:, None]
        j = jnp.arange(T)[None, :]
        mask = (i < j).astype(x.dtype)[None, None, :, :]
        s = s - jnp.asarray(INF_APPROX, x.dtype) * mask
        p = jax.nn.softmax(s, axis=-1)
        o = jnp.einsum('bhij,bjhd->bihd', p, v)
        r = jnp.einsum('bihd,hdm->bim', o, w_ao)
        return r

    def _L0_attn_b_ref(X, W_qkv, b_qkv, W_out, b_out):
        import jax, jax.numpy as jnp
        import numpy as np
        B, L, E, H, D = (4, 256, 128, 16, 64)

        def alibi_matrix(n, n_heads, causal=True):
            idx = jnp.arange(n, dtype=jnp.float32)
            dists = -jnp.abs(idx[None, :] - idx[:, None])
            slopes = 2.0 ** (-jnp.linspace(1.0, 8.0, n_heads, dtype=jnp.float32))
            alibi = slopes[:, None, None] * dists[None, :, :]
            if causal:
                causal_ok = idx[:, None] >= idx[None, :]
                alibi = jnp.where(causal_ok[None, :, :], alibi, -jnp.inf)
            return alibi[None]
        b, l, _ = X.shape
        qkv = X @ W_qkv + b_qkv
        qkv = qkv.reshape(b, l, H, 3, D)
        Q, K, V = (qkv[..., 0, :], qkv[..., 1, :], qkv[..., 2, :])
        scale = D ** 0.5
        alibi = alibi_matrix(l, H, causal=True)
        scores = jnp.einsum('bqhd,bkhd->bhqk', Q, K) / scale + alibi
        weights = jax.nn.softmax(scores, axis=-1)
        attn = jnp.einsum('bhqk,bkhd->bqhd', weights, V)
        attn = attn.reshape(b, l, H * D)
        return attn @ W_out + b_out

    def _L0_ffn_ref(x, ln1_w, ln1_b, w_qkv, w_proj, ln2_w, ln2_b, gate_w, gate_b, w1, w2):
        import jax, jax.numpy as jnp
        import numpy as np
        B, N, D, H, E = (4, 128, 128, 16, 8)
        DK = D // H
        HID = 4 * D
        EPS = 1e-05

        def _layernorm(x, w, b):
            m = jnp.mean(x, axis=-1, keepdims=True)
            v = jnp.mean(jnp.square(x - m), axis=-1, keepdims=True)
            return (x - m) * jax.lax.rsqrt(v + EPS) * w + b

        def _msa(x, w_qkv, w_proj):
            b, n, d = x.shape
            qkv = (x @ w_qkv).reshape(b, n, 3, H, DK)
            q = qkv[:, :, 0].transpose(0, 2, 1, 3)
            k = qkv[:, :, 1].transpose(0, 2, 1, 3)
            v = qkv[:, :, 2].transpose(0, 2, 1, 3)
            attn = jnp.einsum('bhnd,bhmd->bhnm', q, k) * (1.0 / np.sqrt(DK))
            attn = jax.nn.softmax(attn, axis=-1)
            y = jnp.einsum('bhnm,bhmd->bhnd', attn, v)
            y = y.transpose(0, 2, 1, 3).reshape(b, n, d)
            return y @ w_proj

        def _moe_mlp(x, gate_w, gate_b, w1, w2):
            b, n, d = x.shape
            xf = x.reshape(b * n, d)
            logits = xf @ gate_w + gate_b
            one_hot = jax.nn.one_hot(jnp.argmax(logits, axis=-1), E, dtype=xf.dtype)
            h = jax.nn.gelu(jnp.einsum('td,edh->teh', xf, w1), approximate=True)
            y = jnp.einsum('teh,ehd->ted', h, w2)
            out = jnp.einsum('te,ted->td', one_hot, y)
            return out.reshape(b, n, d)
        x = x + _msa(_layernorm(x, ln1_w, ln1_b), w_qkv, w_proj)
        x = x + _moe_mlp(_layernorm(x, ln2_w, ln2_b), gate_w, gate_b, w1, w2)
        return x

    def _L1_attn_a_ref(x, Wq, bq, Wk, bk, Wv, bv, Wo, bo, scale):
        import jax, jax.numpy as jnp
        import numpy as np
        B, L, D, N = (2, 256, 128, 16)
        H = D // N
        THETA = 10000.0

        def apply_rope(x):
            l, h = (x.shape[-2], x.shape[-1])
            freqs = THETA ** (-jnp.arange(0, h, 2, dtype=jnp.float32) / h)
            ang = jnp.arange(l, dtype=jnp.float32)[:, None] * freqs
            cos, sin = (jnp.cos(ang), jnp.sin(ang))
            x_even = x[..., 0::2]
            x_odd = x[..., 1::2]
            out_even = cos * x_even - sin * x_odd
            out_odd = sin * x_even + cos * x_odd
            return jnp.stack((out_even, out_odd), axis=-1).reshape(x.shape)
        b, l, d = x.shape
        q = x @ Wq.T + bq
        k = x @ Wk.T + bk
        v = x @ Wv.T + bv
        q = q.reshape(b, l, N, H).transpose(0, 2, 1, 3)
        k = k.reshape(b, l, N, H).transpose(0, 2, 1, 3)
        v = v.reshape(b, l, N, H).transpose(0, 2, 1, 3)
        q = apply_rope(q) * scale
        k = apply_rope(k)
        dots = jnp.einsum('bnih,bnjh->bnij', q, k)
        i = jnp.arange(l)
        mask = i[:, None] < i[None, :]
        dots = jnp.where(mask, jnp.float32(-100000.0), dots)
        attn = jax.nn.softmax(dots, axis=-1)
        o = jnp.einsum('bnij,bnjh->bnih', attn, v)
        o = o.transpose(0, 2, 1, 3).reshape(b, l, d)
        return o @ Wo.T + bo

    def _L1_attn_b_ref(x, ln1_g, ln1_b, in_proj_w, conv_w, conv_b, x_proj_w, dt_proj_w, dt_proj_b, A_log, D_skip, out_proj_w, ln2_g, ln2_b, q_w, k_w, v_w, o_w, ln3_g, ln3_b, w1, w2, w3):
        import jax, jax.numpy as jnp
        import numpy as np
        EPS = 1e-05
        N_HEADS, KV_HEADS = (16, 4)

        def layernorm(x, g, b):
            m = jnp.mean(x, -1, keepdims=True)
            v = jnp.var(x, -1, keepdims=True)
            return (x - m) / jnp.sqrt(v + EPS) * g + b

        def mamba_block(x, ln_g, ln_b, in_w, conv_w, conv_b, xp_w, dt_w, dt_b, A_log, D_skip, out_w):
            Bsz, L, _ = x.shape
            d_inner = D_skip.shape[0]
            d_conv = conv_w.shape[-1]
            res = x
            h = layernorm(x, ln_g, ln_b)
            xs, gate = jnp.split(h @ in_w, 2, axis=-1)
            xc = jnp.pad(xs.transpose(0, 2, 1), ((0, 0), (0, 0), (d_conv - 1, 0)))
            xc = jax.lax.conv_general_dilated(xc, conv_w, (1,), 'VALID', dimension_numbers=('NCH', 'OIH', 'NCH'), feature_group_count=d_inner)
            xs = jax.nn.silu(xc.transpose(0, 2, 1) + conv_b)
            Bm, Cm = jnp.split(xs @ xp_w, 2, axis=-1)
            dt = jax.nn.softplus(Bm @ dt_w + dt_b)
            A = -jnp.exp(A_log)

            def step(hst, inp):
                xt, dtt, Bt, Ct = inp
                dA = jnp.exp(dtt[..., None] * A)
                hst = hst * dA + dtt[..., None] * Bt[:, None, :] * xt[..., None]
                yt = jnp.sum(hst * Ct[:, None, :], -1)
                return (hst, yt)
            h0 = jnp.zeros((Bsz, d_inner, A.shape[-1]), xs.dtype)
            _, y = jax.lax.scan(step, h0, (xs.transpose(1, 0, 2), dt.transpose(1, 0, 2), Bm.transpose(1, 0, 2), Cm.transpose(1, 0, 2)))
            y = y.transpose(1, 0, 2)
            y = (y + D_skip * xs) * jax.nn.silu(gate)
            return y @ out_w + res

        def attn_block(x, ln_g, ln_b, q_w, k_w, v_w, o_w):
            Bsz, L, D = x.shape
            H, KV = (N_HEADS, KV_HEADS)
            dh = D // H
            res = x
            h = layernorm(x, ln_g, ln_b)
            q = (h @ q_w).reshape(Bsz, L, H, dh).transpose(0, 2, 1, 3)
            k = (h @ k_w).reshape(Bsz, L, KV, dh).transpose(0, 2, 1, 3)
            v = (h @ v_w).reshape(Bsz, L, KV, dh).transpose(0, 2, 1, 3)
            inv = 1.0 / 10000.0 ** (jnp.arange(0, dh, 2, dtype=jnp.float32) / dh)
            fr = jnp.arange(L, dtype=jnp.float32)[:, None] * inv
            emb = jnp.concatenate([fr, fr], -1)
            cos, sin = (jnp.cos(emb), jnp.sin(emb))

            def rot(t):
                t1, t2 = jnp.split(t, 2, -1)
                return jnp.concatenate([-t2, t1], -1)
            q = q * cos + rot(q) * sin
            k = k * cos + rot(k) * sin
            g = H // KV
            k = jnp.repeat(k, g, axis=1)
            v = jnp.repeat(v, g, axis=1)
            sc = jnp.einsum('bhqd,bhkd->bhqk', q, k) / jnp.sqrt(jnp.float32(dh))
            mask = jnp.where(jnp.tril(jnp.ones((L, L), bool)), 0.0, -1000000000.0)
            p = jax.nn.softmax((sc + mask).astype(jnp.float32), -1).astype(q.dtype)
            o = jnp.einsum('bhqk,bhkd->bhqd', p, v).transpose(0, 2, 1, 3).reshape(Bsz, L, D)
            return o @ o_w + res
        x = mamba_block(x, ln1_g, ln1_b, in_proj_w, conv_w, conv_b, x_proj_w, dt_proj_w, dt_proj_b, A_log, D_skip, out_proj_w)
        x = attn_block(x, ln2_g, ln2_b, q_w, k_w, v_w, o_w)
        h = layernorm(x, ln3_g, ln3_b)
        return x + jax.nn.silu(h @ w1) * (h @ w3) @ w2

    def _L1_ffn_ref(x, Wq, bq, Wk, bk, Wv, bv, Wo, bo, ln1_g, ln1_b, ln2_g, ln2_b, gate_w, gate_b, W1, b1, W2, b2):
        import jax, jax.numpy as jnp
        import numpy as np
        import math
        B, S, D = (4, 256, 128)
        H = 16
        E = 8
        K = 2
        F = 512

        def _layernorm(x, g, b, eps=1e-05):
            mu = jnp.mean(x, axis=-1, keepdims=True)
            var = jnp.mean(jnp.square(x - mu), axis=-1, keepdims=True)
            return (x - mu) * jax.lax.rsqrt(var + eps) * g + b

        def _attention(x, Wq, bq, Wk, bk, Wv, bv, Wo, bo):
            b, s, d = x.shape
            dh = d // H
            q = (x @ Wq + bq).reshape(b, s, H, dh)
            k = (x @ Wk + bk).reshape(b, s, H, dh)
            v = (x @ Wv + bv).reshape(b, s, H, dh)
            scores = jnp.einsum('bqhd,bkhd->bhqk', q, k) / math.sqrt(dh)
            attn = jax.nn.softmax(scores, axis=-1)
            out = jnp.einsum('bhqk,bkhd->bqhd', attn, v).reshape(b, s, d)
            return out @ Wo + bo

        def _moe(x, gate_w, gate_b, W1, b1, W2, b2):
            b, s, d = x.shape
            xt = x.reshape(b * s, d)
            probs = jax.nn.softmax(xt @ gate_w + gate_b, axis=-1)
            top_v, top_i = jax.lax.top_k(probs, K)
            combine = jnp.sum(jax.nn.one_hot(top_i, E, dtype=xt.dtype) * top_v[..., None], axis=1)
            out = jnp.zeros_like(xt)
            for e in range(E):
                h = jax.nn.gelu(xt @ W1[e] + b1[e], approximate=False) @ W2[e] + b2[e]
                out = out + combine[:, e:e + 1] * h
            return out.reshape(b, s, d)
        x = x + _layernorm(_attention(x, Wq, bq, Wk, bk, Wv, bv, Wo, bo), ln1_g, ln1_b)
        x = x + _layernorm(_moe(x, gate_w, gate_b, W1, b1, W2, b2), ln2_g, ln2_b)
        return x
    x = L0_attn_a_x
    x = x + _L0_attn_a_ref(_layernorm(x, axis=-1), L0_attn_a_w_aq, L0_attn_a_w_ak, L0_attn_a_w_av, L0_attn_a_w_ao)
    x = x + _L0_ffn_ref(_layernorm(x, axis=-1), L0_ffn_ln1_w, L0_ffn_ln1_b, L0_ffn_w_qkv, L0_ffn_w_proj, L0_ffn_ln2_w, L0_ffn_ln2_b, L0_ffn_gate_w, L0_ffn_gate_b, L0_ffn_w1, L0_ffn_w2)
    x = x + _L0_attn_b_ref(_layernorm(x, axis=-1), L0_attn_b_W_qkv, L0_attn_b_b_qkv, L0_attn_b_W_out, L0_attn_b_b_out)
    x = x + _L0_ffn_ref(_layernorm(x, axis=-1), L0_ffn_ln1_w, L0_ffn_ln1_b, L0_ffn_w_qkv, L0_ffn_w_proj, L0_ffn_ln2_w, L0_ffn_ln2_b, L0_ffn_gate_w, L0_ffn_gate_b, L0_ffn_w1, L0_ffn_w2)
    x = x + _L1_attn_a_ref(_layernorm(x, axis=-1), L1_attn_a_Wq, L1_attn_a_bq, L1_attn_a_Wk, L1_attn_a_bk, L1_attn_a_Wv, L1_attn_a_bv, L1_attn_a_Wo, L1_attn_a_bo, L1_attn_a_scale)
    x = x + _L1_ffn_ref(_layernorm(x, axis=-1), L1_ffn_Wq, L1_ffn_bq, L1_ffn_Wk, L1_ffn_bk, L1_ffn_Wv, L1_ffn_bv, L1_ffn_Wo, L1_ffn_bo, L1_ffn_ln1_g, L1_ffn_ln1_b, L1_ffn_ln2_g, L1_ffn_ln2_b, L1_ffn_gate_w, L1_ffn_gate_b, L1_ffn_W1, L1_ffn_b1, L1_ffn_W2, L1_ffn_b2)
    x = x + _L1_attn_b_ref(_layernorm(x, axis=-1), L1_attn_b_ln1_g, L1_attn_b_ln1_b, L1_attn_b_in_proj_w, L1_attn_b_conv_w, L1_attn_b_conv_b, L1_attn_b_x_proj_w, L1_attn_b_dt_proj_w, L1_attn_b_dt_proj_b, L1_attn_b_A_log, L1_attn_b_D_skip, L1_attn_b_out_proj_w, L1_attn_b_ln2_g, L1_attn_b_ln2_b, L1_attn_b_q_w, L1_attn_b_k_w, L1_attn_b_v_w, L1_attn_b_o_w, L1_attn_b_ln3_g, L1_attn_b_ln3_b, L1_attn_b_w1, L1_attn_b_w2, L1_attn_b_w3)
    x = x + _L1_ffn_ref(_layernorm(x, axis=-1), L1_ffn_Wq, L1_ffn_bq, L1_ffn_Wk, L1_ffn_bk, L1_ffn_Wv, L1_ffn_bv, L1_ffn_Wo, L1_ffn_bo, L1_ffn_ln1_g, L1_ffn_ln1_b, L1_ffn_ln2_g, L1_ffn_ln2_b, L1_ffn_gate_w, L1_ffn_gate_b, L1_ffn_W1, L1_ffn_b1, L1_ffn_W2, L1_ffn_b2)
    return x

_drawn_inputs = setup_inputs


def setup_inputs(seed=0):
    import zlib

    import numpy as np

    out = dict(_drawn_inputs(seed))
    spreads = {'L0_attn_a_w_aq': (0.0, 0.498),
     'L0_attn_b_b_qkv': (0.0, 0.1),
     'L0_attn_b_b_out': (0.0, 0.1),
     'L0_ffn_ln1_w': (1.0, 0.6),
     'L0_ffn_ln1_b': (0.0, 0.299),
     'L0_ffn_ln2_w': (1.0, 0.2),
     'L0_ffn_ln2_b': (0.0, 0.327),
     'L0_ffn_gate_b': (0.0, 0.1),
     'L1_attn_b_ln1_g': (1.0, 0.6),
     'L1_attn_b_ln1_b': (0.0, 0.8),
     'L1_attn_b_conv_b': (0.0, 0.8),
     'L1_attn_b_dt_proj_b': (0.0, 0.8),
     'L1_attn_b_D_skip': (1.0, 0.6),
     'L1_attn_b_ln2_g': (1.0, 0.6),
     'L1_attn_b_ln2_b': (0.0, 0.8),
     'L1_attn_b_ln3_g': (1.0, 0.6),
     'L1_attn_b_ln3_b': (0.0, 0.8),
     'L1_ffn_bq': (0.0, 0.1),
     'L1_ffn_bk': (0.0, 0.8),
     'L1_ffn_bv': (0.0, 0.1),
     'L1_ffn_bo': (0.0, 0.1),
     'L1_ffn_ln1_g': (1.0, 0.2),
     'L1_ffn_ln1_b': (0.0, 0.1),
     'L1_ffn_ln2_g': (1.0, 0.2),
     'L1_ffn_ln2_b': (0.0, 0.1),
     'L1_ffn_gate_b': (0.0, 0.1),
     'L1_ffn_b1': (0.0, 0.268),
     'L1_ffn_b2': (0.0, 0.1)}
    factors = {'L0_attn_a_w_ak': 4.218,
     'L1_attn_a_Wq': 8.0,
     'L1_attn_a_bq': 8.0,
     'L1_attn_a_Wk': 8.0,
     'L1_attn_a_bk': 8.0,
     'L1_attn_a_Wv': 3.515,
     'L1_attn_a_bv': 5.671,
     'L1_attn_a_Wo': 3.051,
     'L1_attn_b_in_proj_w': 8.0,
     'L1_attn_b_conv_w': 8.0,
     'L1_attn_b_x_proj_w': 8.0,
     'L1_attn_b_dt_proj_w': 8.0,
     'L1_attn_b_A_log': 8.0,
     'L1_attn_b_out_proj_w': 8.0,
     'L1_attn_b_q_w': 8.0,
     'L1_attn_b_k_w': 8.0,
     'L1_attn_b_v_w': 8.0,
     'L1_attn_b_o_w': 8.0,
     'L1_attn_b_w1': 8.0,
     'L1_attn_b_w2': 8.0,
     'L1_attn_b_w3': 8.0}
    for name, (base, spread) in spreads.items():
        noise = np.random.default_rng([zlib.crc32(name.encode()), seed]).standard_normal(out[name].shape)
        drawn = base * np.exp(spread * noise) if base else spread * noise
        out[name] = jnp.asarray(drawn.astype(out[name].dtype))
    for name, factor in factors.items():
        out[name] = (out[name] * factor).astype(out[name].dtype)
    return out
```

```python
from contextlib import ExitStack

import concourse.bass as bass
from concourse import mybir
import numpy as np

F32 = mybir.dt.float32
BF16 = mybir.dt.bfloat16
ALU = mybir.AluOpType
ACT = mybir.ActivationFunctionType
AX = mybir.AxisListType

P = 128
SEQS, L, D = 16, 256, 128
TILES = SEQS * L // P
QT = L // P
TURNS = SEQS // 2
GT = 2 * QT
GN = GT * P
EPS = 1e-5
MASKED = -1e30


class Signal:

    def __init__(self, sem, per=1, lead=0):
        self.sem = sem
        self.per, self.lead = per, lead

    def at(self, i, k=1):
        return i * self.per + (k + self.lead)


class Chain:

    def __init__(self, eng, own, i):
        self.eng, self.own, self.i, self.n = eng, own, i, 0

    def step(self, ins):
        ins.then_inc(self.own.sem, 1)
        self.n += 1

    def settle(self):
        self.eng.wait_ge(self.own.sem, self.own.at(self.i, self.n))

    def counted(self):
        assert self.n == self.own.per, (self.n, self.own.per)


class Core:
    pass


def allocator(nc, ctx, prefix):
    held = []

    def clear():
        nc.clear_and_free_semaphores(held)
        nc.all_engine_barrier()

    ctx.callback(clear)

    def sb(name, shape, dt=F32):
        return ctx.enter_context(nc.sbuf_tensor(prefix + name, shape, dt))

    def ps(name, shape=(P, 512), dt=F32):
        return ctx.enter_context(nc.psum_tensor(prefix + name, list(shape), dt))

    def sig(name, per=1, lead=0):
        sem = nc.alloc_semaphore(prefix + name)
        held.append(sem)
        return Signal(sem, per, lead)

    return sb, ps, sig


def per_feature(t, k=0):
    return t[:, k:k + 1]


class Norm:
    def __init__(self, sb, sig, name, tiles=GT, per=1):
        self.tiles = tiles
        self.stats = sb(name + "_stats", [P, tiles, 6])
        self.mv = sb(name + "_mv", [P, tiles, 2])
        self.ve = sb(name + "_ve", [P, tiles])
        self.rstd = sb(name + "_rstd", [P, tiles])
        self.var_ready = sig(name + "_var_ready", per)
        self.rstd_ready = sig(name + "_rstd_ready", per)

    def statistics(self, dve, chain, hold, src):
        for t in range(self.tiles):
            chain.step(dve.bn_stats(self.stats[:, t, :], src(t)))
        chain.settle()
        dve.sem_inc(hold, 1)
        for t in range(self.tiles):
            chain.step(dve.bn_aggr(self.mv[:, t, :], self.stats[:, t, :]))
        chain.settle()
        dve.tensor_scalar(self.ve[:], self.mv[:, :, 1], EPS, None, ALU.add).then_inc(self.var_ready.sem, 1)

    def apply(self, dve, chain, i, s, src, dst):
        dve.wait_ge(self.rstd_ready.sem, self.rstd_ready.at(i, s + 1))
        for t in range(self.tiles):
            chain.step(dve.tensor_scalar(dst(t), src(t), self.mv[:, t, 0:1], self.rstd[:, t:t + 1],
                                         ALU.subtract, ALU.mult))

    def on_vector(self, dve, chain, hold, i, src, dst):
        self.statistics(dve, chain, hold, src)
        self.apply(dve, chain, i, 0, src, dst)

    def on_pool(self, pool, core, i, s=0):
        pool.wait_ge(self.var_ready.sem, self.var_ready.at(i, s + 1))
        pool.tensor_tensor(out=self.rstd[:], in0=self.ve[:], in1=core.minus_half[:, 0:self.tiles], op=ALU.pow)\
            .then_inc(self.rstd_ready.sem, 1)


NORM_STEPS = 3 * GT


def small_attention(nc, core, name, *, src, norms, affine, w, q_scale, bq=None, bk=None, bv=None,
                    rope=None, causal=False, finish, out_norm=None, prefetch=None):
    H, DH = 16, 8
    UNITS = QT * H // 2
    with ExitStack() as ctx:
        sb, ps, sig = allocator(nc, ctx, name)
        SRC = core.X if src == "X" else core.Y
        DST = core.X if finish == "X_plus" else core.Y
        fronts = ["h", "q"] + (["qr"] if rope else []) + ["k"] + (["kr"] if rope else []) + ["v"]
        tails = ["n0", "n1", "on", "out"]
        order = fronts + tails
        NORM_SLOTS = (0, 1, 3)
        at_slot = {"h": NORM_SLOTS[norms] + 1}
        for n, x in enumerate(fronts[1:]):
            at_slot[x] = at_slot["h"] + 1 + n
        T0 = at_slot["v"] + 1
        at_slot["n0"], at_slot["on"], at_slot["out"] = T0, T0 + 2, T0 + 3
        F = [ps("F0"), ps("F1")]
        S = [ps("S0"), ps("S1")]
        T = [ps("T0"), ps("T1")]
        O = [ps("O0"), ps("O1")]

        def bank(part):
            return F[order.index(part) % 2]

        raw = sb("raw", [P, QT, D])
        yn = sb("yn", [P, QT, D])
        hn = sb("hn", [P, QT, D]) if norms == 2 else yn
        hT = sb("hT", [P, L])
        qT = sb("qT", [P, 2, L])
        kT = sb("kT", [P, 2, L])
        rt = sb("rt", [P, 2, L]) if rope else None
        kblk = sb("kblk", [P, 2, H, L])
        Vp = sb("Vp", [P, GT, H, 32])
        nmax = sb("nmax", [P, 4, 2])
        prob = sb("prob", [P, 4, 2, L])
        probT = sb("probT", [P, 4, 2, L])
        oT = sb("oT", [P, 4, L])
        rden = sb("rden", [P, QT, H])
        on = sb("on", [P, QT, D])
        onT = sb("onT", [P, L])
        fin = sb("fin", [P, QT, D])

        lns = [Norm(sb, sig, f"ln{n}", QT, 2) for n in range(norms)]
        oln = Norm(sb, sig, "oln", QT, 2) if out_norm else None
        keeps = finish in ("y_plus", "y_norm")
        front_steps = norms * 3 * QT + (1 if rope else 0)
        tail_steps = 1 + (3 * QT + 2 if out_norm else 0)
        front_chain = sig("front_chain", 2 * front_steps)
        tail_chain = sig("tail_chain", 2 * tail_steps)
        hold = sig("hold").sem
        fetched, kept, normed = sig("fetched", 2), sig("kept", 2), sig("normed", 2)
        added = sig("added", 2)
        made = {x: sig("made_" + x, 2) for x in order}
        taken = {x: sig("taken_" + x, 2, 3) for x in order}
        ready = {x: sig("ready_" + x, 2) if rope else taken[x] for x in "qk"}
        zeroed = sig("zeroed")
        k_spread = sig("k_spread", 2)
        scored = sig("scored", 2 * UNITS, UNITS + 1)
        maxed = sig("maxed", 2 * UNITS)
        exped = sig("exped", 2 * UNITS, 4)
        turned = sig("turned", 2 * UNITS, 4)
        turn_copied = [sig(f"turn_copied{n}", UNITS, 2) for n in range(2)]
        pv_done = sig("pv_done", 2 * UNITS, 4)
        oT_copied = sig("oT_copied", 2, 1)
        block = ctx.enter_context(nc.Block())

        def keys(w_):
            return (w_ % UNITS // (H // 2) + 1) * P if causal else L

        def turns(eng, turn):
            turn(0, True, False)
            with eng.Fori(1, TURNS - 1) as i:
                turn(i, False, False)
            turn(TURNS - 1, False, True)

        @block.sync
        def _(sp):
            if prefetch:
                prefetch(sp)

        @block.gpsimd
        def _(pool):
            for s in range(2):
                pool.memset(kblk[:, s], 0.0).then_inc(zeroed.sem, 1)
            pool.wait_ge(zeroed.sem, 2)

            def front(i, s):
                for ln in lns:
                    ln.on_pool(pool, core, i, s)
                pool.wait_ge(ready["k"].sem, ready["k"].at(i, s + 1))
                pool.wait_ge(scored.sem, scored.at(i, (s - 1) * UNITS))
                for g in range(4):
                    rows = slice(32 * g, 32 * g + 32)
                    ins = pool.tensor_tensor(
                        out=kblk[rows, s % 2, 4 * g:4 * g + 4, :],
                        in0=kT[rows, s % 2, None, :].to_broadcast([32, 4, L]),
                        in1=core.head_mask[rows, :, None].to_broadcast([32, 4, L]), op=ALU.mult)
                ins.then_inc(k_spread.sem, 1)
                pool.wait_ge(k_spread.sem, k_spread.at(i, s + 1))

            def turn(i, first, last):
                for s in range(2):
                    if not (last and s == 1):
                        front(i, s + 1)
                    if oln and not (first and s == 0):
                        oln.on_pool(pool, core, i, s - 1)

            front(0, 0)
            turns(pool, turn)
            if oln:
                oln.on_pool(pool, core, TURNS - 1, 1)

        @block.scalar
        def _(act):
            for g in (exped, oT_copied, turn_copied[1]):
                act.sem_inc(g.sem, g.lead)
            for x in ("h", "on") + (() if rope else ("k",)):
                act.sem_inc(taken[x].sem, taken[x].lead)

            def front_h(i, s):
                act.wait_ge(made["h"].sem, made["h"].at(i, s + 1))
                if affine:
                    act.activation(hT[:], bank("h")[:, 0:L], ACT.Identity, scale=affine[0],
                                   bias=affine[1]).then_inc(taken["h"].sem, 1)
                else:
                    act.activation(hT[:], bank("h")[:, 0:L], ACT.Copy).then_inc(taken["h"].sem, 1)

            def front_k(i, s):
                act.wait_ge(made["k"].sem, made["k"].at(i, s + 1))
                if bk is not None:
                    act.activation(kT[:, s % 2, :], bank("k")[:, 0:L], ACT.Identity, bias=bk)\
                        .then_inc(taken["k"].sem, 1)
                else:
                    act.activation(kT[:, s % 2, :], bank("k")[:, 0:L], ACT.Copy).then_inc(taken["k"].sem, 1)

            def copy_turned(i, w_):
                act.wait_ge(turned.sem, turned.at(i, w_ + 1))
                act.wait_ge(pv_done.sem, pv_done.at(i, w_ - 3))
                act.activation(probT[:, w_ % 4, :, 0:keys(w_)],
                               T[1][:, 0:2 * keys(w_)].rearrange("p (j k) -> p j k", j=2), ACT.Copy)\
                    .then_inc(turn_copied[1].sem, 1)

            def tail_o(i, s):
                act.wait_ge(pv_done.sem, pv_done.at(i, (s + 1) * UNITS))
                for m in range(2):
                    ins = act.activation(oT[:, 2 * m:2 * m + 2, :], O[m][:].rearrange("p (g q) -> p g q", g=2),
                                         ACT.Copy)
                ins.then_inc(oT_copied.sem, 1)

            def tail_on(i, s):
                act.wait_ge(made["on"].sem, made["on"].at(i, s + 1))
                act.activation(onT[:], bank("on")[:, 0:L], ACT.Copy).then_inc(taken["on"].sem, 1)

            def turn(i, first, last):
                for w_ in range(2 * UNITS):
                    s, u = w_ // UNITS, w_ % UNITS
                    has_front, has_tail = not (last and s == 1), not (first and s == 0)
                    act.wait_ge(maxed.sem, maxed.at(i, w_ + 1))
                    act.wait_ge(turned.sem, turned.at(i, w_ - 3))
                    for j in range(2):
                        ins = act.activation(prob[:, w_ % 4, j, 0:keys(w_)],
                                             S[w_ % 2][:, j * keys(w_):(j + 1) * keys(w_)], ACT.Exp,
                                             bias=nmax[:, w_ % 4, j:j + 1])
                    ins.then_inc(exped.sem, 1)
                    if w_ % 2 == 1 and not (first and w_ < 2):
                        copy_turned(i, w_ - 2)
                    if has_tail and u == 2:
                        tail_o(i, s - 1)
                    if has_front and u == at_slot["h"]:
                        front_h(i, s + 1)
                    if has_front and not rope and u == at_slot["k"]:
                        front_k(i, s + 1)
                    if has_tail and u == at_slot["on"]:
                        tail_on(i, s - 1)

            front_h(0, 0)
            if not rope:
                front_k(0, 0)
            turns(act, turn)
            copy_turned(TURNS - 1, 2 * UNITS - 1)
            tail_o(TURNS - 1, 1)
            tail_on(TURNS - 1, 1)

        @block.vector
        def _(dve):
            dve.memset(Vp[:], 0.0).then_inc(zeroed.sem, 1)
            dve.wait_ge(zeroed.sem, 3)
            dve.memset(Vp[:, :, :, DH:DH + 1], 1.0).then_inc(zeroed.sem, 1)
            dve.wait_ge(zeroed.sem, 4)
            dve.sem_inc(turn_copied[0].sem, turn_copied[0].lead)
            for x in ("q", "v", "n0", "n1", "out") + (("qr", "k", "kr") if rope else ()):
                dve.sem_inc(taken[x].sem, taken[x].lead)

            def here(buf):
                return lambda t: buf[:, t, :]

            def stream(buf, i, s):
                return buf[:, bass.ds(i * GT + QT * s, QT), :]

            def front_norm(i, s, chain, part):
                if part == 0:
                    dve.tensor_scalar(raw[:], stream(SRC, i, s), 1.0, None, ALU.mult).then_inc(fetched.sem, 1)
                    dve.wait_ge(fetched.sem, fetched.at(i, s + 1))
                    lns[0].statistics(dve, chain, hold, here(raw))
                elif part == 1:
                    lns[0].apply(dve, chain, i, s, here(raw), here(yn))
                    chain.settle()
                    if keeps:
                        dve.tensor_scalar(stream(core.Y, i, s), yn[:], 1.0, None, ALU.mult).then_inc(kept.sem, 1)
                        dve.wait_ge(kept.sem, kept.at(i, s + 1))
                    if norms == 2:
                        dve.sem_inc(hold, 1)
                        lns[1].statistics(dve, chain, hold, here(yn))
                    else:
                        dve.sem_inc(normed.sem, 1)
                elif norms == 2:
                    lns[1].apply(dve, chain, i, s, here(yn), here(hn))
                    chain.settle()
                    dve.sem_inc(normed.sem, 1)

            def front_part(x, i, s, chain):
                if rope and x != "v":
                    a = x[0]
                    n = len(x) - 1
                    bias = (bq if a == "q" else bk)
                    dst = (qT if a == "q" else kT)[:, s % 2, :]
                    dve.wait_ge(made[x].sem, made[x].at(i, s + 1))
                    dve.scalar_tensor_tensor(out=rt[:, n, :], in0=bank(x)[:, 0:L],
                                             scalar=bias[n] if bias is not None else 0.0, in1=rope[n],
                                             op0=ALU.add, op1=ALU.mult).then_inc(taken[x].sem, 1)
                    if n == 1:
                        dve.wait_ge(taken[x].sem, taken[x].at(i, s + 1))
                        dve.wait_ge(taken[a].sem, taken[a].at(i, s + 1))
                        summed = dve.tensor_tensor(out=dst, in0=rt[:, 0], in1=rt[:, 1], op=ALU.add)
                        if a == "q":
                            chain.step(summed)
                            chain.settle()
                            dve.tensor_scalar(dst, dst, q_scale, None, ALU.mult).then_inc(ready["q"].sem, 1)
                        else:
                            summed.then_inc(ready["k"].sem, 1)
                        dve.wait_ge(ready[a].sem, ready[a].at(i, s + 1))
                elif x == "q":
                    dve.wait_ge(made["q"].sem, made["q"].at(i, s + 1))
                    dve.tensor_scalar(qT[:, s % 2, :], bank("q")[:, 0:L], bq if bq is not None else 0.0, q_scale,
                                      ALU.add, ALU.mult).then_inc(taken["q"].sem, 1)
                elif x == "v":
                    dve.wait_ge(made["v"].sem, made["v"].at(i, s + 1))
                    vsrc = bank("v")[:, 0:L].rearrange("p (t h d) -> p t h d", t=QT, h=H)
                    for t in range(QT):
                        dst = Vp[:, s % 2 * QT + t, :, 0:DH]
                        if bv is not None:
                            ins = dve.tensor_tensor(out=dst, in0=vsrc[:, t],
                                                    in1=bv[:].rearrange("p (h d) -> p h d", h=H), op=ALU.add)
                        else:
                            ins = dve.tensor_copy(dst, vsrc[:, t])
                    ins.then_inc(taken["v"].sem, 1)

            def tail_n(i, s, chain):
                nat = [bank(f"n{t}")[:].rearrange("p (h r) -> p h r", h=H) for t in range(QT)]
                for t in range(QT):
                    dve.wait_ge(made[f"n{t}"].sem, made[f"n{t}"].at(i, s + 1))
                    ins = dve.reciprocal(rden[:, t, :], nat[t][:, :, DH])
                chain.step(ins)
                chain.settle()
                for t in range(QT):
                    dve.tensor_tensor(out=on[:, t, :].rearrange("p (h d) -> p h d", h=H), in0=nat[t][:, :, 0:DH],
                                      in1=rden[:, t, :, None].to_broadcast([P, H, DH]), op=ALU.mult)\
                        .then_inc(taken[f"n{t}"].sem, 1)

            def tail_out(i, s, chain, part):
                got = bank("out")[:, 0:L].rearrange("p (t d) -> p t d", t=QT)
                onto = stream(DST, i, s)
                if part == 0:
                    dve.wait_ge(made["out"].sem, made["out"].at(i, s + 1))
                    if finish in ("y_plus", "Y_plus"):
                        dve.tensor_tensor(out=onto, in0=got, in1=onto, op=ALU.add).then_inc(taken["out"].sem, 1)
                        return
                    dve.tensor_tensor(out=fin[:], in0=got, in1=w["bo"][:, None, :].to_broadcast([P, QT, D]),
                                      op=ALU.add).then_inc(taken["out"].sem, 1)
                    dve.wait_ge(taken["out"].sem, taken["out"].at(i, s + 1))
                    if oln:
                        dve.sem_inc(hold, 1)
                        oln.statistics(dve, chain, hold, here(fin))
                        return
                elif not oln:
                    return
                else:
                    oln.apply(dve, chain, i, s, here(fin), here(fin))
                    chain.settle()
                    for other, op in ((out_norm[0], ALU.mult), (out_norm[1], ALU.add)):
                        chain.step(dve.tensor_tensor(out=fin[:], in0=fin[:],
                                                     in1=other[:, None, :].to_broadcast([P, QT, D]), op=op))
                        chain.settle()
                dve.tensor_tensor(out=onto, in0=fin[:], in1=onto, op=ALU.add).then_inc(added.sem, 1)
                dve.wait_ge(added.sem, added.at(i, s + 1))

            def chain_of(signal, i, s, n):
                c = Chain(dve, signal, i)
                c.n = s * n
                return c

            def maximum(i, w_):
                dve.wait_ge(scored.sem, scored.at(i, w_ + 1))
                dve.wait_ge(exped.sem, exped.at(i, w_ - 3))
                dve.tensor_reduce(out=nmax[:, w_ % 4, :],
                                  in_=S[w_ % 2][:, 0:2 * keys(w_)].rearrange("p (j k) -> p j k", j=2),
                                  op=ALU.max, axis=AX.X, negate=True).then_inc(maxed.sem, 1)

            def copy_turned(i, w_):
                dve.wait_ge(turned.sem, turned.at(i, w_ + 1))
                dve.wait_ge(pv_done.sem, pv_done.at(i, w_ - 3))
                dve.tensor_copy(probT[:, w_ % 4, :, 0:keys(w_)],
                                T[w_ % 2][:, 0:2 * keys(w_)].rearrange("p (j k) -> p j k", j=2))\
                    .then_inc(turn_copied[0].sem, 1)

            def turn(i, first, last):
                for s in range(2):
                    fc = chain_of(front_chain, i, s + 1, front_steps)
                    tc = chain_of(tail_chain, i, s - 1, tail_steps)
                    for u in range(UNITS):
                        w_ = s * UNITS + u
                        maximum(i, w_)
                        if w_ % 2 == 0 and not (first and w_ < 2):
                            copy_turned(i, w_ - 2)
                        if not (last and s == 1):
                            if u in NORM_SLOTS:
                                front_norm(i, s + 1, fc, NORM_SLOTS.index(u))
                            for x in fronts[1:]:
                                if u == at_slot[x]:
                                    front_part(x, i, s + 1, fc)
                        if not (first and s == 0):
                            if u == at_slot["n0"] + 1:
                                tail_n(i, s - 1, tc)
                            if u == at_slot["out"]:
                                tail_out(i, s - 1, tc, 0)
                            if u == at_slot["out"] + 1:
                                tail_out(i, s - 1, tc, 1)
                    assert (last and s == 1) or fc.n == (s + 2) * front_steps, (fc.n, front_steps)
                    assert (first and s == 0) or tc.n <= s * tail_steps, (tc.n, tail_steps)

            fc = chain_of(front_chain, 0, 0, front_steps)
            for part in range(3):
                front_norm(0, 0, fc, part)
            for x in fronts[1:]:
                front_part(x, 0, 0, fc)
            turns(dve, turn)
            copy_turned(TURNS - 1, 2 * UNITS - 2)
            tc = chain_of(tail_chain, TURNS - 1, 1, tail_steps)
            tail_n(TURNS - 1, 1, tc)
            for part in range(2):
                tail_out(TURNS - 1, 1, tc, part)

        @block.tensor
        def _(pe):
            for g in (scored, turned, pv_done):
                pe.sem_inc(g.sem, g.lead)

            def claim(x, i, s, no_front=False):
                n = order.index(x) - 2
                if x in fronts:
                    prev, k = order[n], s + 1 if n >= 0 else s - 2
                elif n >= len(fronts):
                    prev, k = order[n], s + 1
                elif no_front:
                    prev, k = order[n + len(tails)], s
                else:
                    prev, k = order[n], s + 3
                pe.wait_ge(taken[prev].sem, taken[prev].at(i, k))

            def front_part(x, i, s):
                if x == "h":
                    pe.wait_ge(normed.sem, normed.at(i, s + 1))
                    claim("h", i, s)
                    for t in range(QT):
                        ins = pe.transpose(bank("h")[:, t * P:(t + 1) * P], hn[:, t, :], core.ident[:])
                    ins.then_inc(made["h"].sem, 1)
                    return
                pe.wait_ge(taken["h"].sem, taken["h"].at(i, s + 1))
                claim(x, i, s)
                if x == "v":
                    for t in range(QT):
                        ins = pe.matmul(bank("v")[:, t * P:(t + 1) * P], hT[:, t * P:(t + 1) * P], w["v"][:],
                                        start=True, stop=True)
                    ins.then_inc(made["v"].sem, 1)
                else:
                    pe.matmul(bank(x)[:, 0:L], w[x][:], hT[:], start=True, stop=True).then_inc(made[x].sem, 1)

            def tail_part(x, i, s, no_front=False):
                if x == "n0":
                    pe.wait_ge(oT_copied.sem, oT_copied.at(i, s + 1))
                    for t in range(QT):
                        claim(f"n{t}", i, s, no_front)
                        for g in range(4):
                            ins = pe.transpose(bank(f"n{t}")[:, g * P:(g + 1) * P], oT[:, g, t * P:(t + 1) * P],
                                               core.ident[:])
                        ins.then_inc(made[f"n{t}"].sem, 1)
                elif x == "on":
                    for t in range(QT):
                        pe.wait_ge(taken[f"n{t}"].sem, taken[f"n{t}"].at(i, s + 1))
                    for t in range(QT):
                        ins = pe.transpose(bank("on")[:, t * P:(t + 1) * P], on[:, t, :], core.ident[:])
                    ins.then_inc(made["on"].sem, 1)
                else:
                    pe.wait_ge(taken["on"].sem, taken["on"].at(i, s + 1))
                    claim("out", i, s)
                    for t in range(QT):
                        ins = pe.matmul(bank("out")[:, t * P:(t + 1) * P], onT[:, t * P:(t + 1) * P], w["o"][:],
                                        start=True, stop=True)
                    ins.then_inc(made["out"].sem, 1)

            def score(i, w_):
                s, u = w_ // UNITS, w_ % UNITS
                t, pair = u // (H // 2), u % (H // 2)
                if u == 0:
                    pe.wait_ge(ready["q"].sem, ready["q"].at(i, s + 1))
                    pe.wait_ge(taken["v"].sem, taken["v"].at(i, s + 1))
                    pe.wait_ge(k_spread.sem, k_spread.at(i, s + 1))
                pe.wait_ge(exped.sem, exped.at(i, w_ - 1))
                out = S[w_ % 2][:, 0:2 * keys(w_)]
                ins = pe.matmul(out, qT[:, s % 2, t * P:(t + 1) * P], kblk[:, s % 2, 2 * pair:2 * pair + 2, 0:keys(w_)],
                                start=True, stop=not causal)
                if causal:
                    ins = pe.matmul(out.rearrange("p (j k) -> p j k", j=2)[:, :, t * P:(t + 1) * P],
                                    core.ident16[:], core.causal16[:, None, :].to_broadcast([P, 2, P]),
                                    start=False, stop=True)
                ins.then_inc(scored.sem, 1)

            def turn_unit(i, w_):
                pe.wait_ge(exped.sem, exped.at(i, w_ + 1))
                pe.wait_ge(turn_copied[w_ % 2].sem, turn_copied[w_ % 2].at(i, w_ // 2))
                for j in range(2):
                    for kt in range(keys(w_) // P):
                        ins = pe.transpose(T[w_ % 2][:, j * keys(w_) + kt * P:j * keys(w_) + (kt + 1) * P],
                                           prob[:, w_ % 4, j, kt * P:(kt + 1) * P], core.ident[:])
                ins.then_inc(turned.sem, 1)

            def weigh(i, w_):
                s, u = w_ // UNITS, w_ % UNITS
                t, pair = u // (H // 2), u % (H // 2)
                pe.wait_ge(turn_copied[w_ % 2].sem, turn_copied[w_ % 2].at(i, w_ // 2 + 1))
                if u == 0:
                    pe.wait_ge(oT_copied.sem, oT_copied.at(i, s))
                for kt in range(keys(w_) // P):
                    for j in range(2):
                        h = 2 * pair + j
                        g, c = h // 4, h % 4
                        ins = pe.matmul(O[g // 2][32 * c:32 * c + 32, (g % 2) * L + t * P:(g % 2) * L + (t + 1) * P],
                                        Vp[:, s % 2 * QT + kt, h, :], probT[:, w_ % 4, j, kt * P:(kt + 1) * P],
                                        start=kt == 0, stop=kt == keys(w_) // P - 1)
                ins.then_inc(pv_done.sem, 1)

            def turn(i, first, last):
                for w_ in range(2 * UNITS):
                    s, u = w_ // UNITS, w_ % UNITS
                    score(i, w_)
                    if not (first and w_ < 2):
                        turn_unit(i, w_ - 2)
                    if not (first and w_ < 3):
                        weigh(i, w_ - 3)
                    if not (last and s == 1):
                        for x in fronts:
                            if u == at_slot[x]:
                                front_part(x, i, s + 1)
                    if not (first and s == 0):
                        for x in ("n0", "on", "out"):
                            if u == at_slot[x]:
                                tail_part(x, i, s - 1, last and s == 1)

            for x in fronts:
                front_part(x, 0, 0)
            turns(pe, turn)
            for w_ in range(2 * UNITS, 2 * UNITS + 3):
                if w_ - 2 < 2 * UNITS:
                    turn_unit(TURNS - 1, w_ - 2)
                weigh(TURNS - 1, w_ - 3)
            for x in ("n0", "on", "out"):
                tail_part(x, TURNS - 1, 1, True)


def wide_attention(nc, core, name, *, heads_per_step, w, w_loaded, rope=None, bq=None, bk=None, bv=None,
                   q_scale=1.0, slopes=None, bo=None, prefetch=None):
    STEPS = 8
    HS = heads_per_step
    DH = P // HS
    VS = 4
    US = 2 * HS
    UNITS = STEPS * US
    W0, W1 = P, 2 * P
    WIDE = W0 + W1
    with ExitStack() as ctx:
        sb, ps, sig = allocator(nc, ctx, name)
        F = [ps("F0"), ps("F1")]
        S = [ps("S0"), ps("S1")]
        T = ps("T")
        O = [ps("O0"), ps("O1")]
        Z = ps("Z")
        uses = [("h", 0)] + [(x, m) for m in range(STEPS) for x in "qkv"] + [("out", 0)]

        raw = sb("raw", [P, GT, D])
        yn = sb("yn", [P, GT, D])
        hT = sb("hT", [P, GN])
        qT = sb("qT", [P, 2, GN])
        kT = sb("kT", [P, 2, HS, GN])
        rt = sb("rt", [P, 2, 2, GN]) if rope else None
        V = sb("V", [P, VS, GT, P])
        biased = sb("biased", [P, 2, WIDE]) if slopes else None
        nmax = sb("nmax", [P, 4, 2])
        total = sb("total", [P, 4, 2])
        rden = sb("rden", [P, 4, 2])
        prob = sb("prob", [P, 4, WIDE])
        probT = sb("probT", [P, 4, WIDE])
        oT = sb("oT", [P, 2, GN])
        yT = sb("yT", [P, GN])
        fin = sb("fin", [P, GT, D])

        ln = Norm(sb, sig, "ln")
        chained = sig("chained", NORM_STEPS + (1 if bo is not None else 0))
        hold = sig("hold").sem
        fetched, normed, streamed = sig("fetched"), sig("normed"), sig("streamed")
        made = {"h": sig("made_h"), "q": sig("made_q", STEPS), "k": sig("made_k", STEPS),
                "v": sig("made_v", STEPS), "out": sig("made_out")}
        taken = {"h": sig("taken_h", 1, 1), "q": sig("taken_q", STEPS, 1), "k": sig("taken_k", STEPS, 1),
                 "v": sig("taken_v", STEPS, 1), "out": sig("taken_out", 1, 1)}
        ready = {x: sig("ready_" + x, STEPS, 1) if rope else taken[x] for x in "qk"}
        k_zeroed = sig("k_zeroed")
        scored = sig("scored", UNITS, 2 * US)
        biased_up = sig("biased_up", UNITS, 2) if slopes else None
        maxed = sig("maxed", UNITS)
        exped = sig("exped", UNITS, 4)
        inverted = sig("inverted", UNITS)
        divided = sig("divided", UNITS)
        turned = sig("turned", UNITS, 4)
        turn_copied = sig("turn_copied", UNITS, 4)
        pv_done = sig("pv_done", UNITS, VS * US)
        oT_copied = sig("oT_copied", STEPS, 2)
        projected = sig("projected", STEPS, 2)
        yT_copied = sig("yT_copied", 1, 1)
        block = ctx.enter_context(nc.Block())

        parts = ((0, W0), (W0, WIDE))

        @block.sync
        def _(sp):
            if prefetch:
                prefetch(sp)

        def bank(x, m):
            return F[uses.index((x, m)) % 2]

        @block.gpsimd
        def _(pool):
            if rope:
                for x in "qk":
                    pool.sem_inc(ready[x].sem, ready[x].lead)
            with pool.Fori(0, TURNS) as i:
                ln.on_pool(pool, core, i)

                def rotate(m):
                    for n, x in enumerate("qk"):
                        pool.wait_ge(taken[x].sem, taken[x].at(i, m + 1))
                        pool.wait_ge(scored.sem, scored.at(i, (m - 1) * US))
                        dst = qT[:, m % 2, :] if x == "q" else kT[:, m % 2, 0, :]
                        pool.tensor_tensor(out=dst, in0=rt[:, n, 0, :], in1=rt[:, n, 1, :], op=ALU.add)\
                            .then_inc(ready[x].sem, 1)

                if rope:
                    rotate(0)
                for w_ in range(UNITS):
                    if rope and w_ % US == US - 1 and w_ // US + 1 < STEPS:
                        rotate(w_ // US + 1)
                    pool.wait_ge(inverted.sem, inverted.at(i, w_ + 1))
                    for n, (a, b) in enumerate(parts):
                        ins = pool.tensor_tensor(out=prob[:, w_ % 4, a:b], in0=prob[:, w_ % 4, a:b],
                                                 in1=rden[:, w_ % 4, n:n + 1].to_broadcast([P, b - a]), op=ALU.mult)
                    ins.then_inc(divided.sem, 1)

        @block.scalar
        def _(act):
            for g in (taken["h"], exped, oT_copied, yT_copied) + (() if rope else (taken["k"],)) \
                    + ((taken["v"],) if bv is None else ()):
                act.sem_inc(g.sem, g.lead)
            if HS == 2:
                act.wait_ge(k_zeroed.sem, 1)
            with act.Fori(0, TURNS) as i:
                act.wait_ge(made["h"].sem, made["h"].at(i))
                act.activation(hT[:], bank("h", 0)[:], ACT.Copy).then_inc(taken["h"].sem, 1)

                def evacuate(m):
                    if not rope:
                        act.wait_ge(made["k"].sem, made["k"].at(i, m + 1))
                        act.wait_ge(scored.sem, scored.at(i, (m - 1) * US))
                        for j in range(HS):
                            rows = slice(j * DH, (j + 1) * DH)
                            ins = act.activation(kT[rows, m % 2, j, :], bank("k", m)[rows, :], ACT.Identity,
                                                 bias=bk[rows, m:m + 1])
                        ins.then_inc(taken["k"].sem, 1)
                    if bv is None:
                        act.wait_ge(made["v"].sem, made["v"].at(i, m + 1))
                        act.wait_ge(pv_done.sem, pv_done.at(i, (m + 1 - VS) * US))
                        act.activation(V[:, m % VS], bank("v", m)[:].rearrange("p (t d) -> p t d", t=GT),
                                       ACT.Copy).then_inc(taken["v"].sem, 1)

                def copy_out(m):
                    act.wait_ge(pv_done.sem, pv_done.at(i, (m + 1) * US))
                    act.wait_ge(projected.sem, projected.at(i, m - 1))
                    act.activation(oT[:, m % 2, :], O[m % 2][:], ACT.Copy).then_inc(oT_copied.sem, 1)

                evacuate(0)
                for w_ in range(UNITS + 4):
                    if w_ < UNITS:
                        act.wait_ge(maxed.sem, maxed.at(i, w_ + 1))
                        act.wait_ge(turned.sem, turned.at(i, w_ - 3))
                        for n, (a, b) in enumerate(parts):
                            src = biased[:, w_ % 2, a:b] if slopes else S[w_ % 2][:, a:b]
                            ins = act.activation(prob[:, w_ % 4, a:b], src, ACT.Exp,
                                                 bias=nmax[:, w_ % 4, n:n + 1],
                                                 accum_out=total[:, w_ % 4, n:n + 1])
                        ins.then_inc(exped.sem, 1)
                        if w_ % US == 0 and w_ // US + 1 < STEPS:
                            evacuate(w_ // US + 1)
                    if w_ >= 4 and (w_ - 4) % US == US - 1:
                        copy_out((w_ - 4) // US)
                act.wait_ge(projected.sem, projected.at(i, STEPS))
                act.activation(yT[:], Z[:], ACT.Copy).then_inc(yT_copied.sem, 1)

        @block.vector
        def _(dve):
            if HS == 2:
                dve.memset(kT[:], 0.0).then_inc(k_zeroed.sem, 1)
            for g in (taken["q"], taken["out"], turn_copied) + ((taken["k"],) if rope else ()) \
                    + ((taken["v"],) if bv is not None else ()) + ((biased_up,) if slopes else ()):
                dve.sem_inc(g.sem, g.lead)
            with dve.Fori(0, TURNS) as i:
                chain = Chain(dve, chained, i)

                def here(buf):
                    return lambda t: buf[:, t, :]

                dve.tensor_copy(raw[:], core.X[:, bass.ds(i * GT, GT), :]).then_inc(fetched.sem, 1)
                dve.wait_ge(fetched.sem, fetched.at(i))
                ln.on_vector(dve, chain, hold, i, here(raw), here(yn))
                chain.settle()
                dve.sem_inc(normed.sem, 1)

                def evacuate(m):
                    if rope:
                        for n, x in enumerate("qk"):
                            cos, sin = rope[n]
                            psum = bank(x, m)[:].rearrange("p (s q) -> p s q", s=2)
                            dve.wait_ge(made[x].sem, made[x].at(i, m + 1))
                            dve.wait_ge(ready[x].sem, ready[x].at(i, m))
                            dve.tensor_tensor(out=rt[:, n, 0, :].rearrange("p (s q) -> p s q", s=2), in0=psum,
                                              in1=cos[:, None, :].to_broadcast([P, 2, L]), op=ALU.mult)
                            for lo, hi in ((0, P // 2), (P // 2, 0)):
                                ins = dve.tensor_tensor(
                                    out=rt[lo:lo + P // 2, n, 1, :].rearrange("p (s q) -> p s q", s=2),
                                    in0=psum[hi:hi + P // 2],
                                    in1=sin[hi:hi + P // 2, None, :].to_broadcast([P // 2, 2, L]), op=ALU.mult)
                            ins.then_inc(taken[x].sem, 1)
                    else:
                        dve.wait_ge(made["q"].sem, made["q"].at(i, m + 1))
                        dve.wait_ge(scored.sem, scored.at(i, (m - 1) * US))
                        dve.tensor_scalar(qT[:, m % 2, :], bank("q", m)[:], bq[:, m:m + 1], q_scale,
                                          ALU.add, ALU.mult).then_inc(taken["q"].sem, 1)
                    if bv is not None:
                        dve.wait_ge(made["v"].sem, made["v"].at(i, m + 1))
                        dve.wait_ge(pv_done.sem, pv_done.at(i, (m + 1 - VS) * US))
                        dve.tensor_tensor(out=V[:, m % VS], in0=bank("v", m)[:].rearrange("p (t d) -> p t d", t=GT),
                                          in1=bv[:, None, m * P:(m + 1) * P].to_broadcast([P, GT, P]),
                                          op=ALU.add).then_inc(taken["v"].sem, 1)

                evacuate(0)
                for w_ in range(UNITS + 2):
                    if w_ < UNITS:
                        dve.wait_ge(scored.sem, scored.at(i, w_ + 1))
                        src = S[w_ % 2]
                        if slopes:
                            m, j = w_ // US, w_ % HS
                            dve.wait_ge(exped.sem, exped.at(i, w_ - 1))
                            dve.scalar_tensor_tensor(out=biased[:, w_ % 2, :], in0=core.distance[:],
                                                     scalar=slopes[m * HS + j], in1=S[w_ % 2][:, 0:WIDE],
                                                     op0=ALU.mult, op1=ALU.add).then_inc(biased_up.sem, 1)
                            dve.wait_ge(biased_up.sem, biased_up.at(i, w_ + 1))
                            src = biased[:, w_ % 2]
                        dve.wait_ge(exped.sem, exped.at(i, w_ - 3))
                        for n, (a, b) in enumerate(parts):
                            ins = dve.tensor_reduce(out=nmax[:, w_ % 4, n:n + 1], in_=src[:, a:b], op=ALU.max,
                                                    axis=AX.X, negate=True)
                        ins.then_inc(maxed.sem, 1)
                        if w_ % US == 0 and w_ // US + 1 < STEPS:
                            evacuate(w_ // US + 1)
                    if 1 <= w_ <= UNITS:
                        dve.wait_ge(exped.sem, exped.at(i, w_))
                        dve.reciprocal(rden[:, (w_ - 1) % 4, :], total[:, (w_ - 1) % 4, :]).then_inc(inverted.sem, 1)
                    if w_ >= 2:
                        dve.wait_ge(turned.sem, turned.at(i, w_ - 1))
                        dve.wait_ge(pv_done.sem, pv_done.at(i, w_ - 5))
                        dve.tensor_copy(probT[:, (w_ - 2) % 4, :], T[:, 0:WIDE]).then_inc(turn_copied.sem, 1)
                dve.wait_ge(made["out"].sem, made["out"].at(i))
                dve.tensor_tensor(out=fin[:], in0=bank("out", 0)[:].rearrange("p (t d) -> p t d", t=GT), in1=raw[:],
                                  op=ALU.add).then_inc(taken["out"].sem, 1)
                dve.wait_ge(taken["out"].sem, taken["out"].at(i))
                if bo is not None:
                    chain.step(dve.tensor_tensor(out=fin[:], in0=fin[:], in1=bo[:, None, :].to_broadcast([P, GT, D]),
                                                 op=ALU.add))
                    chain.settle()
                dve.sem_inc(hold, 1)
                dve.tensor_copy(core.X[:, bass.ds(i * GT, GT), :], fin[:]).then_inc(streamed.sem, 1)
                dve.wait_ge(streamed.sem, streamed.at(i))
                dve.sem_inc(hold, 1)
                chain.counted()

        @block.tensor
        def _(pe):
            for g in (scored, turned, pv_done, projected):
                pe.sem_inc(g.sem, g.lead)
            pe.wait_ge(w_loaded[0], w_loaded[1])
            with pe.Fori(0, TURNS) as i:
                def claim(x, m):
                    y, n = uses[uses.index((x, m)) - 2]
                    if uses.index((x, m)) >= 2:
                        pe.wait_ge(taken[y].sem, taken[y].at(i, n + 1))
                    else:
                        pe.wait_ge(taken[y].sem, taken[y].at(i, 0))

                pe.wait_ge(normed.sem, normed.at(i))
                claim("h", 0)
                for t in range(GT):
                    ins = pe.transpose(bank("h", 0)[:, t * P:(t + 1) * P], yn[:, t, :], core.ident[:])
                ins.then_inc(made["h"].sem, 1)
                pe.wait_ge(taken["h"].sem, taken["h"].at(i))

                def project(m):
                    cols = slice(m * P, (m + 1) * P)
                    for x in "qk":
                        claim(x, m)
                        pe.matmul(bank(x, m)[:], w[x][:, cols], hT[:], start=True, stop=True)\
                            .then_inc(made[x].sem, 1)
                    claim("v", m)
                    for t in range(GT):
                        ins = pe.matmul(bank("v", m)[:, t * P:(t + 1) * P], hT[:, t * P:(t + 1) * P],
                                        w["v"][:, cols], start=True, stop=True)
                    ins.then_inc(made["v"].sem, 1)

                def unit(w_):
                    return w_ // US, (w_ % US) // HS, w_ % HS

                def score(w_):
                    m, s, j = unit(w_)
                    if w_ % US == 0:
                        for x in "qk":
                            pe.wait_ge(ready[x].sem, ready[x].at(i, m + 1))
                    if slopes:
                        pe.wait_ge(biased_up.sem, biased_up.at(i, w_ - 1))
                    else:
                        pe.wait_ge(exped.sem, exped.at(i, w_ - 1))
                    for t, (a, b) in enumerate(parts):
                        ins = pe.matmul(S[w_ % 2][:, a:b], qT[:, m % 2, s * L + t * P:s * L + (t + 1) * P],
                                        kT[:, m % 2, j, s * L:s * L + b - a], start=True, stop=bool(slopes))
                        if not slopes:
                            ins = pe.matmul(S[w_ % 2][:, b - P:b], core.ident16[:], core.causal16[:],
                                            start=False, stop=True)
                    ins.then_inc(scored.sem, 1)

                def turn(w_):
                    pe.wait_ge(divided.sem, divided.at(i, w_ + 1))
                    pe.wait_ge(turn_copied.sem, turn_copied.at(i, w_))
                    for n in range(3):
                        ins = pe.transpose(T[:, n * P:(n + 1) * P], prob[:, w_ % 4, n * P:(n + 1) * P], core.ident[:])
                    ins.then_inc(turned.sem, 1)

                def weigh(w_):
                    m, s, j = unit(w_)
                    pe.wait_ge(turn_copied.sem, turn_copied.at(i, w_ + 1))
                    if w_ % US == 0:
                        pe.wait_ge(taken["v"].sem, taken["v"].at(i, m + 1))
                        pe.wait_ge(oT_copied.sem, oT_copied.at(i, m - 1))
                    out = O[m % 2][j * DH:(j + 1) * DH, :]
                    cols = slice(j * DH, (j + 1) * DH)
                    pe.matmul(out[:, s * L:(s + 1) * L], V[:, m % VS, s * QT, cols], probT[:, w_ % 4, 0:L],
                              start=True, stop=False)
                    pe.matmul(out[:, s * L + P:(s + 1) * L], V[:, m % VS, s * QT + 1, cols], probT[:, w_ % 4, L:WIDE],
                              start=False, stop=True).then_inc(pv_done.sem, 1)

                def output(m):
                    pe.wait_ge(oT_copied.sem, oT_copied.at(i, m + 1))
                    if m == 0:
                        pe.wait_ge(yT_copied.sem, yT_copied.at(i, 0))
                    pe.matmul(Z[:], w["o"][:, m, :], oT[:, m % 2, :], start=m == 0, stop=m == STEPS - 1)\
                        .then_inc(projected.sem, 1)

                project(0)
                for w_ in range(UNITS + 5):
                    if w_ < UNITS:
                        score(w_)
                        if w_ % US == 0 and w_ // US + 1 < STEPS:
                            project(w_ // US + 1)
                    if 2 <= w_ < UNITS + 2:
                        turn(w_ - 2)
                    if 3 <= w_ < UNITS + 3:
                        weigh(w_ - 3)
                    if w_ >= 5 and (w_ - 5) % US == US - 1:
                        output((w_ - 5) // US)
                pe.wait_ge(yT_copied.sem, yT_copied.at(i))
                claim("out", 0)
                for t in range(GT):
                    ins = pe.transpose(bank("out", 0)[:, t * P:(t + 1) * P], yT[:, t * P:(t + 1) * P], core.ident[:])
                ins.then_inc(made["out"].sem, 1)


def experts(nc, core, name, *, affine, normed_in, w_loaded, gate, gate_b, act_fn, top, b1=None, b2=None,
            out_norm=None, prefetch=None):
    E, FC = 8, 4
    with ExitStack() as ctx:
        sb, ps, sig = allocator(nc, ctx, name)
        steps = ["h", "logit"] + (["comb", "bias"] if top == 2 else [])
        F = [ps("F0"), ps("F1")]
        H = [ps(f"H{n}") for n in range(FC)]
        YB = [ps("Y0"), ps("Y1")]

        def bank(s):
            return F[steps.index(s) % 2]

        raw = sb("raw", [P, GT, D])
        yn = sb("yn", [P, GT, D]) if normed_in else raw
        hT = sb("hT", [P, GN])
        hidden = sb("hidden", [P, 2, FC, GN])
        acc = sb("acc", [P, GT, D])
        fin = sb("fin", [P, GT, D])
        lg = sb("lg", [P, GT, E])
        pr = sb("pr", [P, GT, E])
        pick = sb("pick", [P, 2, GT, E])
        tmp = sb("tmp", [P, GT, E])
        top_v = sb("top_v", [P, GT])
        comb = sb("comb", [P, GT, E])
        combT = sb("combT", [E, GN])
        lns = [Norm(sb, sig, "ln")] if normed_in else []
        oln = Norm(sb, sig, "oln") if out_norm else None
        n_norms = len(lns) + (1 if oln else 0)
        chained = sig("chained", NORM_STEPS * n_norms + (16 if top == 2 else 5) + 1 + (2 if oln else 0))
        hold = sig("hold").sem
        fetched, normed, streamed = sig("fetched"), sig("normed"), sig("streamed")
        made = {s: sig("made_" + s) for s in steps}
        taken = {s: sig("taken_" + s, 1, 1) for s in steps}
        shifted, softened = sig("shifted"), sig("softened")
        combined = sig("combined")
        hid = sig("hid", E * FC)
        acted = sig("acted", E * FC, FC)
        y_done = sig("y_done", E, 2)
        added = sig("added", E, 2)
        block = ctx.enter_context(nc.Block())

        @block.sync
        def _(sp):
            if prefetch:
                prefetch(sp)

        @block.gpsimd
        def _(pool):
            if n_norms:
                with pool.Fori(0, TURNS) as i:
                    for ln in lns + ([oln] if oln else []):
                        ln.on_pool(pool, core, i)

        @block.scalar
        def _(act):
            for g in [taken[s] for s in steps if s in ("h", "comb")] + [acted]:
                act.sem_inc(g.sem, g.lead)
            with act.Fori(0, TURNS) as i:
                act.wait_ge(made["h"].sem, made["h"].at(i))
                if affine:
                    act.activation(hT[:], bank("h")[:], ACT.Identity, scale=affine[0],
                                   bias=affine[1]).then_inc(taken["h"].sem, 1)
                else:
                    act.activation(hT[:], bank("h")[:], ACT.Copy).then_inc(taken["h"].sem, 1)
                for e in range(E):
                    act.wait_ge(y_done.sem, y_done.at(i, e - 1))
                    for f in range(FC):
                        n = e * FC + f
                        act.wait_ge(hid.sem, hid.at(i, n + 1))
                        if b1 is not None:
                            ins = act.activation(hidden[:, e % 2, f, :], H[f][:], act_fn, bias=b1[:, n:n + 1])
                        else:
                            ins = act.activation(hidden[:, e % 2, f, :], H[f][:], act_fn)
                        ins.then_inc(acted.sem, 1)
                    if e == 0 and top == 2:
                        act.wait_ge(shifted.sem, shifted.at(i))
                        act.activation(pr[:], lg[:], ACT.Exp).then_inc(softened.sem, 1)
                    if e == 1 and top == 2:
                        act.wait_ge(made["comb"].sem, made["comb"].at(i))
                        act.activation(combT[:], bank("comb")[0:E, :], ACT.Copy).then_inc(taken["comb"].sem, 1)

        @block.vector
        def _(dve):
            for g in [taken[s] for s in steps if s in ("logit", "bias")] + [added]:
                dve.sem_inc(g.sem, g.lead)
            with dve.Fori(0, TURNS) as i:
                chain = Chain(dve, chained, i)

                def here(buf):
                    return lambda t: buf[:, t, :]

                def run(ins):
                    chain.step(ins)
                    chain.settle()

                def over(t):
                    return t[:, :, None].to_broadcast([P, GT, E])

                rank = core.rank[:, None, :].to_broadcast([P, GT, E])

                def choose(src, dst):
                    run(dve.tensor_reduce(out=top_v[:], in_=src, op=ALU.max, axis=AX.X))
                    run(dve.tensor_tensor(out=tmp[:], in0=src, in1=over(top_v[:]), op=ALU.is_ge))
                    run(dve.tensor_tensor(out=tmp[:], in0=tmp[:], in1=rank, op=ALU.mult))
                    run(dve.tensor_reduce(out=top_v[:], in_=tmp[:], op=ALU.max, axis=AX.X))
                    run(dve.tensor_tensor(out=dst, in0=rank, in1=over(top_v[:]), op=ALU.is_equal))

                dve.tensor_copy(raw[:], core.Y[:, bass.ds(i * GT, GT), :]).then_inc(fetched.sem, 1)
                dve.wait_ge(fetched.sem, fetched.at(i))
                if lns:
                    lns[0].on_vector(dve, chain, hold, i, here(raw), here(yn))
                    chain.settle()
                dve.sem_inc(normed.sem, 1)
                dve.wait_ge(made["logit"].sem, made["logit"].at(i))
                dve.tensor_tensor(out=lg[:], in0=bank("logit")[:, 0:GT * E].rearrange("p (t e) -> p t e", t=GT),
                                  in1=gate_b[:, None, :].to_broadcast([P, GT, E]), op=ALU.add)\
                    .then_inc(taken["logit"].sem, 1)
                dve.wait_ge(taken["logit"].sem, taken["logit"].at(i))
                if top == 1:
                    choose(lg[:], comb[:])
                else:
                    run(dve.tensor_reduce(out=top_v[:], in_=lg[:], op=ALU.max, axis=AX.X))
                    dve.tensor_tensor(out=lg[:], in0=lg[:], in1=over(top_v[:]), op=ALU.subtract)\
                        .then_inc(shifted.sem, 1)
                    dve.wait_ge(softened.sem, softened.at(i))
                    run(dve.reduce_sum(top_v[:], pr[:], axis=AX.X))
                    run(dve.reciprocal(top_v[:], top_v[:]))
                    run(dve.tensor_tensor(out=pr[:], in0=pr[:], in1=over(top_v[:]), op=ALU.mult))
                    choose(pr[:], pick[:, 0])
                    run(dve.scalar_tensor_tensor(out=lg[:], in0=pick[:, 0], scalar=-2.0, in1=pr[:], op0=ALU.mult,
                                                 op1=ALU.add))
                    choose(lg[:], pick[:, 1])
                    run(dve.tensor_tensor(out=tmp[:], in0=pick[:, 0], in1=pick[:, 1], op=ALU.add))
                    dve.tensor_tensor(out=comb[:], in0=tmp[:], in1=pr[:], op=ALU.mult).then_inc(combined.sem, 1)
                    dve.wait_ge(combined.sem, combined.at(i))
                    dve.wait_ge(made["bias"].sem, made["bias"].at(i))
                    dve.tensor_copy(acc[:], bank("bias")[:].rearrange("p (t d) -> p t d", t=GT))\
                        .then_inc(taken["bias"].sem, 1)
                    dve.wait_ge(taken["bias"].sem, taken["bias"].at(i))
                for e in range(E):
                    dve.wait_ge(y_done.sem, y_done.at(i, e + 1))
                    if e:
                        dve.wait_ge(added.sem, added.at(i, e))
                    for t in range(GT):
                        y = YB[e % 2][:, t * P:(t + 1) * P]
                        if e == 0 and top == 1:
                            ins = dve.tensor_scalar(acc[:, t, :], y, comb[:, t, 0:1], None, ALU.mult)
                        else:
                            ins = dve.scalar_tensor_tensor(out=acc[:, t, :], in0=y, scalar=comb[:, t, e:e + 1],
                                                           in1=acc[:, t, :], op0=ALU.mult, op1=ALU.add)
                    ins.then_inc(added.sem, 1)
                dve.wait_ge(added.sem, added.at(i, E))
                res = acc
                if oln:
                    dve.sem_inc(hold, 1)
                    oln.on_vector(dve, chain, hold, i, here(acc), here(fin))
                    chain.settle()
                    g, b = out_norm
                    run(dve.tensor_tensor(out=fin[:], in0=fin[:], in1=g[:, None, :].to_broadcast([P, GT, D]),
                                          op=ALU.mult))
                    run(dve.tensor_tensor(out=fin[:], in0=fin[:], in1=b[:, None, :].to_broadcast([P, GT, D]),
                                          op=ALU.add))
                    res = fin
                run(dve.tensor_tensor(out=fin[:], in0=res[:], in1=raw[:], op=ALU.add))
                Xt = core.X[:, bass.ds(i * GT, GT), :]
                dve.tensor_tensor(out=Xt, in0=fin[:], in1=Xt, op=ALU.add).then_inc(streamed.sem, 1)
                dve.wait_ge(streamed.sem, streamed.at(i))
                dve.sem_inc(hold, 1)
                chain.counted()

        @block.tensor
        def _(pe):
            pe.sem_inc(y_done.sem, y_done.lead)
            pe.wait_ge(w_loaded[0], w_loaded[1])
            with pe.Fori(0, TURNS) as i:
                def claim(s):
                    n = steps.index(s) - 2
                    pe.wait_ge(taken[steps[n]].sem, taken[steps[n]].at(i, 1 if n >= 0 else 0))

                pe.wait_ge(normed.sem, normed.at(i))
                claim("h")
                for t in range(GT):
                    ins = pe.transpose(bank("h")[:, t * P:(t + 1) * P], yn[:, t, :], core.ident[:])
                ins.then_inc(made["h"].sem, 1)
                pe.wait_ge(taken["h"].sem, taken["h"].at(i))
                claim("logit")
                for t in range(GT):
                    ins = pe.matmul(bank("logit")[:, t * E:(t + 1) * E], hT[:, t * P:(t + 1) * P], gate[:],
                                    start=True, stop=True)
                ins.then_inc(made["logit"].sem, 1)

                def hidden_layer(e):
                    for f in range(FC):
                        n = e * FC + f
                        pe.wait_ge(acted.sem, acted.at(i, n - FC + 1))
                        pe.matmul(H[f][:], core.W1[:, e, f * P:(f + 1) * P], hT[:], start=True, stop=True)\
                            .then_inc(hid.sem, 1)

                def output(e):
                    pe.wait_ge(acted.sem, acted.at(i, (e + 1) * FC))
                    pe.wait_ge(added.sem, added.at(i, e - 1))
                    for t in range(GT):
                        for f in range(FC):
                            ins = pe.matmul(YB[e % 2][:, t * P:(t + 1) * P], hidden[:, e % 2, f, t * P:(t + 1) * P],
                                            core.W2[:, e, f, :], start=f == 0, stop=f == FC - 1)
                    ins.then_inc(y_done.sem, 1)

                for e in range(E + 1):
                    if e < E:
                        hidden_layer(e)
                    if e >= 1:
                        output(e - 1)
                    if e == 1 and top == 2:
                        pe.wait_ge(combined.sem, combined.at(i))
                        claim("comb")
                        for t in range(GT):
                            ins = pe.transpose(bank("comb")[0:E, t * P:(t + 1) * P], comb[:, t, :], core.ident[:])
                        ins.then_inc(made["comb"].sem, 1)
                        pe.wait_ge(taken["comb"].sem, taken["comb"].at(i))
                        claim("bias")
                        for t in range(GT):
                            ins = pe.matmul(bank("bias")[:, t * P:(t + 1) * P], combT[:, t * P:(t + 1) * P], b2[:],
                                            start=True, stop=True)
                        ins.then_inc(made["bias"].sem, 1)


def state_space(nc, core, name, *, affine):
    N, CT = 16, 2
    WS = N * CT
    with ExitStack() as ctx:
        sb, ps, sig = allocator(nc, ctx, name)
        F = [ps("F0"), ps("F1"), ps("F2")]
        BB = [ps("B0"), ps("B1")]
        CB = ps("C")
        YS = [ps("Y0"), ps("Y1")]
        uses = ["h", "x0", "x1", "g0", "g1", "bc", "dt0", "dt1", "out"]
        assert len(uses) % len(F) == 0

        def bank(u):
            return F[uses.index(u) % len(F)]

        raw = sb("raw", [P, GT, D])
        yn = sb("yn", [P, GT, D])
        hn = raw
        hT = sb("hT", [P, GN])
        xpad = sb("xpad", [P, CT, 2, 3 + L])
        conv = sb("conv", [P, CT, 2, L])
        xc = sb("xc", [P, CT, GN])
        sg = sb("sg", [P, CT, GN])
        bc = sb("bc", [32, GN])
        left = sb("left", [32, 2, GN])
        bc3 = sb("bc3", [96, GN], BF16)
        sel = sb("sel", [96, 2 * N, P], BF16)
        ab = sb("ab", [P, CT, GN])
        lg = conv[:].rearrange("p c s q -> p c (s q)")
        dt = sb("dt", [P, CT, GN])
        du = sb("du", [P, CT, GN])
        A = sb("A", [P, CT, N])
        one = sb("one", [P, 1])
        dA = sb("dA", [P, 4, GN])
        bu = sb("bu", [P, 3, GN])
        hs = sb("hs", [P, 4, GN])
        Cs = sb("Cs", [P, 2, GN])
        hc = sb("hc", [P, 4, GN])
        yg = ab
        fin = sb("fin", [P, GT, D])
        lns = [Norm(sb, sig, "ln0"), Norm(sb, sig, "ln1")]
        chained = sig("chained", 2 * NORM_STEPS + 4 * CT + 4 + CT + 2 * CT)
        hold = sig("hold").sem
        fetched, normed, streamed = sig("fetched"), sig("normed"), sig("streamed")
        made = {u: sig("made_" + u) for u in uses}
        taken = {u: sig("taken_" + u, 1, 1) for u in uses}
        ready = sig("ready", 4)
        convolved = sig("convolved")
        activated = sig("activated")
        split = sig("split")
        magnitude = sig("magnitude", CT)
        log_made = sig("log_made")
        dt_made = sig("dt_made")
        dt_exp = sig("dt_exp")
        a_made = sig("a_made", 1)
        b_made = sig("b_made", N)
        c_made, c_taken = sig("c_made", N), sig("c_taken", N, 1)
        dA_made, scanned = sig("dA_made", WS), sig("scanned", WS, 4)
        bu_made = sig("bu_made", WS, 2 * CT)
        hc_made, summed = sig("hc_made", WS, 4), sig("summed", WS, 4)
        gated = sig("gated", 1, 1)
        block = ctx.enter_context(nc.Block())

        @block.gpsimd
        def _(pool):
            pool.sem_inc(hc_made.sem, hc_made.lead)
            pool.memset(xpad[:], 0.0).then_inc(ready.sem, 1)
            pool.memset(one[:], 1.0).then_inc(ready.sem, 1)
            pool.memset(sel[:], 0.0).then_inc(ready.sem, 1)
            pool.wait_ge(ready.sem, 3)
            for g in range(3):
                rows = sel[32 * g:32 * g + 32]
                pool.affine_select(out=rows, in_=rows, compare_op=ALU.not_equal, fill=1.0, base=0,
                                   pattern=[[-1, 2 * N], [0, P]], channel_multiplier=1).then_inc(ready.sem, 1)
            pool.wait_ge(ready.sem, 6)
            with pool.Fori(0, TURNS) as i:
                for ln in lns:
                    ln.on_pool(pool, core, i)
                for w_ in range(WS):
                    pool.wait_ge(scanned.sem, scanned.at(i, w_ + 1))
                    pool.wait_ge(c_taken.sem, c_taken.at(i, w_ // CT + 1))
                    pool.wait_ge(summed.sem, summed.at(i, w_ - 3))
                    pool.tensor_tensor(out=hc[:, w_ % 4, :], in0=hs[:, w_ % 4, :], in1=Cs[:, (w_ // CT) % 2, :],
                                       op=ALU.mult).then_inc(hc_made.sem, 1)

        @block.scalar
        def _(act):
            for g in (taken["h"], taken["x0"], taken["x1"], taken["g0"], taken["g1"], c_taken):
                act.sem_inc(g.sem, g.lead)
            act.activation(A[:], core.a_log[:], ACT.Exp).then_inc(a_made.sem, 1)
            act.wait_ge(ready.sem, 6)
            with act.Fori(0, TURNS) as i:
                act.wait_ge(made["h"].sem, made["h"].at(i))
                act.activation(hT[:], bank("h")[:], ACT.Identity, scale=affine[0], bias=affine[1])\
                    .then_inc(taken["h"].sem, 1)
                for c in range(CT):
                    act.wait_ge(made[f"x{c}"].sem, made[f"x{c}"].at(i))
                    act.activation(xpad[:, c, :, 3:3 + L], bank(f"x{c}")[:].rearrange("p (s q) -> p s q", s=2),
                                   ACT.Copy).then_inc(taken[f"x{c}"].sem, 1)
                act.wait_ge(gated.sem, gated.at(i, 0))
                for c in range(CT):
                    act.wait_ge(made[f"g{c}"].sem, made[f"g{c}"].at(i))
                    act.activation(sg[:, c, :], bank(f"g{c}")[:], ACT.Silu).then_inc(taken[f"g{c}"].sem, 1)
                act.wait_ge(convolved.sem, convolved.at(i))
                for c in range(CT):
                    ins = act.activation(xc[:, c, :], conv[:, c].rearrange("p s q -> p (s q)"), ACT.Silu,
                                         bias=core.conv_b[:, c:c + 1])
                ins.then_inc(activated.sem, 1)
                for c in range(CT):
                    act.wait_ge(made[f"dt{c}"].sem, made[f"dt{c}"].at(i))
                    act.activation(ab[:, c, :], bank(f"dt{c}")[:], ACT.Abs, bias=core.dt_b[:, c:c + 1])\
                        .then_inc(magnitude.sem, 1)
                act.wait_ge(magnitude.sem, magnitude.at(i, CT))
                act.activation(lg, ab[:], ACT.Exp, scale=-1.0).then_inc(dt_exp.sem, 1)
                act.wait_ge(dt_exp.sem, dt_exp.at(i))
                act.activation(ab[:], lg, ACT.Ln, bias=one[:, 0:1]).then_inc(log_made.sem, 1)
                act.wait_ge(dt_made.sem, dt_made.at(i))
                for w_ in range(WS):
                    n, c = w_ // CT, w_ % CT
                    act.wait_ge(scanned.sem, scanned.at(i, w_ - 3))
                    act.activation(dA[:, w_ % 4, :], dt[:, c, :], ACT.Exp, scale=A[:, c, n:n + 1])\
                        .then_inc(dA_made.sem, 1)
                    if c == 0:
                        act.wait_ge(c_made.sem, c_made.at(i, n + 1))
                        act.wait_ge(hc_made.sem, hc_made.at(i, 2 * n - 2))
                        act.activation(Cs[:, n % 2, :], CB[:], ACT.Copy).then_inc(c_taken.sem, 1)

        @block.vector
        def _(dve):
            for g in (taken["bc"], taken["dt0"], taken["dt1"], taken["out"], bu_made, scanned, gated):
                dve.sem_inc(g.sem, g.lead)
            dve.wait_ge(a_made.sem, 1)
            dve.tensor_scalar(A[:], A[:], -1.0, None, ALU.mult).then_inc(a_made.sem, 1)
            dve.wait_ge(a_made.sem, 2)
            with dve.Fori(0, TURNS) as i:
                chain = Chain(dve, chained, i)

                def here(buf):
                    return lambda t: buf[:, t, :]

                def run(ins):
                    chain.step(ins)
                    chain.settle()

                dve.tensor_copy(raw[:], core.X[:, bass.ds(i * GT, GT), :]).then_inc(fetched.sem, 1)
                dve.wait_ge(fetched.sem, fetched.at(i))
                lns[0].on_vector(dve, chain, hold, i, here(raw), here(yn))
                chain.settle()
                lns[1].on_vector(dve, chain, hold, i, here(yn), here(hn))
                chain.settle()
                dve.sem_inc(normed.sem, 1)
                for c in range(CT):
                    dve.wait_ge(taken[f"x{c}"].sem, taken[f"x{c}"].at(i))
                for k in range(4):
                    for c in range(CT):
                        tap = xpad[:, c, :, k:k + L]
                        wk = core.conv_w[:, c, k:k + 1]
                        if k == 0:
                            chain.step(dve.tensor_scalar(conv[:, c], tap, wk, None, ALU.mult))
                        else:
                            chain.step(dve.scalar_tensor_tensor(out=conv[:, c], in0=tap, scalar=wk, in1=conv[:, c],
                                                                op0=ALU.mult, op1=ALU.add))
                    chain.settle()
                dve.sem_inc(convolved.sem, 1)
                dve.wait_ge(made["bc"].sem, made["bc"].at(i))
                dve.tensor_copy(bc[:], bank("bc")[0:32, :]).then_inc(taken["bc"].sem, 1)
                dve.wait_ge(taken["bc"].sem, taken["bc"].at(i))
                run(dve.tensor_copy(bc3[0:32, :], bc[:]))
                run(dve.tensor_tensor(out=left[:, 0, :], in0=bc[:], in1=bc3[0:32, :], op=ALU.subtract))
                run(dve.tensor_copy(bc3[32:64, :], left[:, 0, :]))
                run(dve.tensor_copy(left[:, 1, :], bc3[32:64, :]))
                dve.tensor_tensor(out=bc3[64:96, :], in0=left[:, 0, :], in1=left[:, 1, :], op=ALU.subtract)\
                    .then_inc(split.sem, 1)
                for c in range(CT):
                    dve.wait_ge(magnitude.sem, magnitude.at(i, c + 1))
                    dve.tensor_scalar(dt[:, c, :], bank(f"dt{c}")[:], core.dt_b[:, c:c + 1], 0.0, ALU.add,
                                      ALU.max).then_inc(taken[f"dt{c}"].sem, 1)
                    dve.wait_ge(taken[f"dt{c}"].sem, taken[f"dt{c}"].at(i))
                dve.wait_ge(log_made.sem, log_made.at(i))
                dve.tensor_tensor(out=dt[:], in0=dt[:], in1=ab[:], op=ALU.add).then_inc(dt_made.sem, 1)
                dve.wait_ge(dt_made.sem, dt_made.at(i))
                for c in range(CT):
                    chain.step(dve.tensor_tensor(out=du[:, c, :], in0=dt[:, c, :], in1=xc[:, c, :], op=ALU.mult))
                chain.settle()

                def inflow(w_):
                    n, c = w_ // CT, w_ % CT
                    if c == 0:
                        dve.wait_ge(b_made.sem, b_made.at(i, n + 1))
                    dve.wait_ge(scanned.sem, scanned.at(i, w_ - 2))
                    dve.tensor_tensor(out=bu[:, w_ % 3, :], in0=du[:, c, :], in1=BB[n % 2][:], op=ALU.mult)\
                        .then_inc(bu_made.sem, 1)

                inflow(0)
                for w_ in range(WS):
                    if w_ + 1 < WS:
                        inflow(w_ + 1)
                    dve.wait_ge(bu_made.sem, bu_made.at(i, w_ + 1))
                    dve.wait_ge(dA_made.sem, dA_made.at(i, w_ + 1))
                    dve.wait_ge(hc_made.sem, hc_made.at(i, w_ - 3))
                    for s in range(2):
                        q = slice(s * L, (s + 1) * L)
                        ins = dve.tensor_tensor_scan(hs[:, w_ % 4, q], dA[:, w_ % 4, q], bu[:, w_ % 3, q], 0.0,
                                                     ALU.mult, ALU.add)
                    ins.then_inc(scanned.sem, 1)
                dve.wait_ge(summed.sem, summed.at(i, WS))
                for c in range(CT):
                    chain.step(dve.scalar_tensor_tensor(out=yg[:, c, :], in0=xc[:, c, :], scalar=core.d_skip[:, c:c + 1],
                                                        in1=YS[c][:], op0=ALU.mult, op1=ALU.add))
                chain.settle()
                for c in range(CT):
                    chain.step(dve.tensor_tensor(out=yg[:, c, :], in0=yg[:, c, :], in1=sg[:, c, :], op=ALU.mult))
                chain.settle()
                dve.sem_inc(gated.sem, 1)
                dve.wait_ge(made["out"].sem, made["out"].at(i))
                dve.tensor_tensor(out=fin[:], in0=bank("out")[:].rearrange("p (t d) -> p t d", t=GT), in1=yn[:],
                                  op=ALU.add).then_inc(taken["out"].sem, 1)
                dve.wait_ge(taken["out"].sem, taken["out"].at(i))
                dve.sem_inc(hold, 1)
                dve.tensor_copy(core.Y[:, bass.ds(i * GT, GT), :], fin[:]).then_inc(streamed.sem, 1)
                dve.wait_ge(streamed.sem, streamed.at(i))
                dve.sem_inc(hold, 1)
                chain.counted()

        @block.tensor
        def _(pe):
            pe.sem_inc(summed.sem, summed.lead)
            pe.wait_ge(ready.sem, 6)
            with pe.Fori(0, TURNS) as i:
                def claim(u):
                    n = uses.index(u) - len(F)
                    pe.wait_ge(taken[uses[n]].sem, taken[uses[n]].at(i, 1 if n >= 0 else 0))

                pe.wait_ge(normed.sem, normed.at(i))
                claim("h")
                for t in range(GT):
                    ins = pe.transpose(bank("h")[:, t * P:(t + 1) * P], hn[:, t, :], core.ident[:])
                ins.then_inc(made["h"].sem, 1)
                pe.wait_ge(taken["h"].sem, taken["h"].at(i))
                for n, u in enumerate(("x0", "x1", "g0", "g1")):
                    claim(u)
                    pe.matmul(bank(u)[:], core.in_w[:, n * P:(n + 1) * P], hT[:], start=True, stop=True)\
                        .then_inc(made[u].sem, 1)
                pe.wait_ge(activated.sem, activated.at(i))
                claim("bc")
                for c in range(CT):
                    ins = pe.matmul(bank("bc")[0:32, :], core.x_w[:, c, :], xc[:, c, :], start=c == 0, stop=c == 1)
                ins.then_inc(made["bc"].sem, 1)
                pe.wait_ge(taken["bc"].sem, taken["bc"].at(i))
                for c in range(CT):
                    claim(f"dt{c}")
                    pe.matmul(bank(f"dt{c}")[:], core.dt_w[:, c * P:(c + 1) * P], bc[0:N, :], start=True, stop=True)\
                        .then_inc(made[f"dt{c}"].sem, 1)
                pe.wait_ge(split.sem, split.at(i))
                for n in range(N + 2):
                    if n < N:
                        pe.wait_ge(bu_made.sem, bu_made.at(i, CT * (n - 1)))
                        pe.matmul(BB[n % 2][:], sel[:, n, :], bc3[:], start=True, stop=True).then_inc(b_made.sem, 1)
                        pe.wait_ge(c_taken.sem, c_taken.at(i, n))
                        pe.matmul(CB[:], sel[:, N + n, :], bc3[:], start=True, stop=True).then_inc(c_made.sem, 1)
                    if n >= 2:
                        for c in range(CT):
                            w_ = (n - 2) * CT + c
                            pe.wait_ge(hc_made.sem, hc_made.at(i, w_ + 1))
                            if n == 2:
                                pe.wait_ge(gated.sem, gated.at(i, 0))
                            pe.matmul(YS[c][:], core.ident[:], hc[:, w_ % 4, :], start=n == 2, stop=n == N + 1)\
                                .then_inc(summed.sem, 1)
                pe.wait_ge(gated.sem, gated.at(i))
                claim("out")
                for t in range(GT):
                    for c in range(CT):
                        ins = pe.matmul(bank("out")[:, t * P:(t + 1) * P], yg[:, c, t * P:(t + 1) * P],
                                        core.out_w[:, c, :], start=c == 0, stop=c == 1)
                ins.then_inc(made["out"].sem, 1)


def gated_dense(nc, core, name, *, affine):
    FC = 4
    with ExitStack() as ctx:
        sb, ps, sig = allocator(nc, ctx, name)
        TP, OUT = ps("TP"), ps("OUT")
        H1, H3 = [ps("H10"), ps("H11")], [ps("H30"), ps("H31")]
        raw = sb("raw", [P, GT, D])
        yn = sb("yn", [P, GT, D])
        hT = sb("hT", [P, GN])
        act1 = sb("act1", [P, 2, GN])
        prod = sb("prod", [P, FC, GN])
        fin = sb("fin", [P, GT, D])
        ln = Norm(sb, sig, "ln")
        chained = sig("chained", NORM_STEPS)
        hold = sig("hold").sem
        fetched, normed, streamed = sig("fetched"), sig("normed"), sig("streamed")
        h_made, h_taken = sig("h_made"), sig("h_taken", 1, 1)
        first_made, second_made = sig("first_made", FC), sig("second_made", FC)
        first_taken = sig("first_taken", FC, 2)
        multiplied = sig("multiplied", FC, 2)
        out_made, out_taken = sig("out_made"), sig("out_taken", 1, 1)
        block = ctx.enter_context(nc.Block())

        @block.gpsimd
        def _(pool):
            with pool.Fori(0, TURNS) as i:
                ln.on_pool(pool, core, i)

        @block.scalar
        def _(act):
            for g in (h_taken, first_taken):
                act.sem_inc(g.sem, g.lead)
            with act.Fori(0, TURNS) as i:
                act.wait_ge(h_made.sem, h_made.at(i))
                act.activation(hT[:], TP[:], ACT.Identity, scale=affine[0], bias=affine[1]).then_inc(h_taken.sem, 1)
                for f in range(FC):
                    act.wait_ge(first_made.sem, first_made.at(i, f + 1))
                    act.wait_ge(multiplied.sem, multiplied.at(i, f - 1))
                    act.activation(act1[:, f % 2, :], H1[f % 2][:], ACT.Silu).then_inc(first_taken.sem, 1)

        @block.vector
        def _(dve):
            for g in (multiplied, out_taken):
                dve.sem_inc(g.sem, g.lead)
            with dve.Fori(0, TURNS) as i:
                chain = Chain(dve, chained, i)

                def here(buf):
                    return lambda t: buf[:, t, :]

                dve.tensor_copy(raw[:], core.Y[:, bass.ds(i * GT, GT), :]).then_inc(fetched.sem, 1)
                dve.wait_ge(fetched.sem, fetched.at(i))
                ln.on_vector(dve, chain, hold, i, here(raw), here(yn))
                chain.settle()
                dve.sem_inc(normed.sem, 1)
                for f in range(FC):
                    dve.wait_ge(second_made.sem, second_made.at(i, f + 1))
                    dve.wait_ge(first_taken.sem, first_taken.at(i, f + 1))
                    dve.tensor_tensor(out=prod[:, f, :], in0=act1[:, f % 2, :], in1=H3[f % 2][:], op=ALU.mult)\
                        .then_inc(multiplied.sem, 1)
                dve.wait_ge(out_made.sem, out_made.at(i))
                dve.tensor_tensor(out=fin[:], in0=OUT[:].rearrange("p (t d) -> p t d", t=GT), in1=raw[:],
                                  op=ALU.add).then_inc(out_taken.sem, 1)
                dve.wait_ge(out_taken.sem, out_taken.at(i))
                Xt = core.X[:, bass.ds(i * GT, GT), :]
                dve.tensor_tensor(out=Xt, in0=fin[:], in1=Xt, op=ALU.add).then_inc(streamed.sem, 1)
                dve.wait_ge(streamed.sem, streamed.at(i))
                dve.sem_inc(hold, 1)
                chain.counted()

        @block.tensor
        def _(pe):
            with pe.Fori(0, TURNS) as i:
                pe.wait_ge(normed.sem, normed.at(i))
                pe.wait_ge(h_taken.sem, h_taken.at(i, 0))
                for t in range(GT):
                    ins = pe.transpose(TP[:, t * P:(t + 1) * P], yn[:, t, :], core.ident[:])
                ins.then_inc(h_made.sem, 1)
                pe.wait_ge(h_taken.sem, h_taken.at(i))
                for f in range(FC):
                    cols = slice(f * P, (f + 1) * P)
                    pe.wait_ge(first_taken.sem, first_taken.at(i, f - 1))
                    pe.matmul(H1[f % 2][:], core.w1[:, cols], hT[:], start=True, stop=True)\
                        .then_inc(first_made.sem, 1)
                    pe.wait_ge(multiplied.sem, multiplied.at(i, f - 1))
                    pe.matmul(H3[f % 2][:], core.w3[:, cols], hT[:], start=True, stop=True)\
                        .then_inc(second_made.sem, 1)
                pe.wait_ge(multiplied.sem, multiplied.at(i, FC))
                pe.wait_ge(out_taken.sem, out_taken.at(i, 0))
                for t in range(GT):
                    for f in range(FC):
                        ins = pe.matmul(OUT[:, t * P:(t + 1) * P], prod[:, f, t * P:(t + 1) * P], core.w2[:, f, :],
                                        start=f == 0, stop=f == FC - 1)
                ins.then_inc(out_made.sem, 1)


COLS = ("L0_ffn_ln1_w L0_ffn_ln1_b L0_ffn_ln2_w L0_ffn_ln2_b "
        "L1_attn_a_bq bq_r L1_attn_a_bk bk_r "
        "L1_attn_b_ln1_g L1_attn_b_ln1_b L1_attn_b_ln2_g L1_attn_b_ln2_b L1_attn_b_ln3_g L1_attn_b_ln3_b "
        "L1_ffn_bq L1_ffn_bk").split()
ROWS = ("L1_attn_a_bv L1_attn_a_bo L1_ffn_bv L1_ffn_bo L1_ffn_ln1_g L1_ffn_ln1_b L1_ffn_ln2_g L1_ffn_ln2_b "
        "L0_attn_b_b_out").split()
SQUARE = ("a_q a_qr a_k a_kr a_v a_o f_q f_k f_v f_o b_q b_qr b_k b_kr b_v b_o "
          "l_q l_k l_v l_o").split()


def load(nc, core, ctx, a):
    sb, ps, sig = allocator(nc, ctx, "core_")
    core.X = sb("X", [P, TILES, D])
    core.Y = sb("Y", [P, TILES, D])
    core.ident = sb("ident", [P, P])
    core.ident16 = sb("ident16", [P, P], BF16)
    core.causal16 = sb("causal16", [P, P], BF16)
    core.head_mask = sb("head_mask", [P, 4])
    core.minus_half = sb("minus_half", [P, GT])
    core.cols = sb("cols", [P, len(COLS)])
    core.rows = sb("rows", [P, len(ROWS), D])
    core.square = sb("square", [P, len(SQUARE), D])
    core.small_rope = sb("small_rope", [P, 4, L])
    core.scale = sb("scale", [P, 1])
    core.rank = sb("rank", [P, 8])
    core.distance = sb("distance", [P, 3 * P])
    core.wide_rope = sb("wide_rope", [P, 4, L])
    core.gates = sb("gates", [P, 2, 8])
    core.gate_b = sb("gate_b", [P, 2, 8])
    core.b1 = sb("b1", [P, 32])
    core.b2 = sb("b2", [8, D])
    core.bqk = sb("bqk", [P, 2, 8])
    core.bvb = sb("bvb", [P, 1024])
    core.W1 = sb("W1", [P, 8, 512])
    core.W2 = sb("W2", [P, 8, 4, D])
    core.AW = {x: sb("AW_" + x, [P, 1024]) for x in "qkvo"}
    core.in_w = sb("in_w", [P, 512])
    core.out_w = sb("out_w", [P, 2, D])
    core.x_w = sb("x_w", [P, 2, 32])
    core.dt_w = sb("dt_w", [16, 256])
    core.conv_w = sb("conv_w", [P, 2, 4])
    core.conv_b = sb("conv_b", [P, 2])
    core.dt_b = sb("dt_b", [P, 2])
    core.d_skip = sb("d_skip", [P, 2])
    core.a_log = sb("a_log", [P, 2, 16])
    core.w1 = sb("w1", [P, 512])
    core.w3 = sb("w3", [P, 512])
    core.w2 = sb("w2", [P, 4, D])
    core.aw_loaded = sig("aw_loaded", 0)
    core.moe_loaded = sig("moe_loaded", 0)
    core.loaded = sig("loaded", 0)
    built = sig("built", 0)
    with nc.Block() as block:
        @block.sync
        def _(sp):
            n = 0
            for dst, src in (
                    (core.X[:], a["x"].rearrange("(t p) d -> p t d", p=P)),
                    (core.cols[:], a["cols"]), (core.square[:], a["square"]),
                    (core.rows[:], a["rows"].rearrange("(o r) d -> o r d", o=1).to_broadcast([P, len(ROWS), D])),
                    (core.small_rope[:], a["small_rope"]), (core.rank[:], a["rank"]),
                    (core.distance[:], a["distance"]), (core.wide_rope[:], a["wide_rope"]),
                    (core.gates[:], a["gates"]), (core.b1[:], a["b1"]), (core.b2[:], a["b2"]),
                    (core.gate_b[:], a["gate_b"].rearrange("(o r) d -> o r d", o=1).to_broadcast([P, 2, 8])),
                    (core.bqk[:], a["bqk"]), (core.in_w[:], a["in_w"]),
                    (core.out_w[:], a["out_w"].rearrange("(c p) d -> p c d", p=P)),
                    (core.x_w[:], a["x_w"].rearrange("(c p) d -> p c d", p=P)), (core.dt_w[:], a["dt_w"]),
                    (core.conv_w[:], a["conv_w"].rearrange("(c p) k -> p c k", p=P)),
                    (core.conv_b[:], a["channel"][:, 0:2]), (core.dt_b[:], a["channel"][:, 2:4]),
                    (core.d_skip[:], a["channel"][:, 4:6]),
                    (core.a_log[:], a["a_log"].rearrange("(c p) k -> p c k", p=P)),
                    (core.w1[:], a["w1"]), (core.w3[:], a["w3"]),
                    (core.w2[:], a["w2"].rearrange("(c p) d -> p c d", p=P)),
                    (core.bvb[:], a["bvb"].rearrange("(o r) -> o r", o=1).to_broadcast([P, 1024])),
                    (core.scale[:], a["scale"].rearrange("(o n) -> o n", o=1).to_broadcast([P, 1]))):
                sp.dma_start(dst, src).then_inc(core.loaded.sem, 16)
                n += 16
            core.loads = n
            load_attention(sp, core, a, "a")
            load_experts(sp, core, a, "l0")
            sp.wait_ge(core.loaded.sem, n)

        @block.gpsimd
        def _(pool):
            pool.memset(core.ident[:], 0.0).then_inc(built.sem, 1)
            pool.memset(core.causal16[:], 0.0).then_inc(built.sem, 1)
            pool.memset(core.head_mask[:], 1.0).then_inc(built.sem, 1)
            pool.memset(core.minus_half[:], -0.5).then_inc(built.sem, 1)
            pool.wait_ge(built.sem, 4)
            pool.affine_select(out=core.ident[:], in_=core.ident[:], compare_op=ALU.not_equal, fill=1.0,
                               base=0, pattern=[[-1, P]], channel_multiplier=1).then_inc(built.sem, 1)
            pool.affine_select(out=core.causal16[:], in_=core.causal16[:], compare_op=ALU.is_ge, fill=MASKED,
                               base=0, pattern=[[-1, P]], channel_multiplier=1).then_inc(built.sem, 1)
            for g in range(4):
                rows = core.head_mask[32 * g:32 * g + 32, :]
                pool.affine_select(out=rows, in_=rows, compare_op=ALU.is_ge, fill=0.0,
                                   base=0, pattern=[[-8, 4]], channel_multiplier=1).then_inc(built.sem, 1)
                pool.wait_ge(built.sem, 7 + 2 * g)
                pool.affine_select(out=rows, in_=rows, compare_op=ALU.is_ge, fill=0.0,
                                   base=7, pattern=[[8, 4]], channel_multiplier=-1).then_inc(built.sem, 1)
            pool.wait_ge(built.sem, 14)
            pool.tensor_copy(core.ident16[:], core.ident[:]).then_inc(built.sem, 1)
            pool.wait_ge(built.sem, 15)


def load_attention(sp, core, a, which):
    for x in "qkvo":
        sp.dma_start(core.AW[x][:], a[f"aw_{which}_{x}"]).then_inc(core.aw_loaded.sem, 16)


def load_experts(sp, core, a, which):
    sp.dma_start(core.W1[:], a[which + "_W1"].rearrange("e d f -> d e f")).then_inc(core.moe_loaded.sem, 16)
    sp.dma_start(core.W2[:], a[which + "_W2"].rearrange("e (c f) d -> f e c d", f=P))\
        .then_inc(core.moe_loaded.sem, 16)


def store(nc, core, ctx, out):
    with nc.Block() as block:
        @block.sync
        def _(sp):
            base = core.loads
            sp.dma_start(out.rearrange("(t p) d -> p t d", p=P), core.X[:]).then_inc(core.loaded.sem, 16)
            sp.wait_ge(core.loaded.sem, base + 16)


def network(nc, a, out):
    core = Core()
    with ExitStack() as ctx:
        load(nc, core, ctx, a)

        def col(name):
            k = COLS.index(name)
            return core.cols[:, k:k + 1]

        def row(name):
            return core.rows[:, ROWS.index(name), :]

        def sq(prefix, parts):
            return {x: core.square[:, SQUARE.index(prefix + "_" + x), :] for x in parts}

        r = core.small_rope

        def l0_ffn_attention(n, prefetch=None):
            small_attention(nc, core, f"l0att{n}_", src="X", norms=2,
                            affine=(col("L0_ffn_ln1_w"), col("L0_ffn_ln1_b")), w=sq("l", "qkvo"),
                            q_scale=8 ** -0.5, finish="y_plus", prefetch=prefetch)

        aw = {x: core.AW[x] for x in "qkv"}
        aw["o"] = core.AW["o"][:].rearrange("p (m d) -> p m d", m=8)
        wr = core.wide_rope

        def l0_attention_a():
            wide_attention(nc, core, "wa_", heads_per_step=1, w=aw, w_loaded=(core.aw_loaded.sem, 64),
                           rope=((wr[:, 0], wr[:, 1]), (wr[:, 2], wr[:, 3])))

        def l0_attention_b():
            wide_attention(nc, core, "wb_", heads_per_step=2, w=aw, w_loaded=(core.aw_loaded.sem, 128),
                           bq=core.bqk[:, 0, :], bk=core.bqk[:, 1, :], bv=core.bvb, q_scale=64 ** -0.5,
                           slopes=[float(v) for v in 2.0 ** -np.linspace(1.0, 8.0, 16)], bo=row("L0_attn_b_b_out"))

        def l0_experts(n, prefetch=None):
            experts(nc, core, f"e0{n}_", affine=(col("L0_ffn_ln2_w"), col("L0_ffn_ln2_b")), normed_in=True,
                    w_loaded=(core.moe_loaded.sem, 32), gate=core.gates[:, 0, :], gate_b=core.gate_b[:, 0, :],
                    act_fn=ACT.Gelu_apprx_tanh, top=1, prefetch=prefetch)

        def l1_experts(n):
            experts(nc, core, f"e1{n}_", affine=None, normed_in=False, w_loaded=(core.moe_loaded.sem, 64),
                    gate=core.gates[:, 1, :], gate_b=core.gate_b[:, 1, :], act_fn=ACT.Gelu, top=2,
                    b1=core.b1, b2=core.b2, out_norm=(row("L1_ffn_ln2_g"), row("L1_ffn_ln2_b")))

        def l1_attention(n, prefetch=None):
            w = sq("a", ("q", "qr", "k", "kr", "v", "o"))
            w["bo"] = row("L1_attn_a_bo")
            small_attention(nc, core, f"l1att{n}_", src="X", norms=1, affine=None, w=w, q_scale=core.scale[:, 0:1],
                            bq=(col("L1_attn_a_bq"), col("bq_r")), bk=(col("L1_attn_a_bk"), col("bk_r")),
                            bv=row("L1_attn_a_bv"), rope=(r[:, 0], r[:, 1]), causal=True, finish="X_plus",
                            prefetch=prefetch)

        def l1_ffn_attention(n):
            w = sq("f", "qkvo")
            w["bo"] = row("L1_ffn_bo")
            small_attention(nc, core, f"l1ffn{n}_", src="X", norms=1, affine=None, w=w, q_scale=8 ** -0.5,
                            bq=col("L1_ffn_bq"), bk=col("L1_ffn_bk"), bv=row("L1_ffn_bv"), finish="y_norm",
                            out_norm=(row("L1_ffn_ln1_g"), row("L1_ffn_ln1_b")))

        def grouped_attention():
            small_attention(nc, core, "gqa_", src="Y", norms=1,
                            affine=(col("L1_attn_b_ln2_g"), col("L1_attn_b_ln2_b")),
                            w=sq("b", ("q", "qr", "k", "kr", "v", "o")), q_scale=8 ** -0.5,
                            rope=(r[:, 2], r[:, 3]), causal=True, finish="Y_plus")

        def l1_mamba():
            state_space(nc, core, "ssm_", affine=(col("L1_attn_b_ln1_g"), col("L1_attn_b_ln1_b")))

        def l1_dense():
            gated_dense(nc, core, "swi_", affine=(col("L1_attn_b_ln3_g"), col("L1_attn_b_ln3_b")))

        l0_attention_a()
        l0_ffn_attention(0, prefetch=lambda sp: load_attention(sp, core, a, "b"))
        l0_experts(0)
        l0_attention_b()
        l0_ffn_attention(1)
        l0_experts(1)
        l1_attention(0, prefetch=lambda sp: load_experts(sp, core, a, "l1"))
        l1_ffn_attention(0)
        l1_experts(0)
        l1_mamba()
        grouped_attention()
        l1_dense()
        l1_ffn_attention(1)
        l1_experts(1)
        store(nc, core, ctx, out)


def _program_inputs(inputs):
    g = {k: np.ascontiguousarray(np.asarray(v)) for k, v in inputs.items()}
    heads = np.arange(D).reshape(16, 8)
    swap = np.arange(D).reshape(-1, 2)[:, ::-1].reshape(-1)
    turn = np.concatenate([heads[:, 4:], heads[:, :4]], 1).reshape(-1)
    kv = ((np.arange(16) // 4)[:, None] * 8 + np.arange(8)).reshape(-1)
    g["bq_r"], g["bk_r"] = g["L1_attn_a_bq"][swap], g["L1_attn_a_bk"][swap]
    a = {"x": g["L0_attn_a_x"].reshape(TILES * P, D)}
    a["cols"] = np.stack([g[c] for c in COLS], 1)
    a["rows"] = np.stack([g[c] for c in ROWS], 0)
    wq, wk = g["L1_attn_a_Wq"].T, g["L1_attn_a_Wk"].T
    bk = g["L1_attn_b_k_w"][:, kv]
    qkv = g["L0_ffn_w_qkv"]
    sq = {"a_q": wq, "a_qr": wq[:, swap], "a_k": wk, "a_kr": wk[:, swap], "a_v": g["L1_attn_a_Wv"].T,
          "a_o": g["L1_attn_a_Wo"].T,
          "f_q": g["L1_ffn_Wq"], "f_k": g["L1_ffn_Wk"], "f_v": g["L1_ffn_Wv"], "f_o": g["L1_ffn_Wo"],
          "b_q": g["L1_attn_b_q_w"], "b_qr": g["L1_attn_b_q_w"][:, turn], "b_k": bk, "b_kr": bk[:, turn],
          "b_v": g["L1_attn_b_v_w"][:, kv], "b_o": g["L1_attn_b_o_w"],
          "l_q": qkv[:, 0:D], "l_k": qkv[:, D:2 * D], "l_v": qkv[:, 2 * D:], "l_o": g["L0_ffn_w_proj"]}
    a["square"] = np.stack([sq[s] for s in SQUARE], 1)
    a["scale"] = g["L1_attn_a_scale"]
    pos = np.arange(L, dtype=np.float32)
    ta = (np.float32(10000.0) ** (-np.arange(0, 8, 2, dtype=np.float32) / 8)).astype(np.float32)
    ang = (pos[:, None] * ta).astype(np.float32)
    ia = (np.arange(D) % 8) // 2
    sign_a = np.where(np.arange(D) % 2 == 0, -1, 1).astype(np.float32)[:, None]
    tb = (np.float32(1.0) / np.float32(10000.0) ** (np.arange(0, 8, 2, dtype=np.float32) / 8)).astype(np.float32)
    angb = (pos[:, None] * tb).astype(np.float32)
    ib = np.arange(D) % 4
    sign_b = np.where(np.arange(D) % 8 < 4, -1, 1).astype(np.float32)[:, None]
    a["small_rope"] = np.stack([np.cos(ang).T[ia], np.sin(ang).T[ia] * sign_a,
                                np.cos(angb).T[ib], np.sin(angb).T[ib] * sign_b], 1).astype(np.float32)
    fr = np.power(np.float32(10000.0), -np.arange(64, dtype=np.float32) / np.float32(64)).astype(np.float32)
    angw = (pos[:, None] * fr[None, :]).astype(np.float32)
    cos = np.concatenate([np.cos(angw).T] * 2, 0).astype(np.float32)
    sin = np.concatenate([np.sin(angw).T, -np.sin(angw).T], 0).astype(np.float32)
    unit = np.float32(1 / 128)
    a["wide_rope"] = np.stack([cos * unit, sin * unit, cos, sin], 1)
    a["aw_a_q"], a["aw_a_k"], a["aw_a_v"] = (g["L0_attn_a_w_a" + x].reshape(D, 1024) for x in "qkv")
    a["aw_a_o"] = g["L0_attn_a_w_ao"].transpose(1, 0, 2).reshape(D, 1024)
    three = g["L0_attn_b_W_qkv"].reshape(D, 16, 3, 64)
    for n, x in enumerate("qkv"):
        a["aw_b_" + x] = three[:, :, n].reshape(D, 1024)
    a["aw_b_o"] = g["L0_attn_b_W_out"].reshape(8, P, D).transpose(1, 0, 2).reshape(P, 1024)
    bqkv = g["L0_attn_b_b_qkv"].reshape(16, 3, 64)
    a["bqk"] = np.stack([bqkv[:, n].reshape(8, P).T for n in range(2)], 1)
    a["bvb"] = bqkv[:, 2].reshape(1024)
    q, k = np.arange(P)[:, None], np.arange(L)[None, :]
    tiles = [np.where(k <= q, k - q, MASKED)[:, :P], np.where(k <= q + P, k - q - P, MASKED)]
    a["distance"] = np.concatenate(tiles, 1).astype(np.float32)
    a["rank"] = np.broadcast_to(8.0 - np.arange(8), (P, 8)).astype(np.float32)
    a["gates"] = np.stack([g["L0_ffn_gate_w"], g["L1_ffn_gate_w"]], 1)
    a["gate_b"] = np.stack([g["L0_ffn_gate_b"], g["L1_ffn_gate_b"]], 0)
    a["b1"] = g["L1_ffn_b1"].reshape(32, P).T
    a["b2"] = g["L1_ffn_b2"]
    b = {k[len("L1_attn_b_"):]: v for k, v in g.items() if k.startswith("L1_attn_b_")}
    a["in_w"], a["out_w"], a["x_w"], a["dt_w"] = b["in_proj_w"], b["out_proj_w"], b["x_proj_w"], b["dt_proj_w"]
    a["conv_w"], a["a_log"] = b["conv_w"][:, 0], b["A_log"]
    a["w1"], a["w2"], a["w3"] = b["w1"], b["w2"], b["w3"]
    a["channel"] = np.concatenate([b[x].reshape(2, P).T for x in ("conv_b", "dt_proj_b", "D_skip")], 1)
    a["l0_W1"], a["l0_W2"], a["l1_W1"], a["l1_W2"] = g["L0_ffn_w1"], g["L0_ffn_w2"], g["L1_ffn_W1"], g["L1_ffn_W2"]
    return {k: np.ascontiguousarray(v) for k, v in a.items()}


def kernel(**inputs):
    import concourse.bacc as bacc
    from concourse.bass_utils import run_bass_kernel_spmd as run

    nc = bacc.Bacc("TRN2", target_bir_lowering=False, num_devices=1)
    arrays = {f"in_{k}_dram": v for k, v in _program_inputs(inputs).items()}
    aps = {k[3:-5]: nc.dram_tensor(k, v.shape, mybir.dt.from_np(v.dtype), kind="ExternalInput").ap()
           for k, v in arrays.items()}
    out = nc.dram_tensor("out_dram", (TILES * P, D), F32, kind="ExternalOutput").ap()
    network(nc, aps, out)
    r = run(nc, [arrays], core_ids=[0])
    return r.results[0]["out_dram"].reshape(SEQS, L, D)
```

```python
from contextlib import ExitStack

import concourse.bass as bass
from concourse import mybir
import numpy as np

F32 = mybir.dt.float32
BF16 = mybir.dt.bfloat16
F32R = mybir.dt.float32r
ALU = mybir.AluOpType
ACT = mybir.ActivationFunctionType
AX = mybir.AxisListType

P = 128
SEQS, L, D = 16, 256, 128
TILES = SEQS * L // P
QT = L // P
TURNS = SEQS // 2
GT = 2 * QT
GN = GT * P
EPS = 1e-5
MASKED = -1e30


class Signal:

    def __init__(self, sem, per=1, lead=0):
        self.sem = sem
        self.per, self.lead = per, lead

    def at(self, i, k=1):
        return i * self.per + (k + self.lead)


class Chain:

    def __init__(self, eng, own, i):
        self.eng, self.own, self.i, self.n = eng, own, i, 0

    def step(self, ins):
        ins.then_inc(self.own.sem, 1)
        self.n += 1

    def settle(self):
        self.eng.wait_ge(self.own.sem, self.own.at(self.i, self.n))

    def counted(self):
        assert self.n == self.own.per, (self.n, self.own.per)


class Core:
    pass


def allocator(nc, ctx, prefix):
    held = []

    def clear():
        nc.clear_and_free_semaphores(held)
        nc.all_engine_barrier()

    ctx.callback(clear)

    def sb(name, shape, dt=F32):
        return ctx.enter_context(nc.sbuf_tensor(prefix + name, shape, dt))

    def ps(name, shape=(P, 512), dt=F32):
        return ctx.enter_context(nc.psum_tensor(prefix + name, list(shape), dt))

    def sig(name, per=1, lead=0):
        sem = nc.alloc_semaphore(prefix + name)
        held.append(sem)
        return Signal(sem, per, lead)

    return sb, ps, sig


def per_feature(t, k=0):
    return t[:, k:k + 1]


class Norm:
    def __init__(self, sb, sig, name, tiles=GT, per=1):
        self.tiles = tiles
        self.stats = sb(name + "_stats", [P, tiles, 6])
        self.mv = sb(name + "_mv", [P, tiles, 2])
        self.ve = sb(name + "_ve", [P, tiles])
        self.rstd = sb(name + "_rstd", [P, tiles])
        self.var_ready = sig(name + "_var_ready", per)
        self.rstd_ready = sig(name + "_rstd_ready", per)

    def statistics(self, dve, chain, hold, src):
        for t in range(self.tiles):
            chain.step(dve.bn_stats(self.stats[:, t, :], src(t)))
        chain.settle()
        dve.sem_inc(hold, 1)
        for t in range(self.tiles):
            chain.step(dve.bn_aggr(self.mv[:, t, :], self.stats[:, t, :]))
        chain.settle()
        dve.tensor_scalar(self.ve[:], self.mv[:, :, 1], EPS, None, ALU.add).then_inc(self.var_ready.sem, 1)

    def apply(self, dve, chain, i, s, src, dst):
        dve.wait_ge(self.rstd_ready.sem, self.rstd_ready.at(i, s + 1))
        for t in range(self.tiles):
            chain.step(dve.tensor_scalar(dst(t), src(t), self.mv[:, t, 0:1], self.rstd[:, t:t + 1],
                                         ALU.subtract, ALU.mult))

    def on_vector(self, dve, chain, hold, i, src, dst):
        self.statistics(dve, chain, hold, src)
        self.apply(dve, chain, i, 0, src, dst)

    def on_pool(self, pool, core, i, s=0):
        pool.wait_ge(self.var_ready.sem, self.var_ready.at(i, s + 1))
        pool.tensor_tensor(out=self.rstd[:], in0=self.ve[:], in1=core.minus_half[:, 0:self.tiles], op=ALU.pow)\
            .then_inc(self.rstd_ready.sem, 1)


NORM_STEPS = 3 * GT


def small_attention(nc, core, name, *, src, norms, affine, w, q_scale, bq=None, bk=None, bv=None,
                    rope=None, causal=False, finish, out_norm=None, prefetch=None):
    H, DH = 16, 8
    UNITS = QT * H // 2
    LAG = 2 if norms == 2 else 3
    with ExitStack() as ctx:
        sb, ps, sig = allocator(nc, ctx, name)
        SRC = core.X if src == "X" else core.Y
        DST = core.X if finish == "X_plus" else core.Y
        fronts = ["h", "q"] + (["qr"] if rope else []) + ["k"] + (["kr"] if rope else []) + ["v"]
        tails = ["n0", "n1", "on", "out"]
        order = fronts + tails
        NORM_SLOTS = (0, 1, 3)
        at_slot = {"h": NORM_SLOTS[norms] + 1}
        for n, x in enumerate(fronts[1:]):
            at_slot[x] = at_slot["h"] + 1 + n
        T0 = at_slot["v"] + 1
        at_slot["n0"], at_slot["on"], at_slot["out"] = T0, T0 + 2, T0 + 3
        F = [ps("F0"), ps("F1")]
        S = [ps("S0"), ps("S1")]
        T = [ps("T0"), ps("T1")]
        O = [ps("O0"), ps("O1")]

        def bank(part):
            return F[order.index(part) % 2]

        raw = sb("raw", [P, QT, D])
        yn = sb("yn", [P, QT, D])
        hn = sb("hn", [P, QT, D]) if norms == 2 else yn
        hT = sb("hT", [P, L])
        qT = sb("qT", [P, 2, L])
        kT = sb("kT", [P, 2, L])
        rt = sb("rt", [P, 2, L]) if rope else None
        kblk = sb("kblk", [P, 2, H, L])
        Vp = sb("Vp", [P, GT, H, 32])
        nmax = sb("nmax", [P, 4, 2])
        prob = sb("prob", [P, 4, 2, L])
        probT = sb("probT", [P, 4, 2, L])
        oT = sb("oT", [P, 4, L])
        rden = sb("rden", [P, QT, H])
        on = sb("on", [P, QT, D])
        onT = sb("onT", [P, L])
        fin = sb("fin", [P, QT, D])

        lns = [Norm(sb, sig, f"ln{n}", QT, 2) for n in range(norms)]
        oln = Norm(sb, sig, "oln", QT, 2) if out_norm else None
        keeps = finish in ("y_plus", "y_norm")
        front_steps = norms * 3 * QT + (1 if rope else 0)
        tail_steps = 1 + (3 * QT + 2 if out_norm else 0)
        front_chain = sig("front_chain", 2 * front_steps)
        tail_chain = sig("tail_chain", 2 * tail_steps)
        hold = sig("hold").sem
        fetched, kept, normed = sig("fetched", 2), sig("kept", 2), sig("normed", 2)
        added = sig("added", 2)
        made = {x: sig("made_" + x, 2) for x in order}
        taken = {x: sig("taken_" + x, 2, 3) for x in order}
        ready = {x: sig("ready_" + x, 2) if rope else taken[x] for x in "qk"}
        zeroed = sig("zeroed")
        k_spread = sig("k_spread", 2)
        scored = sig("scored", 2 * UNITS, UNITS + 1)
        maxed = sig("maxed", 2 * UNITS)
        exped = sig("exped", 2 * UNITS, 4)
        turned = sig("turned", 2 * UNITS, 4)
        turn_copied = [sig(f"turn_copied{n}", UNITS, 2) for n in range(2)]
        pv_done = sig("pv_done", 2 * UNITS, 4)
        oT_copied = sig("oT_copied", 2, 1)
        block = ctx.enter_context(nc.Block())

        def keys(w_):
            return (w_ % UNITS // (H // 2) + 1) * P if causal else L

        def turns(eng, turn):
            turn(0, True, False)
            with eng.Fori(1, TURNS - 1) as i:
                turn(i, False, False)
            turn(TURNS - 1, False, True)

        @block.sync
        def _(sp):
            if prefetch:
                prefetch(sp)

        @block.gpsimd
        def _(pool):
            for s in range(2):
                pool.memset(kblk[:, s], 0.0).then_inc(zeroed.sem, 1)
            pool.wait_ge(zeroed.sem, 2)

            def front(i, s):
                for ln in lns:
                    ln.on_pool(pool, core, i, s)
                pool.wait_ge(ready["k"].sem, ready["k"].at(i, s + 1))
                pool.wait_ge(scored.sem, scored.at(i, (s - 1) * UNITS))
                for g in range(4):
                    rows = slice(32 * g, 32 * g + 32)
                    ins = pool.tensor_tensor(
                        out=kblk[rows, s % 2, 4 * g:4 * g + 4, :],
                        in0=kT[rows, s % 2, None, :].to_broadcast([32, 4, L]),
                        in1=core.head_mask[rows, :, None].to_broadcast([32, 4, L]), op=ALU.mult)
                ins.then_inc(k_spread.sem, 1)
                pool.wait_ge(k_spread.sem, k_spread.at(i, s + 1))

            def turn(i, first, last):
                for s in range(2):
                    if not (last and s == 1):
                        front(i, s + 1)
                    if oln and not (first and s == 0):
                        oln.on_pool(pool, core, i, s - 1)

            front(0, 0)
            turns(pool, turn)
            if oln:
                oln.on_pool(pool, core, TURNS - 1, 1)

        @block.scalar
        def _(act):
            for g in (exped, oT_copied, turn_copied[1]):
                act.sem_inc(g.sem, g.lead)
            for x in ("h", "on") + (() if rope else ("k",)):
                act.sem_inc(taken[x].sem, taken[x].lead)

            def front_h(i, s):
                act.wait_ge(made["h"].sem, made["h"].at(i, s + 1))
                if affine:
                    act.activation(hT[:], bank("h")[:, 0:L], ACT.Identity, scale=affine[0],
                                   bias=affine[1]).then_inc(taken["h"].sem, 1)
                else:
                    act.activation(hT[:], bank("h")[:, 0:L], ACT.Copy).then_inc(taken["h"].sem, 1)

            def front_k(i, s):
                act.wait_ge(made["k"].sem, made["k"].at(i, s + 1))
                if bk is not None:
                    act.activation(kT[:, s % 2, :], bank("k")[:, 0:L], ACT.Identity, bias=bk)\
                        .then_inc(taken["k"].sem, 1)
                else:
                    act.activation(kT[:, s % 2, :], bank("k")[:, 0:L], ACT.Copy).then_inc(taken["k"].sem, 1)

            def copy_turned(i, w_):
                act.wait_ge(turned.sem, turned.at(i, w_ + 1))
                act.wait_ge(pv_done.sem, pv_done.at(i, w_ - 3))
                act.activation(probT[:, w_ % 4, :, 0:keys(w_)],
                               T[1][:, 0:2 * keys(w_)].rearrange("p (j k) -> p j k", j=2), ACT.Copy)\
                    .then_inc(turn_copied[1].sem, 1)

            def tail_o(i, s):
                act.wait_ge(pv_done.sem, pv_done.at(i, (s + 1) * UNITS))
                for m in range(2):
                    ins = act.activation(oT[:, 2 * m:2 * m + 2, :], O[m][:].rearrange("p (g q) -> p g q", g=2),
                                         ACT.Copy)
                ins.then_inc(oT_copied.sem, 1)

            def tail_on(i, s):
                act.wait_ge(made["on"].sem, made["on"].at(i, s + 1))
                act.activation(onT[:], bank("on")[:, 0:L], ACT.Copy).then_inc(taken["on"].sem, 1)

            def turn(i, first, last):
                for w_ in range(2 * UNITS):
                    s, u = w_ // UNITS, w_ % UNITS
                    has_front, has_tail = not (last and s == 1), not (first and s == 0)
                    act.wait_ge(maxed.sem, maxed.at(i, w_ + 1))
                    act.wait_ge(turned.sem, turned.at(i, w_ - 3))
                    for j in range(2):
                        ins = act.activation(prob[:, w_ % 4, j, 0:keys(w_)],
                                             S[w_ % 2][:, j * keys(w_):(j + 1) * keys(w_)], ACT.Exp,
                                             bias=nmax[:, w_ % 4, j:j + 1])
                    ins.then_inc(exped.sem, 1)
                    if (w_ - LAG) % 2 == 1 and not (first and w_ < LAG):
                        copy_turned(i, w_ - LAG)
                    if has_tail and u == LAG:
                        tail_o(i, s - 1)
                    if has_front and u == at_slot["h"]:
                        front_h(i, s + 1)
                    if has_front and not rope and u == at_slot["k"]:
                        front_k(i, s + 1)
                    if has_tail and u == at_slot["on"]:
                        tail_on(i, s - 1)

            front_h(0, 0)
            if not rope:
                front_k(0, 0)
            turns(act, turn)
            for w_ in range(2 * UNITS - LAG, 2 * UNITS):
                if w_ % 2 == 1:
                    copy_turned(TURNS - 1, w_)
            tail_o(TURNS - 1, 1)
            tail_on(TURNS - 1, 1)

        @block.vector
        def _(dve):
            dve.memset(Vp[:], 0.0).then_inc(zeroed.sem, 1)
            dve.wait_ge(zeroed.sem, 3)
            dve.memset(Vp[:, :, :, DH:DH + 1], 1.0).then_inc(zeroed.sem, 1)
            dve.wait_ge(zeroed.sem, 4)
            dve.sem_inc(turn_copied[0].sem, turn_copied[0].lead)
            for x in ("q", "v", "n0", "n1", "out") + (("qr", "k", "kr") if rope else ()):
                dve.sem_inc(taken[x].sem, taken[x].lead)

            def here(buf):
                return lambda t: buf[:, t, :]

            def stream(buf, i, s):
                return buf[:, bass.ds(i * GT + QT * s, QT), :]

            def front_norm(i, s, chain, part):
                if part == 0:
                    dve.tensor_scalar(raw[:], stream(SRC, i, s), 1.0, None, ALU.mult).then_inc(fetched.sem, 1)
                    dve.wait_ge(fetched.sem, fetched.at(i, s + 1))
                    lns[0].statistics(dve, chain, hold, here(raw))
                elif part == 1:
                    lns[0].apply(dve, chain, i, s, here(raw), here(yn))
                    chain.settle()
                    if keeps:
                        dve.tensor_scalar(stream(core.Y, i, s), yn[:], 1.0, None, ALU.mult).then_inc(kept.sem, 1)
                        dve.wait_ge(kept.sem, kept.at(i, s + 1))
                    if norms == 2:
                        dve.sem_inc(hold, 1)
                        lns[1].statistics(dve, chain, hold, here(yn))
                    else:
                        dve.sem_inc(normed.sem, 1)
                elif norms == 2:
                    lns[1].apply(dve, chain, i, s, here(yn), here(hn))
                    chain.settle()
                    dve.sem_inc(normed.sem, 1)

            def front_part(x, i, s, chain):
                if rope and x != "v":
                    a = x[0]
                    n = len(x) - 1
                    bias = (bq if a == "q" else bk)
                    dst = (qT if a == "q" else kT)[:, s % 2, :]
                    dve.wait_ge(made[x].sem, made[x].at(i, s + 1))
                    dve.scalar_tensor_tensor(out=rt[:, n, :], in0=bank(x)[:, 0:L],
                                             scalar=bias[n] if bias is not None else 0.0, in1=rope[n],
                                             op0=ALU.add, op1=ALU.mult).then_inc(taken[x].sem, 1)
                    if n == 1:
                        dve.wait_ge(taken[x].sem, taken[x].at(i, s + 1))
                        dve.wait_ge(taken[a].sem, taken[a].at(i, s + 1))
                        summed = dve.tensor_tensor(out=dst, in0=rt[:, 0], in1=rt[:, 1], op=ALU.add)
                        if a == "q":
                            chain.step(summed)
                            chain.settle()
                            dve.tensor_scalar(dst, dst, q_scale, None, ALU.mult).then_inc(ready["q"].sem, 1)
                        else:
                            summed.then_inc(ready["k"].sem, 1)
                        dve.wait_ge(ready[a].sem, ready[a].at(i, s + 1))
                elif x == "q":
                    dve.wait_ge(made["q"].sem, made["q"].at(i, s + 1))
                    dve.tensor_scalar(qT[:, s % 2, :], bank("q")[:, 0:L], bq if bq is not None else 0.0, q_scale,
                                      ALU.add, ALU.mult).then_inc(taken["q"].sem, 1)
                elif x == "v":
                    dve.wait_ge(made["v"].sem, made["v"].at(i, s + 1))
                    vsrc = bank("v")[:, 0:L].rearrange("p (t h d) -> p t h d", t=QT, h=H)
                    for t in range(QT):
                        dst = Vp[:, s % 2 * QT + t, :, 0:DH]
                        if bv is not None:
                            ins = dve.tensor_tensor(out=dst, in0=vsrc[:, t],
                                                    in1=bv[:].rearrange("p (h d) -> p h d", h=H), op=ALU.add)
                        else:
                            ins = dve.tensor_copy(dst, vsrc[:, t])
                    ins.then_inc(taken["v"].sem, 1)

            def tail_n(i, s, chain):
                nat = [bank(f"n{t}")[:].rearrange("p (h r) -> p h r", h=H) for t in range(QT)]
                for t in range(QT):
                    dve.wait_ge(made[f"n{t}"].sem, made[f"n{t}"].at(i, s + 1))
                    ins = dve.reciprocal(rden[:, t, :], nat[t][:, :, DH])
                chain.step(ins)
                chain.settle()
                for t in range(QT):
                    dve.tensor_tensor(out=on[:, t, :].rearrange("p (h d) -> p h d", h=H), in0=nat[t][:, :, 0:DH],
                                      in1=rden[:, t, :, None].to_broadcast([P, H, DH]), op=ALU.mult)\
                        .then_inc(taken[f"n{t}"].sem, 1)

            def tail_out(i, s, chain, part):
                got = bank("out")[:, 0:L].rearrange("p (t d) -> p t d", t=QT)
                onto = stream(DST, i, s)
                if part == 0:
                    dve.wait_ge(made["out"].sem, made["out"].at(i, s + 1))
                    if finish in ("y_plus", "Y_plus"):
                        dve.tensor_tensor(out=onto, in0=got, in1=onto, op=ALU.add).then_inc(taken["out"].sem, 1)
                        return
                    dve.tensor_tensor(out=fin[:], in0=got, in1=w["bo"][:, None, :].to_broadcast([P, QT, D]),
                                      op=ALU.add).then_inc(taken["out"].sem, 1)
                    dve.wait_ge(taken["out"].sem, taken["out"].at(i, s + 1))
                    if oln:
                        dve.sem_inc(hold, 1)
                        oln.statistics(dve, chain, hold, here(fin))
                        return
                elif not oln:
                    return
                else:
                    oln.apply(dve, chain, i, s, here(fin), here(fin))
                    chain.settle()
                    for other, op in ((out_norm[0], ALU.mult), (out_norm[1], ALU.add)):
                        chain.step(dve.tensor_tensor(out=fin[:], in0=fin[:],
                                                     in1=other[:, None, :].to_broadcast([P, QT, D]), op=op))
                        chain.settle()
                dve.tensor_tensor(out=onto, in0=fin[:], in1=onto, op=ALU.add).then_inc(added.sem, 1)
                dve.wait_ge(added.sem, added.at(i, s + 1))

            def chain_of(signal, i, s, n):
                c = Chain(dve, signal, i)
                c.n = s * n
                return c

            def maximum(i, w_):
                dve.wait_ge(scored.sem, scored.at(i, w_ + 1))
                dve.wait_ge(exped.sem, exped.at(i, w_ - 3))
                dve.tensor_reduce(out=nmax[:, w_ % 4, :],
                                  in_=S[w_ % 2][:, 0:2 * keys(w_)].rearrange("p (j k) -> p j k", j=2),
                                  op=ALU.max, axis=AX.X, negate=True).then_inc(maxed.sem, 1)

            def copy_turned(i, w_):
                dve.wait_ge(turned.sem, turned.at(i, w_ + 1))
                dve.wait_ge(pv_done.sem, pv_done.at(i, w_ - 3))
                dve.tensor_copy(probT[:, w_ % 4, :, 0:keys(w_)],
                                T[w_ % 2][:, 0:2 * keys(w_)].rearrange("p (j k) -> p j k", j=2))\
                    .then_inc(turn_copied[0].sem, 1)

            def turn(i, first, last):
                for s in range(2):
                    fc = chain_of(front_chain, i, s + 1, front_steps)
                    tc = chain_of(tail_chain, i, s - 1, tail_steps)
                    for u in range(UNITS):
                        w_ = s * UNITS + u
                        maximum(i, w_)
                        if (w_ - LAG) % 2 == 0 and not (first and w_ < LAG):
                            copy_turned(i, w_ - LAG)
                        if not (last and s == 1):
                            if u in NORM_SLOTS:
                                front_norm(i, s + 1, fc, NORM_SLOTS.index(u))
                            for x in fronts[1:]:
                                if u == at_slot[x]:
                                    front_part(x, i, s + 1, fc)
                        if not (first and s == 0):
                            if u == at_slot["n0"] + 1:
                                tail_n(i, s - 1, tc)
                            if u == at_slot["out"]:
                                tail_out(i, s - 1, tc, 0)
                            if u == at_slot["out"] + 1:
                                tail_out(i, s - 1, tc, 1)
                    assert (last and s == 1) or fc.n == (s + 2) * front_steps, (fc.n, front_steps)
                    assert (first and s == 0) or tc.n <= s * tail_steps, (tc.n, tail_steps)

            fc = chain_of(front_chain, 0, 0, front_steps)
            for part in range(3):
                front_norm(0, 0, fc, part)
            for x in fronts[1:]:
                front_part(x, 0, 0, fc)
            turns(dve, turn)
            for w_ in range(2 * UNITS - LAG, 2 * UNITS):
                if w_ % 2 == 0:
                    copy_turned(TURNS - 1, w_)
            tc = chain_of(tail_chain, TURNS - 1, 1, tail_steps)
            tail_n(TURNS - 1, 1, tc)
            for part in range(2):
                tail_out(TURNS - 1, 1, tc, part)

        @block.tensor
        def _(pe):
            for g in (scored, turned, pv_done):
                pe.sem_inc(g.sem, g.lead)

            def claim(x, i, s, no_front=False):
                n = order.index(x) - 2
                if x in fronts:
                    prev, k = order[n], s + 1 if n >= 0 else s - 2
                elif n >= len(fronts):
                    prev, k = order[n], s + 1
                elif no_front:
                    prev, k = order[n + len(tails)], s
                else:
                    prev, k = order[n], s + 3
                pe.wait_ge(taken[prev].sem, taken[prev].at(i, k))

            def front_part(x, i, s):
                if x == "h":
                    pe.wait_ge(normed.sem, normed.at(i, s + 1))
                    claim("h", i, s)
                    for t in range(QT):
                        ins = pe.transpose(bank("h")[:, t * P:(t + 1) * P], hn[:, t, :], core.ident[:])
                    ins.then_inc(made["h"].sem, 1)
                    return
                pe.wait_ge(taken["h"].sem, taken["h"].at(i, s + 1))
                claim(x, i, s)
                if x == "v":
                    for t in range(QT):
                        ins = pe.matmul(bank("v")[:, t * P:(t + 1) * P], hT[:, t * P:(t + 1) * P], w["v"][:],
                                        start=True, stop=True)
                    ins.then_inc(made["v"].sem, 1)
                else:
                    pe.matmul(bank(x)[:, 0:L], w[x][:], hT[:], start=True, stop=True).then_inc(made[x].sem, 1)

            def tail_part(x, i, s, no_front=False):
                if x == "n0":
                    pe.wait_ge(oT_copied.sem, oT_copied.at(i, s + 1))
                    for t in range(QT):
                        claim(f"n{t}", i, s, no_front)
                        for g in range(4):
                            ins = pe.transpose(bank(f"n{t}")[:, g * P:(g + 1) * P], oT[:, g, t * P:(t + 1) * P],
                                               core.ident[:])
                        ins.then_inc(made[f"n{t}"].sem, 1)
                elif x == "on":
                    for t in range(QT):
                        pe.wait_ge(taken[f"n{t}"].sem, taken[f"n{t}"].at(i, s + 1))
                    for t in range(QT):
                        ins = pe.transpose(bank("on")[:, t * P:(t + 1) * P], on[:, t, :], core.ident[:])
                    ins.then_inc(made["on"].sem, 1)
                else:
                    pe.wait_ge(taken["on"].sem, taken["on"].at(i, s + 1))
                    claim("out", i, s)
                    for t in range(QT):
                        ins = pe.matmul(bank("out")[:, t * P:(t + 1) * P], onT[:, t * P:(t + 1) * P], w["o"][:],
                                        start=True, stop=True)
                    ins.then_inc(made["out"].sem, 1)

            def score(i, w_):
                s, u = w_ // UNITS, w_ % UNITS
                t, pair = u // (H // 2), u % (H // 2)
                if u == 0:
                    pe.wait_ge(ready["q"].sem, ready["q"].at(i, s + 1))
                    pe.wait_ge(taken["v"].sem, taken["v"].at(i, s + 1))
                    pe.wait_ge(k_spread.sem, k_spread.at(i, s + 1))
                pe.wait_ge(exped.sem, exped.at(i, w_ - 1))
                out = S[w_ % 2][:, 0:2 * keys(w_)]
                ins = pe.matmul(out, qT[:, s % 2, t * P:(t + 1) * P], kblk[:, s % 2, 2 * pair:2 * pair + 2, 0:keys(w_)],
                                start=True, stop=not causal)
                if causal:
                    ins = pe.matmul(out.rearrange("p (j k) -> p j k", j=2)[:, :, t * P:(t + 1) * P],
                                    core.ident16[:], core.causal16[:, None, :].to_broadcast([P, 2, P]),
                                    start=False, stop=True)
                ins.then_inc(scored.sem, 1)

            def turn_unit(i, w_):
                pe.wait_ge(exped.sem, exped.at(i, w_ + 1))
                pe.wait_ge(turn_copied[w_ % 2].sem, turn_copied[w_ % 2].at(i, w_ // 2))
                for j in range(2):
                    for kt in range(keys(w_) // P):
                        ins = pe.transpose(T[w_ % 2][:, j * keys(w_) + kt * P:j * keys(w_) + (kt + 1) * P],
                                           prob[:, w_ % 4, j, kt * P:(kt + 1) * P], core.ident[:])
                ins.then_inc(turned.sem, 1)

            def weigh(i, w_):
                s, u = w_ // UNITS, w_ % UNITS
                t, pair = u // (H // 2), u % (H // 2)
                pe.wait_ge(turn_copied[w_ % 2].sem, turn_copied[w_ % 2].at(i, w_ // 2 + 1))
                if u == 0:
                    pe.wait_ge(oT_copied.sem, oT_copied.at(i, s))
                for kt in range(keys(w_) // P):
                    for j in range(2):
                        h = 2 * pair + j
                        g, c = h // 4, h % 4
                        ins = pe.matmul(O[g // 2][32 * c:32 * c + 32, (g % 2) * L + t * P:(g % 2) * L + (t + 1) * P],
                                        Vp[:, s % 2 * QT + kt, h, :], probT[:, w_ % 4, j, kt * P:(kt + 1) * P],
                                        start=kt == 0, stop=kt == keys(w_) // P - 1)
                ins.then_inc(pv_done.sem, 1)

            def turn(i, first, last):
                for w_ in range(2 * UNITS):
                    s, u = w_ // UNITS, w_ % UNITS
                    score(i, w_)
                    if not (first and w_ < LAG):
                        turn_unit(i, w_ - LAG)
                    if not (first and w_ < LAG + 1):
                        weigh(i, w_ - LAG - 1)
                    if not (last and s == 1):
                        for x in fronts:
                            if u == at_slot[x]:
                                front_part(x, i, s + 1)
                    if not (first and s == 0):
                        for x in ("n0", "on", "out"):
                            if u == at_slot[x]:
                                tail_part(x, i, s - 1, last and s == 1)

            for x in fronts:
                front_part(x, 0, 0)
            turns(pe, turn)
            for w_ in range(2 * UNITS, 2 * UNITS + LAG + 1):
                if w_ - LAG < 2 * UNITS:
                    turn_unit(TURNS - 1, w_ - LAG)
                weigh(TURNS - 1, w_ - LAG - 1)
            for x in ("n0", "on", "out"):
                tail_part(x, TURNS - 1, 1, True)


def wide_attention(nc, core, name, *, heads_per_step, w, w_loaded, rope=None, bq=None, bk=None, bv=None,
                   q_scale=1.0, slopes=None, bo=None, prefetch=None):
    STEPS = 8
    AHEAD = 2
    HS = heads_per_step
    DH = P // HS
    SLOTS = 4
    US = 2 * HS
    UNITS = STEPS * US
    W0, W1 = P, 2 * P
    WIDE = W0 + W1
    pieces = [("q",), ("k", "v")] if HS == 1 else [("q",), (), ("k",), ("v",)]
    STATS_AT, APPLY_AT = 2 * US, 2 * US + 2
    H_AT = (STEPS - AHEAD) * US - 1
    LAG = 2 if HS == 1 else 3
    YT_AT, OUT_AT = LAG + 3, LAG + 4
    uses = []
    for w_ in range(UNITS):
        uses += [(x, w_ // US + AHEAD) for x in pieces[w_ % US]]
        if w_ == OUT_AT:
            uses.append(("out", -1))
        if w_ == H_AT:
            uses.append(("h", 1))
    assert len(uses) % 2 == 0
    with ExitStack() as ctx:
        sb, ps, sig = allocator(nc, ctx, name)
        F = [ps("F0"), ps("F1")]
        S = [ps("S0"), ps("S1")]
        T = ps("T")
        O = [ps("O0"), ps("O1")]
        Z = ps("Z")

        raw = sb("raw", [P, GT, D])
        yn = sb("yn", [P, GT, D])
        hT = sb("hT", [P, GN])
        qT = sb("qT", [P, SLOTS, GN])
        kT = sb("kT", [P, SLOTS, HS, GN])
        rt = sb("rt", [P, 2, 2, GN]) if rope else None
        V = sb("V", [P, SLOTS, GT, P])
        biased = sb("biased", [P, 2, WIDE]) if slopes else None
        nmax = sb("nmax", [P, 4, 2])
        total = sb("total", [P, 4, 2])
        rden = sb("rden", [P, 4, 2])
        prob = sb("prob", [P, 4, WIDE])
        probT = sb("probT", [P, 4, WIDE])
        oT = sb("oT", [P, 2, GN])
        yT = sb("yT", [P, GN])
        fin = sb("fin", [P, GT, D]) if bo is not None else None

        ln = Norm(sb, sig, "ln")
        chained = sig("chained", NORM_STEPS)
        hold = sig("hold").sem
        fetched, normed, streamed = sig("fetched"), sig("normed"), sig("streamed")
        made = {"h": sig("made_h"), "q": sig("made_q", STEPS), "k": sig("made_k", STEPS),
                "v": sig("made_v", STEPS), "out": sig("made_out")}
        taken = {"h": sig("taken_h", 1, 1), "q": sig("taken_q", STEPS, 1), "k": sig("taken_k", STEPS, 1),
                 "v": sig("taken_v", STEPS, 1), "out": sig("taken_out", 1, 1)}
        ready = {x: sig("ready_" + x, STEPS, 1) if rope else taken[x] for x in "qk"}
        k_zeroed = sig("k_zeroed")
        scored = sig("scored", UNITS, SLOTS * US)
        biased_up = sig("biased_up", UNITS, 2) if slopes else None
        maxed = sig("maxed", UNITS)
        exped = sig("exped", UNITS, 4)
        inverted = sig("inverted", UNITS)
        divided = sig("divided", UNITS)
        turned = sig("turned", UNITS, 4)
        turn_copied = sig("turn_copied", UNITS, 4)
        pv_done = sig("pv_done", UNITS, SLOTS * US)
        oT_copied = sig("oT_copied", STEPS, 2)
        projected = sig("projected", STEPS, 2)
        yT_copied = sig("yT_copied", 1, 1)
        block = ctx.enter_context(nc.Block())

        parts = ((0, W0), (W0, WIDE))

        def bank(x, m):
            return F[[(y, n % STEPS if y in "qkv" else n) for y, n in uses]
                     .index((x, m % STEPS if x in "qkv" else m)) % 2]

        def turns(eng, turn):
            turn(0, True, False)
            with eng.Fori(1, TURNS - 1) as i:
                turn(i, False, False)
            turn(TURNS - 1, False, True)

        def projections(w_, last):
            m = w_ // US + AHEAD
            return [] if last and m >= STEPS else [(x, m) for x in pieces[w_ % US]]

        head = [(x, m) for m in range(STEPS, STEPS + AHEAD) for part in pieces for x in part]

        @block.sync
        def _(sp):
            if prefetch:
                prefetch(sp)

        @block.gpsimd
        def _(pool):
            if rope:
                for x in "qk":
                    pool.sem_inc(ready[x].sem, ready[x].lead)

            def rotate(i, x, m):
                n = "qk".index(x)
                pool.wait_ge(taken[x].sem, taken[x].at(i, m + 1))
                pool.wait_ge(scored.sem, scored.at(i, (m + 1 - SLOTS) * US))
                dst = qT[:, m % SLOTS, :] if x == "q" else kT[:, m % SLOTS, 0, :]
                pool.tensor_tensor(out=dst, in0=rt[:, n, 0, :], in1=rt[:, n, 1, :], op=ALU.add)\
                    .then_inc(ready[x].sem, 1)

            def turn(i, first, last):
                for w_ in range(UNITS):
                    if rope:
                        for x, m in projections(w_, last):
                            if x in "qk":
                                rotate(i, x, m)
                    if w_ == STATS_AT and not last:
                        ln.on_pool(pool, core, i, 1)
                    pool.wait_ge(inverted.sem, inverted.at(i, w_ + 1))
                    for n, (a, b) in enumerate(parts):
                        ins = pool.tensor_tensor(out=prob[:, w_ % 4, a:b], in0=prob[:, w_ % 4, a:b],
                                                 in1=rden[:, w_ % 4, n:n + 1].to_broadcast([P, b - a]), op=ALU.mult)
                    ins.then_inc(divided.sem, 1)

            ln.on_pool(pool, core, 0)
            if rope:
                for x, m in head:
                    if x in "qk":
                        rotate(-1, x, m)
            turns(pool, turn)

        @block.scalar
        def _(act):
            for g in (taken["h"], exped, oT_copied, yT_copied) + (() if rope else (taken["k"],)) \
                    + ((taken["v"],) if bv is None else ()):
                act.sem_inc(g.sem, g.lead)
            if HS == 2:
                act.wait_ge(k_zeroed.sem, 1)

            def front_h(i, s):
                act.wait_ge(made["h"].sem, made["h"].at(i, s + 1))
                act.activation(hT[:], bank("h", 1)[:], ACT.Copy).then_inc(taken["h"].sem, 1)

            def evacuate(i, x, m):
                if x == "k" and not rope:
                    act.wait_ge(made["k"].sem, made["k"].at(i, m + 1))
                    act.wait_ge(scored.sem, scored.at(i, (m + 1 - SLOTS) * US))
                    for j in range(HS):
                        rows = slice(j * DH, (j + 1) * DH)
                        ins = act.activation(kT[rows, m % SLOTS, j, :], bank("k", m)[rows, :], ACT.Identity,
                                             bias=bk[rows, m % STEPS:m % STEPS + 1])
                    ins.then_inc(taken["k"].sem, 1)
                if x == "v" and bv is None:
                    act.wait_ge(made["v"].sem, made["v"].at(i, m + 1))
                    act.wait_ge(pv_done.sem, pv_done.at(i, (m + 1 - SLOTS) * US))
                    act.activation(V[:, m % SLOTS], bank("v", m)[:].rearrange("p (t d) -> p t d", t=GT),
                                   ACT.Copy).then_inc(taken["v"].sem, 1)

            def exponentials(i, w_):
                act.wait_ge(maxed.sem, maxed.at(i, w_ + 1))
                act.wait_ge(turned.sem, turned.at(i, w_ - 3))
                for n, (a, b) in enumerate(parts):
                    src = biased[:, w_ % 2, a:b] if slopes else S[w_ % 2][:, a:b]
                    ins = act.activation(prob[:, w_ % 4, a:b], src, ACT.Exp, bias=nmax[:, w_ % 4, n:n + 1],
                                         accum_out=total[:, w_ % 4, n:n + 1])
                ins.then_inc(exped.sem, 1)

            def copy_out(i, w_):
                m = (w_ - LAG - 2) // US
                if (w_ - LAG - 2) % US == US - 1:
                    act.wait_ge(pv_done.sem, pv_done.at(i, (m + 1) * US))
                    act.wait_ge(projected.sem, projected.at(i, m - 1))
                    act.activation(oT[:, m % 2, :], O[m % 2][:], ACT.Copy).then_inc(oT_copied.sem, 1)

            def copy_y(i, s):
                act.wait_ge(projected.sem, projected.at(i, (s + 1) * STEPS))
                act.activation(yT[:], Z[:], ACT.Copy).then_inc(yT_copied.sem, 1)

            def turn(i, first, last):
                for w_ in range(UNITS):
                    exponentials(i, w_)
                    if not (first and w_ < LAG + 2):
                        copy_out(i, w_)
                    for x, m in projections(w_, last):
                        evacuate(i, x, m)
                    if w_ == YT_AT and not first:
                        copy_y(i, -1)
                    if w_ == H_AT and not last:
                        front_h(i, 1)

            front_h(0, 0)
            for x, m in head:
                evacuate(-1, x, m)
            turns(act, turn)
            for w_ in range(UNITS, UNITS + LAG + 2):
                copy_out(TURNS - 1, w_)
            copy_y(TURNS - 1, 0)

        @block.vector
        def _(dve):
            if HS == 2:
                dve.memset(kT[:], 0.0).then_inc(k_zeroed.sem, 1)
            for g in (taken["q"], taken["out"], turn_copied) + ((taken["k"],) if rope else ()) \
                    + ((taken["v"],) if bv is not None else ()) + ((biased_up,) if slopes else ()):
                dve.sem_inc(g.sem, g.lead)

            def here(buf):
                return lambda t: buf[:, t, :]

            def norm_chain(i, s, n):
                chain = Chain(dve, chained, i)
                chain.n = s * chained.per + n
                return chain

            def front_statistics(i, s):
                dve.tensor_copy(raw[:], core.X[:, bass.ds(i * GT + s * GT, GT), :]).then_inc(fetched.sem, 1)
                dve.wait_ge(fetched.sem, fetched.at(i, s + 1))
                ln.statistics(dve, norm_chain(i, s, 0), hold, here(raw))

            def front_apply(i, s):
                chain = norm_chain(i, s, 2 * GT)
                ln.apply(dve, chain, i, s, here(raw), here(yn))
                chain.settle()
                dve.sem_inc(normed.sem, 1)

            def evacuate(i, x, m):
                if rope and x in "qk":
                    n = "qk".index(x)
                    cos, sin = rope[n]
                    psum = bank(x, m)[:].rearrange("p (s q) -> p s q", s=2)
                    dve.wait_ge(made[x].sem, made[x].at(i, m + 1))
                    dve.wait_ge(ready[x].sem, ready[x].at(i, m))
                    dve.tensor_tensor(out=rt[:, n, 0, :].rearrange("p (s q) -> p s q", s=2), in0=psum,
                                      in1=cos[:, None, :].to_broadcast([P, 2, L]), op=ALU.mult)
                    for lo, hi in ((0, P // 2), (P // 2, 0)):
                        ins = dve.tensor_tensor(
                            out=rt[lo:lo + P // 2, n, 1, :].rearrange("p (s q) -> p s q", s=2),
                            in0=psum[hi:hi + P // 2],
                            in1=sin[hi:hi + P // 2, None, :].to_broadcast([P // 2, 2, L]), op=ALU.mult)
                    ins.then_inc(taken[x].sem, 1)
                elif x == "q":
                    dve.wait_ge(made["q"].sem, made["q"].at(i, m + 1))
                    dve.wait_ge(scored.sem, scored.at(i, (m + 1 - SLOTS) * US))
                    dve.tensor_scalar(qT[:, m % SLOTS, :], bank("q", m)[:], bq[:, m % STEPS:m % STEPS + 1], q_scale,
                                      ALU.add, ALU.mult).then_inc(taken["q"].sem, 1)
                elif x == "v" and bv is not None:
                    cols = slice(m % STEPS * P, (m % STEPS + 1) * P)
                    dve.wait_ge(made["v"].sem, made["v"].at(i, m + 1))
                    dve.wait_ge(pv_done.sem, pv_done.at(i, (m + 1 - SLOTS) * US))
                    dve.tensor_tensor(out=V[:, m % SLOTS], in0=bank("v", m)[:].rearrange("p (t d) -> p t d", t=GT),
                                      in1=bv[:, None, cols].to_broadcast([P, GT, P]),
                                      op=ALU.add).then_inc(taken["v"].sem, 1)

            def maximum(i, w_):
                dve.wait_ge(scored.sem, scored.at(i, w_ + 1))
                src = S[w_ % 2]
                if slopes:
                    dve.wait_ge(exped.sem, exped.at(i, w_ - 1))
                    dve.scalar_tensor_tensor(out=biased[:, w_ % 2, :], in0=core.distance[:],
                                             scalar=slopes[w_ // US * HS + w_ % HS], in1=S[w_ % 2][:, 0:WIDE],
                                             op0=ALU.mult, op1=ALU.add).then_inc(biased_up.sem, 1)
                    dve.wait_ge(biased_up.sem, biased_up.at(i, w_ + 1))
                    src = biased[:, w_ % 2]
                dve.wait_ge(exped.sem, exped.at(i, w_ - 3))
                for n, (a, b) in enumerate(parts):
                    ins = dve.tensor_reduce(out=nmax[:, w_ % 4, n:n + 1], in_=src[:, a:b], op=ALU.max,
                                            axis=AX.X, negate=True)
                ins.then_inc(maxed.sem, 1)

            def invert(i, w_):
                dve.wait_ge(exped.sem, exped.at(i, w_ + 1))
                dve.reciprocal(rden[:, w_ % 4, :], total[:, w_ % 4, :]).then_inc(inverted.sem, 1)

            def copy_turned(i, w_):
                dve.wait_ge(turned.sem, turned.at(i, w_ + 1))
                dve.wait_ge(pv_done.sem, pv_done.at(i, w_ - 3))
                dve.tensor_copy(probT[:, w_ % 4, :], T[:, 0:WIDE]).then_inc(turn_copied.sem, 1)

            def tail(i, s):
                got = bank("out", -1)[:].rearrange("p (t d) -> p t d", t=GT)
                onto = core.X[:, bass.ds(i * GT + s * GT, GT), :]
                dve.wait_ge(made["out"].sem, made["out"].at(i, s + 1))
                if bo is None:
                    dve.tensor_tensor(out=onto, in0=got, in1=onto, op=ALU.add).then_inc(taken["out"].sem, 1)
                    return
                dve.tensor_tensor(out=fin[:], in0=got, in1=bo[:, None, :].to_broadcast([P, GT, D]),
                                  op=ALU.add).then_inc(taken["out"].sem, 1)
                dve.wait_ge(taken["out"].sem, taken["out"].at(i, s + 1))
                dve.tensor_tensor(out=onto, in0=fin[:], in1=onto, op=ALU.add).then_inc(streamed.sem, 1)
                dve.wait_ge(streamed.sem, streamed.at(i, s + 1))
                dve.sem_inc(hold, 1)

            def turn(i, first, last):
                for w_ in range(UNITS):
                    maximum(i, w_)
                    if not (first and w_ < 1):
                        invert(i, w_ - 1)
                    if not (first and w_ < LAG):
                        copy_turned(i, w_ - LAG)
                    for x, m in projections(w_, last):
                        evacuate(i, x, m)
                    if w_ == STATS_AT and not last:
                        front_statistics(i, 1)
                    if w_ == APPLY_AT and not last:
                        front_apply(i, 1)
                    if w_ == OUT_AT and not first:
                        tail(i, -1)

            front_statistics(0, 0)
            front_apply(0, 0)
            for x, m in head:
                evacuate(-1, x, m)
            turns(dve, turn)
            invert(TURNS - 1, UNITS - 1)
            for w_ in range(UNITS, UNITS + LAG):
                copy_turned(TURNS - 1, w_ - LAG)
            tail(TURNS - 1, 0)

        @block.tensor
        def _(pe):
            for g in (scored, turned, pv_done, projected):
                pe.sem_inc(g.sem, g.lead)
            pe.wait_ge(w_loaded[0], w_loaded[1])

            def claim(i, x, m):
                n = uses.index((x, m)) - 2
                y, k = uses[n]
                back = 0 if n >= 0 else -1
                pe.wait_ge(taken[y].sem, taken[y].at(i, k + 1 + back * taken[y].per))
                if y == "out":
                    y, k = uses[n - 2]
                    pe.wait_ge(taken[y].sem, taken[y].at(i, k + 1))

            def front_h(i, s):
                pe.wait_ge(normed.sem, normed.at(i, s + 1))
                claim(i - 1 + s, "h", 1)
                for t in range(GT):
                    ins = pe.transpose(bank("h", 1)[:, t * P:(t + 1) * P], yn[:, t, :], core.ident[:])
                ins.then_inc(made["h"].sem, 1)

            def project(i, x, m):
                cols = slice(m % STEPS * P, (m % STEPS + 1) * P)
                if x == "q" and m == STEPS:
                    pe.wait_ge(taken["h"].sem, taken["h"].at(i, 2))
                claim(i, x, m)
                if x == "v":
                    for t in range(GT):
                        ins = pe.matmul(bank("v", m)[:, t * P:(t + 1) * P], hT[:, t * P:(t + 1) * P],
                                        w["v"][:, cols], start=True, stop=True)
                else:
                    ins = pe.matmul(bank(x, m)[:], w[x][:, cols], hT[:], start=True, stop=True)
                ins.then_inc(made[x].sem, 1)

            def unit(w_):
                return w_ // US, (w_ % US) // HS, w_ % HS

            def score(i, w_):
                m, s, j = unit(w_)
                if w_ % US == 0:
                    for x in "qk":
                        pe.wait_ge(ready[x].sem, ready[x].at(i, m + 1))
                if slopes:
                    pe.wait_ge(biased_up.sem, biased_up.at(i, w_ - 1))
                else:
                    pe.wait_ge(exped.sem, exped.at(i, w_ - 1))
                for t, (a, b) in enumerate(parts):
                    ins = pe.matmul(S[w_ % 2][:, a:b], qT[:, m % SLOTS, s * L + t * P:s * L + (t + 1) * P],
                                    kT[:, m % SLOTS, j, s * L:s * L + b - a], start=True, stop=bool(slopes))
                    if not slopes:
                        ins = pe.matmul(S[w_ % 2][:, b - P:b], core.ident16[:], core.causal16[:],
                                        start=False, stop=True)
                ins.then_inc(scored.sem, 1)

            def turn_unit(i, w_):
                pe.wait_ge(divided.sem, divided.at(i, w_ + 1))
                pe.wait_ge(turn_copied.sem, turn_copied.at(i, w_))
                for n in range(3):
                    ins = pe.transpose(T[:, n * P:(n + 1) * P], prob[:, w_ % 4, n * P:(n + 1) * P], core.ident[:])
                ins.then_inc(turned.sem, 1)

            def weigh(i, w_):
                m, s, j = unit(w_)
                pe.wait_ge(turn_copied.sem, turn_copied.at(i, w_ + 1))
                if w_ % US == 0:
                    pe.wait_ge(taken["v"].sem, taken["v"].at(i, m + 1))
                    pe.wait_ge(oT_copied.sem, oT_copied.at(i, m - 1))
                out = O[m % 2][j * DH:(j + 1) * DH, :]
                cols = slice(j * DH, (j + 1) * DH)
                pe.matmul(out[:, s * L:(s + 1) * L], V[:, m % SLOTS, s * QT, cols], probT[:, w_ % 4, 0:L],
                          start=True, stop=False)
                pe.matmul(out[:, s * L + P:(s + 1) * L], V[:, m % SLOTS, s * QT + 1, cols], probT[:, w_ % 4, L:WIDE],
                          start=False, stop=True).then_inc(pv_done.sem, 1)

            def output(i, w_):
                m = (w_ - LAG - 3) // US
                if (w_ - LAG - 3) % US == US - 1:
                    pe.wait_ge(oT_copied.sem, oT_copied.at(i, m + 1))
                    if m == 0:
                        pe.wait_ge(yT_copied.sem, yT_copied.at(i, 0))
                    pe.matmul(Z[:], w["o"][:, m % STEPS, :], oT[:, m % 2, :], start=m % STEPS == 0,
                              stop=m % STEPS == STEPS - 1).then_inc(projected.sem, 1)

            def tail(i, s):
                pe.wait_ge(yT_copied.sem, yT_copied.at(i, s + 1))
                if s < 0:
                    claim(i, "out", -1)
                else:
                    for x in "qkv":
                        pe.wait_ge(taken[x].sem, taken[x].at(i, STEPS))
                for t in range(GT):
                    ins = pe.transpose(bank("out", -1)[:, t * P:(t + 1) * P], yT[:, t * P:(t + 1) * P], core.ident[:])
                ins.then_inc(made["out"].sem, 1)

            def turn(i, first, last):
                for w_ in range(UNITS):
                    score(i, w_)
                    if not (first and w_ < LAG):
                        turn_unit(i, w_ - LAG)
                    if not (first and w_ < LAG + 1):
                        weigh(i, w_ - LAG - 1)
                    if not (first and w_ < LAG + 3):
                        output(i, w_)
                    for x, m in projections(w_, last):
                        project(i, x, m)
                    if w_ == OUT_AT and not first:
                        tail(i, -1)
                    if w_ == H_AT and not last:
                        front_h(i, 1)

            front_h(0, 0)
            for x, m in head:
                project(-1, x, m)
            turns(pe, turn)
            for w_ in range(UNITS, UNITS + LAG + 3):
                if w_ - LAG < UNITS:
                    turn_unit(TURNS - 1, w_ - LAG)
                if w_ - LAG - 1 < UNITS:
                    weigh(TURNS - 1, w_ - LAG - 1)
                output(TURNS - 1, w_)
            tail(TURNS - 1, 0)


def experts(nc, core, name, *, affine, normed_in, w_loaded, gate, gate_b, act_fn, top, b1=None, b2=None,
            out_norm=None, prefetch=None):
    E, FC = 8, 4
    FRONT_AT = 4
    CHOSEN_AT = 3
    with ExitStack() as ctx:
        sb, ps, sig = allocator(nc, ctx, name)
        steps = ["h", "logit"] + (["comb", "bias"] if top == 2 else [])
        F = [ps("F0"), ps("F1")]
        H = [ps(f"H{n}") for n in range(FC)]
        YB = [ps("Y0"), ps("Y1")]

        def bank(s):
            return F[steps.index(s) % 2]

        raw = sb("raw", [P, GT, D])
        yn = sb("yn", [P, GT, D]) if normed_in else raw
        hT = sb("hT", [P, GN])
        h_parts = sb("h_parts", [P, 2, GN], F32R)
        W1_parts = sb("W1_parts", [P, 2, E, FC * P], F32R)
        hidden = sb("hidden", [P, 2, FC, GN])
        acc = sb("acc", [P, GT, D])
        fin = sb("fin", [P, GT, D])
        lg = sb("lg", [P, GT, E])
        pr = sb("pr", [P, GT, E])
        pick = sb("pick", [P, 2, GT, E])
        tmp = sb("tmp", [P, GT, E])
        top_v = sb("top_v", [P, GT])
        comb = sb("comb", [P, GT, E])
        combT = sb("combT", [E, GN])
        lns = [Norm(sb, sig, "ln")] if normed_in else []
        oln = Norm(sb, sig, "oln") if out_norm else None
        front_chain = sig("front_chain", NORM_STEPS * len(lns))
        W1_rounded, W1_split = sig("W1_rounded", 0), sig("W1_split", 0)
        h_split = sig("h_split")
        chained = sig("chained", (NORM_STEPS + 2 if oln else 0) + (16 if top == 2 else 5) + 1)
        hold = sig("hold").sem
        fetched, normed, streamed = sig("fetched"), sig("normed"), sig("streamed")
        made = {s: sig("made_" + s) for s in steps}
        taken = {s: sig("taken_" + s, 1, 1) for s in steps}
        shifted, softened = sig("shifted"), sig("softened")
        combined = sig("combined")
        hid = sig("hid", E * FC)
        acted = sig("acted", E * FC, FC)
        y_done = sig("y_done", E, 2)
        added = sig("added", E, 2)
        block = ctx.enter_context(nc.Block())

        def turns(eng, turn):
            with eng.Fori(0, TURNS - 1) as i:
                turn(i, False)
            turn(TURNS - 1, True)

        @block.sync
        def _(sp):
            if prefetch:
                prefetch(sp)

        @block.gpsimd
        def _(pool):
            def split_h(i, s):
                pool.wait_ge(taken["h"].sem, taken["h"].at(i, s + 1))
                pool.tensor_tensor(out=h_parts[:, 1, :], in0=hT[:], in1=h_parts[:, 0, :], op=ALU.subtract)\
                    .then_inc(h_split.sem, 1)

            def turn(i, last):
                if lns and not last:
                    lns[0].on_pool(pool, core, i, 1)
                if not last:
                    split_h(i, 1)
                if oln:
                    oln.on_pool(pool, core, i)

            if lns:
                lns[0].on_pool(pool, core, 0)
            for e in range(E):
                pool.wait_ge(W1_rounded.sem, e + 1)
                pool.tensor_tensor(out=W1_parts[:, 1, e, :], in0=core.W1[:, e, :], in1=W1_parts[:, 0, e, :],
                                   op=ALU.subtract).then_inc(W1_split.sem, 1)
                if e == 0:
                    split_h(0, 0)
            turns(pool, turn)

        @block.scalar
        def _(act):
            for g in [taken[s] for s in steps if s in ("h", "comb")] + [acted]:
                act.sem_inc(g.sem, g.lead)

            def front(i, s):
                act.wait_ge(made["h"].sem, made["h"].at(i, s + 1))
                for dst in (h_parts[:, 0, :], hT[:]):
                    if affine:
                        ins = act.activation(dst, bank("h")[:], ACT.Identity, scale=affine[0], bias=affine[1])
                    else:
                        ins = act.activation(dst, bank("h")[:], ACT.Copy)
                ins.then_inc(taken["h"].sem, 1)

            def turn(i, last):
                for e in range(E):
                    act.wait_ge(y_done.sem, y_done.at(i, e - 1))
                    for f in range(FC):
                        n = e * FC + f
                        act.wait_ge(hid.sem, hid.at(i, n + 1))
                        if b1 is not None:
                            ins = act.activation(hidden[:, e % 2, f, :], H[f][:], act_fn, bias=b1[:, n:n + 1])
                        else:
                            ins = act.activation(hidden[:, e % 2, f, :], H[f][:], act_fn)
                        ins.then_inc(acted.sem, 1)
                    if e == 0 and top == 2:
                        act.wait_ge(shifted.sem, shifted.at(i))
                        act.activation(pr[:], lg[:], ACT.Exp).then_inc(softened.sem, 1)
                    if e == CHOSEN_AT and top == 2:
                        act.wait_ge(made["comb"].sem, made["comb"].at(i))
                        act.activation(combT[:], bank("comb")[0:E, :], ACT.Copy).then_inc(taken["comb"].sem, 1)
                if not last:
                    front(i, 1)

            front(0, 0)
            turns(act, turn)

        @block.vector
        def _(dve):
            for g in [taken[s] for s in steps if s in ("logit", "bias")] + [added]:
                dve.sem_inc(g.sem, g.lead)

            def here(buf):
                return lambda t: buf[:, t, :]

            def front(i, s):
                chain = Chain(dve, front_chain, i)
                chain.n = s * front_chain.per
                dve.tensor_copy(raw[:], core.Y[:, bass.ds(i * GT + s * GT, GT), :]).then_inc(fetched.sem, 1)
                dve.wait_ge(fetched.sem, fetched.at(i, s + 1))
                if lns:
                    lns[0].statistics(dve, chain, hold, here(raw))
                    lns[0].apply(dve, chain, i, s, here(raw), here(yn))
                    chain.settle()
                dve.sem_inc(normed.sem, 1)

            def turn(i, last):
                chain = Chain(dve, chained, i)

                def run(ins):
                    chain.step(ins)
                    chain.settle()

                def over(t):
                    return t[:, :, None].to_broadcast([P, GT, E])

                rank = core.rank[:, None, :].to_broadcast([P, GT, E])

                def choose(src, dst):
                    run(dve.tensor_reduce(out=top_v[:], in_=src, op=ALU.max, axis=AX.X))
                    run(dve.tensor_tensor(out=tmp[:], in0=src, in1=over(top_v[:]), op=ALU.is_ge))
                    run(dve.tensor_tensor(out=tmp[:], in0=tmp[:], in1=rank, op=ALU.mult))
                    run(dve.tensor_reduce(out=top_v[:], in_=tmp[:], op=ALU.max, axis=AX.X))
                    run(dve.tensor_tensor(out=dst, in0=rank, in1=over(top_v[:]), op=ALU.is_equal))

                dve.wait_ge(made["logit"].sem, made["logit"].at(i))
                dve.tensor_tensor(out=lg[:], in0=bank("logit")[:, 0:GT * E].rearrange("p (t e) -> p t e", t=GT),
                                  in1=gate_b[:, None, :].to_broadcast([P, GT, E]), op=ALU.add)\
                    .then_inc(taken["logit"].sem, 1)
                dve.wait_ge(taken["logit"].sem, taken["logit"].at(i))
                if top == 1:
                    choose(lg[:], comb[:])
                else:
                    run(dve.tensor_reduce(out=top_v[:], in_=lg[:], op=ALU.max, axis=AX.X))
                    dve.tensor_tensor(out=lg[:], in0=lg[:], in1=over(top_v[:]), op=ALU.subtract)\
                        .then_inc(shifted.sem, 1)
                    dve.wait_ge(softened.sem, softened.at(i))
                    run(dve.reduce_sum(top_v[:], pr[:], axis=AX.X))
                    run(dve.reciprocal(top_v[:], top_v[:]))
                    run(dve.tensor_tensor(out=pr[:], in0=pr[:], in1=over(top_v[:]), op=ALU.mult))
                    choose(pr[:], pick[:, 0])
                    run(dve.scalar_tensor_tensor(out=lg[:], in0=pick[:, 0], scalar=-2.0, in1=pr[:], op0=ALU.mult,
                                                 op1=ALU.add))
                    choose(lg[:], pick[:, 1])
                    run(dve.tensor_tensor(out=tmp[:], in0=pick[:, 0], in1=pick[:, 1], op=ALU.add))
                    dve.tensor_tensor(out=comb[:], in0=tmp[:], in1=pr[:], op=ALU.mult).then_inc(combined.sem, 1)
                    dve.wait_ge(combined.sem, combined.at(i))
                for e in range(E):
                    dve.wait_ge(y_done.sem, y_done.at(i, e + 1))
                    if e:
                        dve.wait_ge(added.sem, added.at(i, e))
                    for t in range(GT):
                        y = YB[e % 2][:, t * P:(t + 1) * P]
                        if e == 0:
                            ins = dve.tensor_scalar(acc[:, t, :], y, comb[:, t, 0:1], None, ALU.mult)
                        else:
                            ins = dve.scalar_tensor_tensor(out=acc[:, t, :], in0=y, scalar=comb[:, t, e:e + 1],
                                                           in1=acc[:, t, :], op0=ALU.mult, op1=ALU.add)
                    ins.then_inc(added.sem, 1)
                    if e == CHOSEN_AT and top == 2:
                        dve.wait_ge(made["bias"].sem, made["bias"].at(i))
                        dve.wait_ge(added.sem, added.at(i, e + 1))
                        dve.tensor_tensor(out=acc[:], in0=bank("bias")[:].rearrange("p (t d) -> p t d", t=GT),
                                          in1=acc[:], op=ALU.add).then_inc(taken["bias"].sem, 1)
                        dve.wait_ge(taken["bias"].sem, taken["bias"].at(i))
                    if e == FRONT_AT and not last:
                        front(i, 1)
                dve.wait_ge(added.sem, added.at(i, E))
                res = acc
                if oln:
                    dve.sem_inc(hold, 1)
                    oln.on_vector(dve, chain, hold, i, here(acc), here(fin))
                    chain.settle()
                    g, b = out_norm
                    run(dve.tensor_tensor(out=fin[:], in0=fin[:], in1=g[:, None, :].to_broadcast([P, GT, D]),
                                          op=ALU.mult))
                    run(dve.tensor_tensor(out=fin[:], in0=fin[:], in1=b[:, None, :].to_broadcast([P, GT, D]),
                                          op=ALU.add))
                    res = fin
                run(dve.tensor_tensor(out=fin[:], in0=res[:], in1=core.Y[:, bass.ds(i * GT, GT), :], op=ALU.add))
                Xt = core.X[:, bass.ds(i * GT, GT), :]
                dve.tensor_tensor(out=Xt, in0=fin[:], in1=Xt, op=ALU.add).then_inc(streamed.sem, 1)
                dve.wait_ge(streamed.sem, streamed.at(i))
                dve.sem_inc(hold, 1)
                chain.counted()

            front(0, 0)
            dve.wait_ge(w_loaded[0], w_loaded[1])
            for e in range(E):
                dve.tensor_copy(W1_parts[:, 0, e, :], core.W1[:, e, :]).then_inc(W1_rounded.sem, 1)
            turns(dve, turn)

        @block.tensor
        def _(pe):
            pe.sem_inc(y_done.sem, y_done.lead)
            pe.wait_ge(w_loaded[0], w_loaded[1])

            def claim(x, i, s=0):
                n = steps.index(x) - 2
                pe.wait_ge(taken[steps[n]].sem, taken[steps[n]].at(i, s + (1 if n >= 0 else 0)))

            def front(i, s):
                pe.wait_ge(normed.sem, normed.at(i, s + 1))
                claim("h", i, s)
                for t in range(GT):
                    ins = pe.transpose(bank("h")[:, t * P:(t + 1) * P], yn[:, t, :], core.ident[:])
                ins.then_inc(made["h"].sem, 1)

            def turn(i, last):
                pe.wait_ge(taken["h"].sem, taken["h"].at(i))
                claim("logit", i)
                for t in range(GT):
                    ins = pe.matmul(bank("logit")[:, t * E:(t + 1) * E], hT[:, t * P:(t + 1) * P], gate[:],
                                    start=True, stop=True)
                ins.then_inc(made["logit"].sem, 1)

                pe.wait_ge(h_split.sem, h_split.at(i))

                def hidden_layer(e):
                    pe.wait_ge(W1_split.sem, e + 1)
                    for f in range(FC):
                        n = e * FC + f
                        pe.wait_ge(acted.sem, acted.at(i, n - FC + 1))
                        for k, (a, b) in enumerate(((1, 0), (0, 1), (0, 0))):
                            ins = pe.matmul(H[f][:], W1_parts[:, a, e, f * P:(f + 1) * P], h_parts[:, b, :],
                                            start=k == 0, stop=k == 2)
                        ins.then_inc(hid.sem, 1)

                def output(e):
                    pe.wait_ge(acted.sem, acted.at(i, (e + 1) * FC))
                    pe.wait_ge(added.sem, added.at(i, e - 1))
                    for t in range(GT):
                        for f in range(FC):
                            ins = pe.matmul(YB[e % 2][:, t * P:(t + 1) * P], hidden[:, e % 2, f, t * P:(t + 1) * P],
                                            core.W2[:, e, f, :], start=f == 0, stop=f == FC - 1)
                    ins.then_inc(y_done.sem, 1)

                for e in range(E + 1):
                    if e < E:
                        hidden_layer(e)
                    if e == E - 1 and not last:
                        front(i, 1)
                    if e >= 1:
                        output(e - 1)
                    if e == CHOSEN_AT and top == 2:
                        pe.wait_ge(combined.sem, combined.at(i))
                        claim("comb", i)
                        for t in range(GT):
                            ins = pe.transpose(bank("comb")[0:E, t * P:(t + 1) * P], comb[:, t, :], core.ident[:])
                        ins.then_inc(made["comb"].sem, 1)
                        pe.wait_ge(taken["comb"].sem, taken["comb"].at(i))
                        claim("bias", i)
                        for t in range(GT):
                            ins = pe.matmul(bank("bias")[:, t * P:(t + 1) * P], combT[:, t * P:(t + 1) * P], b2[:],
                                            start=True, stop=True)
                        ins.then_inc(made["bias"].sem, 1)

            front(0, 0)
            turns(pe, turn)


def state_space(nc, core, name, *, affine):
    N, CT = 16, 2
    WS = N * CT
    NORM_AT = (4, 8, 12)
    HT_AT, XPAD_AT = 17, 20
    TAP_AT = (23, 25, 27, 29)
    H_STATE, X_STATE, G_STATE = 8, 9, 12
    with ExitStack() as ctx:
        sb, ps, sig = allocator(nc, ctx, name)
        F = [ps("F0"), ps("F1"), ps("F2")]
        BB = [ps("B0"), ps("B1")]
        CB = ps("C")
        YS = [ps("Y0"), ps("Y1")]
        uses = ["h", "x0", "x1", "g0", "g1", "out", "bc", "dt0", "dt1"]
        assert len(uses) % len(F) == 0

        def bank(u):
            return F[uses.index(u) % len(F)]

        raw = sb("raw", [P, GT, D])
        yn = sb("yn", [P, GT, D])
        hn = raw
        hT = sb("hT", [P, GN])
        xpad = sb("xpad", [P, CT, 2, 3 + L])
        conv = sb("conv", [P, CT, 2, L])
        xc = sb("xc", [P, CT, GN])
        sg = sb("sg", [P, CT, GN])
        bc = sb("bc", [32, GN])
        left = sb("left", [32, 2, GN])
        bc3 = sb("bc3", [96, GN], BF16)
        sel = sb("sel", [96, 2 * N, P], BF16)
        ab = sb("ab", [P, CT, GN])
        lg = conv[:].rearrange("p c s q -> p c (s q)")
        dt = sb("dt", [P, CT, GN])
        du = sb("du", [P, CT, GN])
        A = sb("A", [P, CT, N])
        one = sb("one", [P, 1])
        dA = sb("dA", [P, 4, GN])
        bu = sb("bu", [P, 3, GN])
        hs = sb("hs", [P, 4, GN])
        Cs = sb("Cs", [P, 2, GN])
        hc = sb("hc", [P, 4, GN])
        yg = ab
        lns = [Norm(sb, sig, "ln0"), Norm(sb, sig, "ln1")]
        front_chain = sig("front_chain", 2 * NORM_STEPS + 4 * CT)
        chained = sig("chained", 4 + CT + 2 * CT)
        hold = sig("hold").sem
        fetched, kept, normed = sig("fetched"), sig("kept"), sig("normed")
        made = {u: sig("made_" + u) for u in uses}
        taken = {u: sig("taken_" + u, 1, 1) for u in uses}
        ready = sig("ready", 4)
        convolved = sig("convolved")
        activated = sig("activated")
        split = sig("split")
        magnitude = sig("magnitude", CT)
        log_made = sig("log_made")
        dt_made = sig("dt_made")
        dt_exp = sig("dt_exp")
        a_made = sig("a_made", 1)
        b_made = sig("b_made", N)
        c_made, c_taken = sig("c_made", N), sig("c_taken", N, 1)
        dA_made, scanned = sig("dA_made", WS), sig("scanned", WS, 4)
        bu_made = sig("bu_made", WS, 2 * CT)
        hc_made, summed = sig("hc_made", WS, 4), sig("summed", WS, 4)
        gated = sig("gated", 1, 1)
        block = ctx.enter_context(nc.Block())

        def turns(eng, turn):
            with eng.Fori(0, TURNS - 1) as i:
                turn(i, False)
            turn(TURNS - 1, True)

        @block.gpsimd
        def _(pool):
            pool.sem_inc(hc_made.sem, hc_made.lead)
            pool.memset(xpad[:], 0.0).then_inc(ready.sem, 1)
            pool.memset(one[:], 1.0).then_inc(ready.sem, 1)
            pool.memset(sel[:], 0.0).then_inc(ready.sem, 1)
            for ln in lns:
                ln.on_pool(pool, core, 0)
                pool.wait_ge(ln.rstd_ready.sem, 1)
            pool.wait_ge(ready.sem, 3)
            for g in range(3):
                rows = sel[32 * g:32 * g + 32]
                pool.affine_select(out=rows, in_=rows, compare_op=ALU.not_equal, fill=1.0, base=0,
                                   pattern=[[-1, 2 * N], [0, P]], channel_multiplier=1).then_inc(ready.sem, 1)
            pool.wait_ge(ready.sem, 6)

            def turn(i, last):
                for w_ in range(WS):
                    for ln, at in zip(lns, NORM_AT):
                        if w_ == at and not last:
                            ln.on_pool(pool, core, i, 1)
                    pool.wait_ge(scanned.sem, scanned.at(i, w_ + 1))
                    pool.wait_ge(c_taken.sem, c_taken.at(i, w_ // CT + 1))
                    pool.wait_ge(summed.sem, summed.at(i, w_ - 3))
                    pool.tensor_tensor(out=hc[:, w_ % 4, :], in0=hs[:, w_ % 4, :], in1=Cs[:, (w_ // CT) % 2, :],
                                       op=ALU.mult).then_inc(hc_made.sem, 1)

            turns(pool, turn)

        @block.scalar
        def _(act):
            for g in (taken["h"], taken["x0"], taken["x1"], taken["g0"], taken["g1"], c_taken):
                act.sem_inc(g.sem, g.lead)
            act.activation(A[:], core.a_log[:], ACT.Exp).then_inc(a_made.sem, 1)
            act.wait_ge(ready.sem, 2)

            def front_h(i, s):
                act.wait_ge(made["h"].sem, made["h"].at(i, s + 1))
                act.activation(hT[:], bank("h")[:], ACT.Identity, scale=affine[0], bias=affine[1])\
                    .then_inc(taken["h"].sem, 1)

            def front_x(i, s):
                for c in range(CT):
                    act.wait_ge(made[f"x{c}"].sem, made[f"x{c}"].at(i, s + 1))
                    act.activation(xpad[:, c, :, 3:3 + L], bank(f"x{c}")[:].rearrange("p (s q) -> p s q", s=2),
                                   ACT.Copy).then_inc(taken[f"x{c}"].sem, 1)

            def turn(i, last):
                act.wait_ge(gated.sem, gated.at(i, 0))
                for c in range(CT):
                    act.wait_ge(made[f"g{c}"].sem, made[f"g{c}"].at(i))
                    act.activation(sg[:, c, :], bank(f"g{c}")[:], ACT.Silu).then_inc(taken[f"g{c}"].sem, 1)
                act.wait_ge(convolved.sem, convolved.at(i))
                for c in range(CT):
                    ins = act.activation(xc[:, c, :], conv[:, c].rearrange("p s q -> p (s q)"), ACT.Silu,
                                         bias=core.conv_b[:, c:c + 1])
                ins.then_inc(activated.sem, 1)
                for c in range(CT):
                    act.wait_ge(made[f"dt{c}"].sem, made[f"dt{c}"].at(i))
                    act.activation(ab[:, c, :], bank(f"dt{c}")[:], ACT.Abs, bias=core.dt_b[:, c:c + 1])\
                        .then_inc(magnitude.sem, 1)
                act.wait_ge(magnitude.sem, magnitude.at(i, CT))
                act.activation(lg, ab[:], ACT.Exp, scale=-1.0).then_inc(dt_exp.sem, 1)
                act.wait_ge(dt_exp.sem, dt_exp.at(i))
                act.activation(ab[:], lg, ACT.Ln, bias=one[:, 0:1]).then_inc(log_made.sem, 1)
                act.wait_ge(dt_made.sem, dt_made.at(i))
                for w_ in range(WS):
                    n, c = w_ // CT, w_ % CT
                    act.wait_ge(scanned.sem, scanned.at(i, w_ - 3))
                    act.activation(dA[:, w_ % 4, :], dt[:, c, :], ACT.Exp, scale=A[:, c, n:n + 1])\
                        .then_inc(dA_made.sem, 1)
                    if c == 0:
                        act.wait_ge(c_made.sem, c_made.at(i, n + 1))
                        act.wait_ge(hc_made.sem, hc_made.at(i, 2 * n - 2))
                        act.activation(Cs[:, n % 2, :], CB[:], ACT.Copy).then_inc(c_taken.sem, 1)
                    if w_ == HT_AT and not last:
                        front_h(i, 1)
                    if w_ == XPAD_AT and not last:
                        front_x(i, 1)

            front_h(0, 0)
            front_x(0, 0)
            turns(act, turn)

        @block.vector
        def _(dve):
            for g in (taken["bc"], taken["dt0"], taken["dt1"], taken["out"], bu_made, scanned, gated):
                dve.sem_inc(g.sem, g.lead)
            dve.wait_ge(a_made.sem, 1)
            dve.tensor_scalar(A[:], A[:], -1.0, None, ALU.mult).then_inc(a_made.sem, 1)
            dve.wait_ge(a_made.sem, 2)

            def here(buf):
                return lambda t: buf[:, t, :]

            def front_chain_of(i, s):
                chain = Chain(dve, front_chain, i)
                chain.n = s * front_chain.per
                return chain

            def front_norm(i, s, chain, part):
                if part == 0:
                    dve.tensor_copy(raw[:], core.X[:, bass.ds(i * GT + s * GT, GT), :]).then_inc(fetched.sem, 1)
                    dve.wait_ge(fetched.sem, fetched.at(i, s + 1))
                    lns[0].statistics(dve, chain, hold, here(raw))
                elif part == 1:
                    lns[0].apply(dve, chain, i, s, here(raw), here(yn))
                    chain.settle()
                    dve.tensor_scalar(core.Y[:, bass.ds(i * GT + s * GT, GT), :], yn[:], 1.0, None, ALU.mult)\
                        .then_inc(kept.sem, 1)
                    dve.wait_ge(kept.sem, kept.at(i, s + 1))
                    dve.sem_inc(hold, 1)
                    lns[1].statistics(dve, chain, hold, here(yn))
                else:
                    lns[1].apply(dve, chain, i, s, here(yn), here(hn))
                    chain.settle()
                    dve.sem_inc(normed.sem, 1)

            def front_tap(i, s, chain, k):
                if k == 0:
                    for c in range(CT):
                        dve.wait_ge(taken[f"x{c}"].sem, taken[f"x{c}"].at(i, s + 1))
                for c in range(CT):
                    tap = xpad[:, c, :, k:k + L]
                    wk = core.conv_w[:, c, k:k + 1]
                    if k == 0:
                        chain.step(dve.tensor_scalar(conv[:, c], tap, wk, None, ALU.mult))
                    else:
                        chain.step(dve.scalar_tensor_tensor(out=conv[:, c], in0=tap, scalar=wk, in1=conv[:, c],
                                                            op0=ALU.mult, op1=ALU.add))
                chain.settle()
                if k == 3:
                    dve.sem_inc(convolved.sem, 1)

            def turn(i, last):
                chain = Chain(dve, chained, i)
                fc = front_chain_of(i, 1)

                def run(ins):
                    chain.step(ins)
                    chain.settle()

                dve.wait_ge(made["bc"].sem, made["bc"].at(i))
                dve.tensor_copy(bc[:], bank("bc")[0:32, :]).then_inc(taken["bc"].sem, 1)
                dve.wait_ge(taken["bc"].sem, taken["bc"].at(i))
                run(dve.tensor_copy(bc3[0:32, :], bc[:]))
                run(dve.tensor_tensor(out=left[:, 0, :], in0=bc[:], in1=bc3[0:32, :], op=ALU.subtract))
                run(dve.tensor_copy(bc3[32:64, :], left[:, 0, :]))
                run(dve.tensor_copy(left[:, 1, :], bc3[32:64, :]))
                dve.tensor_tensor(out=bc3[64:96, :], in0=left[:, 0, :], in1=left[:, 1, :], op=ALU.subtract)\
                    .then_inc(split.sem, 1)
                for c in range(CT):
                    dve.wait_ge(magnitude.sem, magnitude.at(i, c + 1))
                    dve.tensor_scalar(dt[:, c, :], bank(f"dt{c}")[:], core.dt_b[:, c:c + 1], 0.0, ALU.add,
                                      ALU.max).then_inc(taken[f"dt{c}"].sem, 1)
                    dve.wait_ge(taken[f"dt{c}"].sem, taken[f"dt{c}"].at(i))
                dve.wait_ge(log_made.sem, log_made.at(i))
                dve.tensor_tensor(out=dt[:], in0=dt[:], in1=ab[:], op=ALU.add).then_inc(dt_made.sem, 1)
                dve.wait_ge(dt_made.sem, dt_made.at(i))
                for c in range(CT):
                    chain.step(dve.tensor_tensor(out=du[:, c, :], in0=dt[:, c, :], in1=xc[:, c, :], op=ALU.mult))
                chain.settle()

                def inflow(w_):
                    n, c = w_ // CT, w_ % CT
                    if c == 0:
                        dve.wait_ge(b_made.sem, b_made.at(i, n + 1))
                    dve.wait_ge(scanned.sem, scanned.at(i, w_ - 2))
                    dve.tensor_tensor(out=bu[:, w_ % 3, :], in0=du[:, c, :], in1=BB[n % 2][:], op=ALU.mult)\
                        .then_inc(bu_made.sem, 1)

                inflow(0)
                for w_ in range(WS):
                    if w_ + 1 < WS:
                        inflow(w_ + 1)
                    dve.wait_ge(bu_made.sem, bu_made.at(i, w_ + 1))
                    dve.wait_ge(dA_made.sem, dA_made.at(i, w_ + 1))
                    dve.wait_ge(hc_made.sem, hc_made.at(i, w_ - 3))
                    for s in range(2):
                        q = slice(s * L, (s + 1) * L)
                        ins = dve.tensor_tensor_scan(hs[:, w_ % 4, q], dA[:, w_ % 4, q], bu[:, w_ % 3, q], 0.0,
                                                     ALU.mult, ALU.add)
                    ins.then_inc(scanned.sem, 1)
                    if not last and w_ in NORM_AT:
                        front_norm(i, 1, fc, NORM_AT.index(w_))
                    if not last and w_ in TAP_AT:
                        front_tap(i, 1, fc, TAP_AT.index(w_))
                dve.wait_ge(summed.sem, summed.at(i, WS))
                for c in range(CT):
                    chain.step(dve.scalar_tensor_tensor(out=yg[:, c, :], in0=xc[:, c, :], scalar=core.d_skip[:, c:c + 1],
                                                        in1=YS[c][:], op0=ALU.mult, op1=ALU.add))
                chain.settle()
                for c in range(CT):
                    chain.step(dve.tensor_tensor(out=yg[:, c, :], in0=yg[:, c, :], in1=sg[:, c, :], op=ALU.mult))
                chain.settle()
                dve.sem_inc(gated.sem, 1)
                dve.wait_ge(made["out"].sem, made["out"].at(i))
                onto = core.Y[:, bass.ds(i * GT, GT), :]
                dve.tensor_tensor(out=onto, in0=bank("out")[:].rearrange("p (t d) -> p t d", t=GT), in1=onto,
                                  op=ALU.add).then_inc(taken["out"].sem, 1)
                chain.counted()

            first = front_chain_of(0, 0)
            for part in range(3):
                front_norm(0, 0, first, part)
            for k in range(4):
                front_tap(0, 0, first, k)
            turns(dve, turn)

        @block.tensor
        def _(pe):
            pe.sem_inc(summed.sem, summed.lead)

            def claim(u, i, s=0):
                y = uses[uses.index(u) - len(F)]
                later = {"h": -1, "x0": -1, "x1": -1, "dt1": -1, "out": 1}.get(u, 0)
                pe.wait_ge(taken[y].sem, taken[y].at(i, s + 1 + later))

            def front_h(i, s):
                pe.wait_ge(normed.sem, normed.at(i, s + 1))
                claim("h", i, s)
                for t in range(GT):
                    ins = pe.transpose(bank("h")[:, t * P:(t + 1) * P], hn[:, t, :], core.ident[:])
                ins.then_inc(made["h"].sem, 1)

            def front_in(u, i, s):
                n = ("x0", "x1", "g0", "g1").index(u)
                pe.wait_ge(taken["h"].sem, taken["h"].at(i, s + 1))
                claim(u, i, s)
                pe.matmul(bank(u)[:], core.in_w[:, n * P:(n + 1) * P], hT[:], start=True, stop=True)\
                    .then_inc(made[u].sem, 1)

            def front(state, i, s):
                if state == H_STATE:
                    front_h(i, s)
                for part, at in (("x", X_STATE), ("g", G_STATE)):
                    if state == at:
                        for c in range(CT):
                            front_in(f"{part}{c}", i, s)

            def turn(i, last):
                pe.wait_ge(activated.sem, activated.at(i))
                claim("bc", i)
                for c in range(CT):
                    ins = pe.matmul(bank("bc")[0:32, :], core.x_w[:, c, :], xc[:, c, :], start=c == 0, stop=c == 1)
                ins.then_inc(made["bc"].sem, 1)
                pe.wait_ge(taken["bc"].sem, taken["bc"].at(i))
                for c in range(CT):
                    claim(f"dt{c}", i)
                    pe.matmul(bank(f"dt{c}")[:], core.dt_w[:, c * P:(c + 1) * P], bc[0:N, :], start=True, stop=True)\
                        .then_inc(made[f"dt{c}"].sem, 1)
                pe.wait_ge(split.sem, split.at(i))
                pe.wait_ge(ready.sem, 6)
                for n in range(N + 2):
                    if n < N:
                        pe.wait_ge(bu_made.sem, bu_made.at(i, CT * (n - 1)))
                        pe.matmul(BB[n % 2][:], sel[:, n, :], bc3[:], start=True, stop=True).then_inc(b_made.sem, 1)
                        pe.wait_ge(c_taken.sem, c_taken.at(i, n))
                        pe.matmul(CB[:], sel[:, N + n, :], bc3[:], start=True, stop=True).then_inc(c_made.sem, 1)
                    if n >= 2:
                        for c in range(CT):
                            w_ = (n - 2) * CT + c
                            pe.wait_ge(hc_made.sem, hc_made.at(i, w_ + 1))
                            if n == 2:
                                pe.wait_ge(gated.sem, gated.at(i, 0))
                            pe.matmul(YS[c][:], core.ident[:], hc[:, w_ % 4, :], start=n == 2, stop=n == N + 1)\
                                .then_inc(summed.sem, 1)
                    if not last:
                        front(n, i, 1)
                pe.wait_ge(gated.sem, gated.at(i))
                if last:
                    pe.wait_ge(taken["x1"].sem, taken["x1"].at(i))
                    pe.wait_ge(taken["dt1"].sem, taken["dt1"].at(i))
                else:
                    claim("out", i)
                for t in range(GT):
                    for c in range(CT):
                        ins = pe.matmul(bank("out")[:, t * P:(t + 1) * P], yg[:, c, t * P:(t + 1) * P],
                                        core.out_w[:, c, :], start=c == 0, stop=c == 1)
                ins.then_inc(made["out"].sem, 1)

            for state in (H_STATE, X_STATE, G_STATE):
                front(state, 0, 0)
            turns(pe, turn)


def gated_dense(nc, core, name, *, affine):
    FC = 4
    with ExitStack() as ctx:
        sb, ps, sig = allocator(nc, ctx, name)
        TP, OUT = ps("TP"), ps("OUT")
        H1, H3 = [ps("H10"), ps("H11")], [ps("H30"), ps("H31")]
        raw = sb("raw", [P, GT, D])
        yn = sb("yn", [P, GT, D])
        hT = sb("hT", [P, GN])
        act1 = sb("act1", [P, 2, GN])
        prod = sb("prod", [P, FC, GN])
        fin = sb("fin", [P, GT, D])
        ln = Norm(sb, sig, "ln")
        chained = sig("chained", NORM_STEPS)
        hold = sig("hold").sem
        fetched, normed, streamed = sig("fetched"), sig("normed"), sig("streamed")
        h_made, h_taken = sig("h_made"), sig("h_taken", 1, 1)
        first_made, second_made = sig("first_made", FC), sig("second_made", FC)
        first_taken = sig("first_taken", FC, 2)
        multiplied = sig("multiplied", FC, 2)
        out_made, out_taken = sig("out_made"), sig("out_taken", 1, 1)
        block = ctx.enter_context(nc.Block())

        def turns(eng, turn):
            with eng.Fori(0, TURNS - 1) as i:
                turn(i, False)
            turn(TURNS - 1, True)

        @block.gpsimd
        def _(pool):
            with pool.Fori(0, TURNS) as i:
                ln.on_pool(pool, core, i)

        @block.scalar
        def _(act):
            for g in (h_taken, first_taken):
                act.sem_inc(g.sem, g.lead)

            def front(i, s):
                act.wait_ge(h_made.sem, h_made.at(i, s + 1))
                act.activation(hT[:], TP[:], ACT.Identity, scale=affine[0], bias=affine[1]).then_inc(h_taken.sem, 1)

            def turn(i, last):
                for f in range(FC):
                    act.wait_ge(first_made.sem, first_made.at(i, f + 1))
                    act.wait_ge(multiplied.sem, multiplied.at(i, f - 1))
                    act.activation(act1[:, f % 2, :], H1[f % 2][:], ACT.Silu).then_inc(first_taken.sem, 1)
                if not last:
                    front(i, 1)

            front(0, 0)
            turns(act, turn)

        @block.vector
        def _(dve):
            for g in (multiplied, out_taken):
                dve.sem_inc(g.sem, g.lead)

            def here(buf):
                return lambda t: buf[:, t, :]

            def front(i, s):
                chain = Chain(dve, chained, i)
                chain.n = s * chained.per
                dve.tensor_copy(raw[:], core.Y[:, bass.ds(i * GT + s * GT, GT), :]).then_inc(fetched.sem, 1)
                dve.wait_ge(fetched.sem, fetched.at(i, s + 1))
                ln.statistics(dve, chain, hold, here(raw))
                ln.apply(dve, chain, i, s, here(raw), here(yn))
                chain.settle()
                dve.sem_inc(normed.sem, 1)

            def turn(i, last):
                for f in range(FC):
                    dve.wait_ge(second_made.sem, second_made.at(i, f + 1))
                    dve.wait_ge(first_taken.sem, first_taken.at(i, f + 1))
                    dve.tensor_tensor(out=prod[:, f, :], in0=act1[:, f % 2, :], in1=H3[f % 2][:], op=ALU.mult)\
                        .then_inc(multiplied.sem, 1)
                    if f == 0 and not last:
                        front(i, 1)
                dve.wait_ge(out_made.sem, out_made.at(i))
                dve.tensor_tensor(out=fin[:], in0=OUT[:].rearrange("p (t d) -> p t d", t=GT),
                                  in1=core.Y[:, bass.ds(i * GT, GT), :], op=ALU.add).then_inc(out_taken.sem, 1)
                dve.wait_ge(out_taken.sem, out_taken.at(i))
                Xt = core.X[:, bass.ds(i * GT, GT), :]
                dve.tensor_tensor(out=Xt, in0=fin[:], in1=Xt, op=ALU.add).then_inc(streamed.sem, 1)
                dve.wait_ge(streamed.sem, streamed.at(i))
                dve.sem_inc(hold, 1)

            front(0, 0)
            turns(dve, turn)

        @block.tensor
        def _(pe):
            def front(i, s):
                pe.wait_ge(normed.sem, normed.at(i, s + 1))
                pe.wait_ge(h_taken.sem, h_taken.at(i, s))
                for t in range(GT):
                    ins = pe.transpose(TP[:, t * P:(t + 1) * P], yn[:, t, :], core.ident[:])
                ins.then_inc(h_made.sem, 1)

            def turn(i, last):
                pe.wait_ge(h_taken.sem, h_taken.at(i))
                for f in range(FC):
                    cols = slice(f * P, (f + 1) * P)
                    pe.wait_ge(first_taken.sem, first_taken.at(i, f - 1))
                    pe.matmul(H1[f % 2][:], core.w1[:, cols], hT[:], start=True, stop=True)\
                        .then_inc(first_made.sem, 1)
                    pe.wait_ge(multiplied.sem, multiplied.at(i, f - 1))
                    pe.matmul(H3[f % 2][:], core.w3[:, cols], hT[:], start=True, stop=True)\
                        .then_inc(second_made.sem, 1)
                if not last:
                    front(i, 1)
                pe.wait_ge(multiplied.sem, multiplied.at(i, FC))
                pe.wait_ge(out_taken.sem, out_taken.at(i, 0))
                for t in range(GT):
                    for f in range(FC):
                        ins = pe.matmul(OUT[:, t * P:(t + 1) * P], prod[:, f, t * P:(t + 1) * P], core.w2[:, f, :],
                                        start=f == 0, stop=f == FC - 1)
                ins.then_inc(out_made.sem, 1)

            front(0, 0)
            turns(pe, turn)


COLS = ("L0_ffn_ln1_w L0_ffn_ln1_b L0_ffn_ln2_w L0_ffn_ln2_b "
        "L1_attn_a_bq bq_r L1_attn_a_bk bk_r "
        "L1_attn_b_ln1_g L1_attn_b_ln1_b L1_attn_b_ln2_g L1_attn_b_ln2_b L1_attn_b_ln3_g L1_attn_b_ln3_b "
        "L1_ffn_bq L1_ffn_bk").split()
ROWS = ("L1_attn_a_bv L1_attn_a_bo L1_ffn_bv L1_ffn_bo L1_ffn_ln1_g L1_ffn_ln1_b L1_ffn_ln2_g L1_ffn_ln2_b "
        "L0_attn_b_b_out").split()
SQUARE = ("a_q a_qr a_k a_kr a_v a_o f_q f_k f_v f_o b_q b_qr b_k b_kr b_v b_o "
          "l_q l_k l_v l_o").split()


def load(nc, core, ctx, a):
    sb, ps, sig = allocator(nc, ctx, "core_")
    core.X = sb("X", [P, TILES, D])
    core.Y = sb("Y", [P, TILES, D])
    core.ident = sb("ident", [P, P])
    core.ident16 = sb("ident16", [P, P], BF16)
    core.causal16 = sb("causal16", [P, P], BF16)
    core.head_mask = sb("head_mask", [P, 4])
    core.minus_half = sb("minus_half", [P, GT])
    core.cols = sb("cols", [P, len(COLS)])
    core.rows = sb("rows", [P, len(ROWS), D])
    core.square = sb("square", [P, len(SQUARE), D])
    core.small_rope = sb("small_rope", [P, 4, L])
    core.scale = sb("scale", [P, 1])
    core.rank = sb("rank", [P, 8])
    core.distance = sb("distance", [P, 3 * P])
    core.wide_rope = sb("wide_rope", [P, 4, L])
    core.gates = sb("gates", [P, 2, 8])
    core.gate_b = sb("gate_b", [P, 2, 8])
    core.b1 = sb("b1", [P, 32])
    core.b2 = sb("b2", [8, D])
    core.bqk = sb("bqk", [P, 2, 8])
    core.bvb = sb("bvb", [P, 1024])
    core.W1 = sb("W1", [P, 8, 512])
    core.W2 = sb("W2", [P, 8, 4, D])
    core.AW = {x: sb("AW_" + x, [P, 1024]) for x in "qkvo"}
    core.in_w = sb("in_w", [P, 512])
    core.out_w = sb("out_w", [P, 2, D])
    core.x_w = sb("x_w", [P, 2, 32])
    core.dt_w = sb("dt_w", [16, 256])
    core.conv_w = sb("conv_w", [P, 2, 4])
    core.conv_b = sb("conv_b", [P, 2])
    core.dt_b = sb("dt_b", [P, 2])
    core.d_skip = sb("d_skip", [P, 2])
    core.a_log = sb("a_log", [P, 2, 16])
    core.w1 = sb("w1", [P, 512])
    core.w3 = sb("w3", [P, 512])
    core.w2 = sb("w2", [P, 4, D])
    core.aw_loaded = sig("aw_loaded", 0)
    core.moe_loaded = sig("moe_loaded", 0)
    core.first_loaded = sig("first_loaded", 0)
    core.loaded = sig("loaded", 0)
    built = sig("built", 0)
    with nc.Block() as block:
        @block.sync
        def _(sp):
            sp.dma_start(core.X[:], a["x"].rearrange("(t p) d -> p t d", p=P)).then_inc(core.first_loaded.sem, 16)
            sp.dma_start(core.wide_rope[:], a["wide_rope"]).then_inc(core.first_loaded.sem, 16)
            load_attention(sp, core, a, "a")
            n = 0
            for dst, src in (
                    (core.cols[:], a["cols"]), (core.square[:], a["square"]),
                    (core.rows[:], a["rows"].rearrange("(o r) d -> o r d", o=1).to_broadcast([P, len(ROWS), D])),
                    (core.small_rope[:], a["small_rope"]), (core.rank[:], a["rank"]),
                    (core.distance[:], a["distance"]),
                    (core.gates[:], a["gates"]), (core.b1[:], a["b1"]), (core.b2[:], a["b2"]),
                    (core.gate_b[:], a["gate_b"].rearrange("(o r) d -> o r d", o=1).to_broadcast([P, 2, 8])),
                    (core.bqk[:], a["bqk"]), (core.in_w[:], a["in_w"]),
                    (core.out_w[:], a["out_w"].rearrange("(c p) d -> p c d", p=P)),
                    (core.x_w[:], a["x_w"].rearrange("(c p) d -> p c d", p=P)), (core.dt_w[:], a["dt_w"]),
                    (core.conv_w[:], a["conv_w"].rearrange("(c p) k -> p c k", p=P)),
                    (core.conv_b[:], a["channel"][:, 0:2]), (core.dt_b[:], a["channel"][:, 2:4]),
                    (core.d_skip[:], a["channel"][:, 4:6]),
                    (core.a_log[:], a["a_log"].rearrange("(c p) k -> p c k", p=P)),
                    (core.w1[:], a["w1"]), (core.w3[:], a["w3"]),
                    (core.w2[:], a["w2"].rearrange("(c p) d -> p c d", p=P)),
                    (core.bvb[:], a["bvb"].rearrange("(o r) -> o r", o=1).to_broadcast([P, 1024])),
                    (core.scale[:], a["scale"].rearrange("(o n) -> o n", o=1).to_broadcast([P, 1]))):
                sp.dma_start(dst, src).then_inc(core.loaded.sem, 16)
                n += 16
            core.loads = n
            load_experts(sp, core, a, "l0")
            sp.wait_ge(core.first_loaded.sem, 32)

        @block.gpsimd
        def _(pool):
            pool.memset(core.ident[:], 0.0).then_inc(built.sem, 1)
            pool.memset(core.causal16[:], 0.0).then_inc(built.sem, 1)
            pool.memset(core.head_mask[:], 1.0).then_inc(built.sem, 1)
            pool.memset(core.minus_half[:], -0.5).then_inc(built.sem, 1)
            pool.wait_ge(built.sem, 4)
            pool.affine_select(out=core.ident[:], in_=core.ident[:], compare_op=ALU.not_equal, fill=1.0,
                               base=0, pattern=[[-1, P]], channel_multiplier=1).then_inc(built.sem, 1)
            pool.affine_select(out=core.causal16[:], in_=core.causal16[:], compare_op=ALU.is_ge, fill=MASKED,
                               base=0, pattern=[[-1, P]], channel_multiplier=1).then_inc(built.sem, 1)
            for g in range(4):
                rows = core.head_mask[32 * g:32 * g + 32, :]
                pool.affine_select(out=rows, in_=rows, compare_op=ALU.is_ge, fill=0.0,
                                   base=0, pattern=[[-8, 4]], channel_multiplier=1).then_inc(built.sem, 1)
                pool.wait_ge(built.sem, 7 + 2 * g)
                pool.affine_select(out=rows, in_=rows, compare_op=ALU.is_ge, fill=0.0,
                                   base=7, pattern=[[8, 4]], channel_multiplier=-1).then_inc(built.sem, 1)
            pool.wait_ge(built.sem, 14)
            pool.tensor_copy(core.ident16[:], core.ident[:]).then_inc(built.sem, 1)
            pool.wait_ge(built.sem, 15)


def load_attention(sp, core, a, which):
    for x in "qkvo":
        sp.dma_start(core.AW[x][:], a[f"aw_{which}_{x}"]).then_inc(core.aw_loaded.sem, 16)


def load_experts(sp, core, a, which):
    sp.dma_start(core.W1[:], a[which + "_W1"].rearrange("e d f -> d e f")).then_inc(core.moe_loaded.sem, 16)
    sp.dma_start(core.W2[:], a[which + "_W2"].rearrange("e (c f) d -> f e c d", f=P))\
        .then_inc(core.moe_loaded.sem, 16)


def store(nc, core, ctx, out):
    with nc.Block() as block:
        @block.sync
        def _(sp):
            base = core.loads
            sp.dma_start(out.rearrange("(t p) d -> p t d", p=P), core.X[:]).then_inc(core.loaded.sem, 16)
            sp.wait_ge(core.loaded.sem, base + 16)


def network(nc, a, out):
    core = Core()
    with ExitStack() as ctx:
        load(nc, core, ctx, a)

        def col(name):
            k = COLS.index(name)
            return core.cols[:, k:k + 1]

        def row(name):
            return core.rows[:, ROWS.index(name), :]

        def sq(prefix, parts):
            return {x: core.square[:, SQUARE.index(prefix + "_" + x), :] for x in parts}

        r = core.small_rope

        def l0_ffn_attention(n, prefetch=None):
            small_attention(nc, core, f"l0att{n}_", src="X", norms=2,
                            affine=(col("L0_ffn_ln1_w"), col("L0_ffn_ln1_b")), w=sq("l", "qkvo"),
                            q_scale=8 ** -0.5, finish="y_plus", prefetch=prefetch)

        aw = {x: core.AW[x] for x in "qkv"}
        aw["o"] = core.AW["o"][:].rearrange("p (m d) -> p m d", m=8)
        wr = core.wide_rope

        def l0_attention_a():
            wide_attention(nc, core, "wa_", heads_per_step=1, w=aw, w_loaded=(core.aw_loaded.sem, 64),
                           rope=((wr[:, 0], wr[:, 1]), (wr[:, 2], wr[:, 3])),
                           prefetch=lambda sp: sp.wait_ge(core.loaded.sem, core.loads))

        def l0_attention_b():
            wide_attention(nc, core, "wb_", heads_per_step=2, w=aw, w_loaded=(core.aw_loaded.sem, 128),
                           bq=core.bqk[:, 0, :], bk=core.bqk[:, 1, :], bv=core.bvb, q_scale=64 ** -0.5,
                           slopes=[float(v) for v in 2.0 ** -np.linspace(1.0, 8.0, 16)], bo=row("L0_attn_b_b_out"))

        def l0_experts(n, prefetch=None):
            experts(nc, core, f"e0{n}_", affine=(col("L0_ffn_ln2_w"), col("L0_ffn_ln2_b")), normed_in=True,
                    w_loaded=(core.moe_loaded.sem, 32), gate=core.gates[:, 0, :], gate_b=core.gate_b[:, 0, :],
                    act_fn=ACT.Gelu_apprx_tanh, top=1, prefetch=prefetch)

        def l1_experts(n):
            experts(nc, core, f"e1{n}_", affine=None, normed_in=False, w_loaded=(core.moe_loaded.sem, 64),
                    gate=core.gates[:, 1, :], gate_b=core.gate_b[:, 1, :], act_fn=ACT.Gelu, top=2,
                    b1=core.b1, b2=core.b2, out_norm=(row("L1_ffn_ln2_g"), row("L1_ffn_ln2_b")))

        def l1_attention(n, prefetch=None):
            w = sq("a", ("q", "qr", "k", "kr", "v", "o"))
            w["bo"] = row("L1_attn_a_bo")
            small_attention(nc, core, f"l1att{n}_", src="X", norms=1, affine=None, w=w, q_scale=core.scale[:, 0:1],
                            bq=(col("L1_attn_a_bq"), col("bq_r")), bk=(col("L1_attn_a_bk"), col("bk_r")),
                            bv=row("L1_attn_a_bv"), rope=(r[:, 0], r[:, 1]), causal=True, finish="X_plus",
                            prefetch=prefetch)

        def l1_ffn_attention(n):
            w = sq("f", "qkvo")
            w["bo"] = row("L1_ffn_bo")
            small_attention(nc, core, f"l1ffn{n}_", src="X", norms=1, affine=None, w=w, q_scale=8 ** -0.5,
                            bq=col("L1_ffn_bq"), bk=col("L1_ffn_bk"), bv=row("L1_ffn_bv"), finish="y_norm",
                            out_norm=(row("L1_ffn_ln1_g"), row("L1_ffn_ln1_b")))

        def grouped_attention():
            small_attention(nc, core, "gqa_", src="Y", norms=1,
                            affine=(col("L1_attn_b_ln2_g"), col("L1_attn_b_ln2_b")),
                            w=sq("b", ("q", "qr", "k", "kr", "v", "o")), q_scale=8 ** -0.5,
                            rope=(r[:, 2], r[:, 3]), causal=True, finish="Y_plus")

        def l1_mamba():
            state_space(nc, core, "ssm_", affine=(col("L1_attn_b_ln1_g"), col("L1_attn_b_ln1_b")))

        def l1_dense():
            gated_dense(nc, core, "swi_", affine=(col("L1_attn_b_ln3_g"), col("L1_attn_b_ln3_b")))

        l0_attention_a()
        l0_ffn_attention(0, prefetch=lambda sp: load_attention(sp, core, a, "b"))
        l0_experts(0)
        l0_attention_b()
        l0_ffn_attention(1)
        l0_experts(1)
        l1_attention(0, prefetch=lambda sp: load_experts(sp, core, a, "l1"))
        l1_ffn_attention(0)
        l1_experts(0)
        l1_mamba()
        grouped_attention()
        l1_dense()
        l1_ffn_attention(1)
        l1_experts(1)
        store(nc, core, ctx, out)


def _program_inputs(inputs):
    g = {k: np.ascontiguousarray(np.asarray(v)) for k, v in inputs.items()}
    heads = np.arange(D).reshape(16, 8)
    swap = np.arange(D).reshape(-1, 2)[:, ::-1].reshape(-1)
    turn = np.concatenate([heads[:, 4:], heads[:, :4]], 1).reshape(-1)
    kv = ((np.arange(16) // 4)[:, None] * 8 + np.arange(8)).reshape(-1)
    g["bq_r"], g["bk_r"] = g["L1_attn_a_bq"][swap], g["L1_attn_a_bk"][swap]
    a = {"x": g["L0_attn_a_x"].reshape(TILES * P, D)}
    a["cols"] = np.stack([g[c] for c in COLS], 1)
    a["rows"] = np.stack([g[c] for c in ROWS], 0)
    wq, wk = g["L1_attn_a_Wq"].T, g["L1_attn_a_Wk"].T
    bk = g["L1_attn_b_k_w"][:, kv]
    qkv = g["L0_ffn_w_qkv"]
    sq = {"a_q": wq, "a_qr": wq[:, swap], "a_k": wk, "a_kr": wk[:, swap], "a_v": g["L1_attn_a_Wv"].T,
          "a_o": g["L1_attn_a_Wo"].T,
          "f_q": g["L1_ffn_Wq"], "f_k": g["L1_ffn_Wk"], "f_v": g["L1_ffn_Wv"], "f_o": g["L1_ffn_Wo"],
          "b_q": g["L1_attn_b_q_w"], "b_qr": g["L1_attn_b_q_w"][:, turn], "b_k": bk, "b_kr": bk[:, turn],
          "b_v": g["L1_attn_b_v_w"][:, kv], "b_o": g["L1_attn_b_o_w"],
          "l_q": qkv[:, 0:D], "l_k": qkv[:, D:2 * D], "l_v": qkv[:, 2 * D:], "l_o": g["L0_ffn_w_proj"]}
    a["square"] = np.stack([sq[s] for s in SQUARE], 1)
    a["scale"] = g["L1_attn_a_scale"]
    pos = np.arange(L, dtype=np.float32)
    ta = (np.float32(10000.0) ** (-np.arange(0, 8, 2, dtype=np.float32) / 8)).astype(np.float32)
    ang = (pos[:, None] * ta).astype(np.float32)
    ia = (np.arange(D) % 8) // 2
    sign_a = np.where(np.arange(D) % 2 == 0, -1, 1).astype(np.float32)[:, None]
    tb = (np.float32(1.0) / np.float32(10000.0) ** (np.arange(0, 8, 2, dtype=np.float32) / 8)).astype(np.float32)
    angb = (pos[:, None] * tb).astype(np.float32)
    ib = np.arange(D) % 4
    sign_b = np.where(np.arange(D) % 8 < 4, -1, 1).astype(np.float32)[:, None]
    a["small_rope"] = np.stack([np.cos(ang).T[ia], np.sin(ang).T[ia] * sign_a,
                                np.cos(angb).T[ib], np.sin(angb).T[ib] * sign_b], 1).astype(np.float32)
    fr = np.power(np.float32(10000.0), -np.arange(64, dtype=np.float32) / np.float32(64)).astype(np.float32)
    angw = (pos[:, None] * fr[None, :]).astype(np.float32)
    cos = np.concatenate([np.cos(angw).T] * 2, 0).astype(np.float32)
    sin = np.concatenate([np.sin(angw).T, -np.sin(angw).T], 0).astype(np.float32)
    unit = np.float32(1 / 128)
    a["wide_rope"] = np.stack([cos * unit, sin * unit, cos, sin], 1)
    a["aw_a_q"], a["aw_a_k"], a["aw_a_v"] = (g["L0_attn_a_w_a" + x].reshape(D, 1024) for x in "qkv")
    a["aw_a_o"] = g["L0_attn_a_w_ao"].transpose(1, 0, 2).reshape(D, 1024)
    three = g["L0_attn_b_W_qkv"].reshape(D, 16, 3, 64)
    for n, x in enumerate("qkv"):
        a["aw_b_" + x] = three[:, :, n].reshape(D, 1024)
    a["aw_b_o"] = g["L0_attn_b_W_out"].reshape(8, P, D).transpose(1, 0, 2).reshape(P, 1024)
    bqkv = g["L0_attn_b_b_qkv"].reshape(16, 3, 64)
    a["bqk"] = np.stack([bqkv[:, n].reshape(8, P).T for n in range(2)], 1)
    a["bvb"] = bqkv[:, 2].reshape(1024)
    q, k = np.arange(P)[:, None], np.arange(L)[None, :]
    tiles = [np.where(k <= q, k - q, MASKED)[:, :P], np.where(k <= q + P, k - q - P, MASKED)]
    a["distance"] = np.concatenate(tiles, 1).astype(np.float32)
    a["rank"] = np.broadcast_to(8.0 - np.arange(8), (P, 8)).astype(np.float32)
    a["gates"] = np.stack([g["L0_ffn_gate_w"], g["L1_ffn_gate_w"]], 1)
    a["gate_b"] = np.stack([g["L0_ffn_gate_b"], g["L1_ffn_gate_b"]], 0)
    a["b1"] = g["L1_ffn_b1"].reshape(32, P).T
    a["b2"] = g["L1_ffn_b2"]
    b = {k[len("L1_attn_b_"):]: v for k, v in g.items() if k.startswith("L1_attn_b_")}
    a["in_w"], a["out_w"], a["x_w"], a["dt_w"] = b["in_proj_w"], b["out_proj_w"], b["x_proj_w"], b["dt_proj_w"]
    a["conv_w"], a["a_log"] = b["conv_w"][:, 0], b["A_log"]
    a["w1"], a["w2"], a["w3"] = b["w1"], b["w2"], b["w3"]
    a["channel"] = np.concatenate([b[x].reshape(2, P).T for x in ("conv_b", "dt_proj_b", "D_skip")], 1)
    a["l0_W1"], a["l0_W2"], a["l1_W1"], a["l1_W2"] = g["L0_ffn_w1"], g["L0_ffn_w2"], g["L1_ffn_W1"], g["L1_ffn_W2"]
    return {k: np.ascontiguousarray(v) for k, v in a.items()}


def kernel(**inputs):
    import concourse.bacc as bacc
    from concourse.bass_utils import run_bass_kernel_spmd as run

    nc = bacc.Bacc("TRN2", target_bir_lowering=False, num_devices=1)
    arrays = {f"in_{k}_dram": v for k, v in _program_inputs(inputs).items()}
    aps = {k[3:-5]: nc.dram_tensor(k, v.shape, mybir.dt.from_np(v.dtype), kind="ExternalInput").ap()
           for k, v in arrays.items()}
    out = nc.dram_tensor("out_dram", (TILES * P, D), F32, kind="ExternalOutput").ap()
    network(nc, aps, out)
    r = run(nc, [arrays], core_ids=[0])
    return r.results[0]["out_dram"].reshape(SEQS, L, D)
```
